# Optimizing a Trainium2 kernel written in Bass

```python
import numpy as np
import jax
import jax.numpy as jnp

def _softmax(x, axis=-1):
    return jax.nn.softmax(x, axis=axis)

def _gelu(x):
    return jax.nn.gelu(x, approximate=True)

def _silu(x):
    return jax.nn.silu(x)

def _sigmoid(x):
    return jax.nn.sigmoid(x)

def _layernorm(x, axis=-1, eps=1e-05):
    m = jnp.mean(x, axis=axis, keepdims=True)
    v = jnp.var(x, axis=axis, keepdims=True)
    return (x - m) / jnp.sqrt(v + eps)

def _scatter_add(tgt, idx, src, axis=0):
    return tgt.at[idx].add(src)

def _segment_sum(src, seg, n):
    return jax.ops.segment_sum(src, seg, n)
kernel_name = 'mk_seq_postln_d4_jaxref_r8_f5676f'

def setup_inputs(seed: int=0):
    np.random.seed(seed)
    _w = jnp.asarray

    def _L0_attn_setup():
        import jax, jax.numpy as jnp
        import numpy as np
        B, S, D, H = (2, 256, 128, 16)
        HD = D // H
        key = jax.random.key(seed)
        ks = jax.random.split(key, 5)
        scale = 1.0 / np.sqrt(D)
        x = jax.random.normal(ks[0], (B, S, D), dtype=jnp.float32)
        W_Q = jax.random.uniform(ks[1], (D, D), jnp.float32, -scale, scale)
        W_K = jax.random.uniform(ks[2], (D, D), jnp.float32, -scale, scale)
        W_V = jax.random.uniform(ks[3], (D, D), jnp.float32, -scale, scale)
        W_O = jax.random.uniform(ks[4], (D, D), jnp.float32, -scale, scale)
        return {'x': x, 'W_Q': W_Q, 'W_K': W_K, 'W_V': W_V, 'W_O': W_O}
    _L0_attn_in = _L0_attn_setup()

    def _L0_ffn_setup():
        import jax, jax.numpy as jnp
        import numpy as np
        B, S, H, DFF, E, K = (2, 256, 128, 256, 8, 2)

        def _moe(x, Wg, W1, b1, W2, b2, W3, b3):
            Bm, Sm, Hm = x.shape
            xt = x.reshape(-1, Hm)
            gout = xt @ Wg.T
            topv, topi = jax.lax.top_k(gout, K)
            w = jax.nn.softmax(topv, axis=-1)
            comb = jnp.einsum('tke,tk->te', jax.nn.one_hot(topi, E, dtype=x.dtype), w)
            g = jnp.einsum('th,efh->etf', xt, W1) + b1[:, None, :]
            v = jnp.einsum('th,efh->etf', xt, W2) + b2[:, None, :]
            h = jax.nn.silu(g) * v
            eo = jnp.einsum('etf,ehf->eth', h, W3) + b3[:, None, :]
            out = jnp.einsum('eth,te->th', eo, comb)
            return out.reshape(Bm, Sm, Hm)
        key = jax.random.key(seed)
        ks = jax.random.split(key, 8)
        sc_h = 1.0 / np.sqrt(H)
        sc_f = 1.0 / np.sqrt(DFF)
        x = jax.random.normal(ks[0], (B, S, H), dtype=jnp.float32)
        Wg = jax.random.uniform(ks[1], (E, H), jnp.float32, -sc_h, sc_h)
        W1 = jax.random.uniform(ks[2], (E, DFF, H), jnp.float32, -sc_h, sc_h)
        b1 = jax.random.uniform(ks[3], (E, DFF), jnp.float32, -sc_h, sc_h)
        W2 = jax.random.uniform(ks[4], (E, DFF, H), jnp.float32, -sc_h, sc_h)
        b2 = jax.random.uniform(ks[5], (E, DFF), jnp.float32, -sc_h, sc_h)
        W3 = jax.random.uniform(ks[6], (E, H, DFF), jnp.float32, -sc_f, sc_f)
        b3 = jax.random.uniform(ks[7], (E, H), jnp.float32, -sc_f, sc_f)
        return {'x': x, 'Wg': Wg, 'W1': W1, 'b1': b1, 'W2': W2, 'b2': b2, 'W3': W3, 'b3': b3}
    _L0_ffn_in = _L0_ffn_setup()

    def _L1_attn_setup():
        import math
        import jax, jax.numpy as jnp
        import numpy as np
        CHUNK = 32
        PROB_FLOOR = 0.02
        EPS = 1e-05

        def l2norm(x):
            return x * jax.lax.rsqrt(jnp.sum(x * x, -1, keepdims=True) + 1e-06)

        def causal_dwconv(x, w):
            B, L, C = x.shape
            K = w.shape[-1]
            y = jax.lax.conv_general_dilated(jnp.transpose(x, (0, 2, 1)), w[:, None, :], (1,), [(K - 1, 0)], feature_group_count=C)
            return jnp.transpose(y, (0, 2, 1))

        def delta_rule_chunkwise(q, k, v, beta, chunk=CHUNK):
            b, h, L, dk = q.shape
            dv = v.shape[-1]
            pad = -L % chunk
            if pad:
                q = jnp.pad(q, ((0, 0), (0, 0), (0, pad), (0, 0)))
                k = jnp.pad(k, ((0, 0), (0, 0), (0, pad), (0, 0)))
                v = jnp.pad(v, ((0, 0), (0, 0), (0, pad), (0, 0)))
                beta = jnp.pad(beta, ((0, 0), (0, 0), (0, pad)))
            Lp = L + pad
            n = Lp // chunk
            q = l2norm(q)
            k = l2norm(k)
            v = v * beta[..., None]
            kb = k * beta[..., None]
            r = lambda t: t.reshape(b, h, n, chunk, t.shape[-1])
            q, k, v, kb = (r(q), r(k), r(v), r(kb))
            i_ = jnp.arange(chunk)
            strict_lower = (i_[:, None] > i_[None, :]).astype(q.dtype)
            lower_incl = (i_[:, None] >= i_[None, :]).astype(q.dtype)
            inv = -(kb @ jnp.swapaxes(k, -1, -2)) * strict_lower
            for i in range(1, chunk):
                inv = inv.at[..., i, :].add(jnp.einsum('...j,...jk->...k', inv[..., i, :], inv))
            inv = inv + jnp.eye(chunk, dtype=q.dtype)
            u = inv @ v
            w = inv @ kb
            mv = lambda t: jnp.moveaxis(t, 2, 0)

            def step(S, xs):
                qi, ki, ui, wi = xs
                attn = qi @ jnp.swapaxes(ki, -1, -2) * lower_incl
                ui2 = ui - wi @ S
                oi = qi @ S + attn @ ui2
                return (S + jnp.swapaxes(ki, -1, -2) @ ui2, oi)
            S0 = jnp.zeros((b, h, dk, dv), q.dtype)
            S, outs = jax.lax.scan(step, S0, (mv(q), mv(k), mv(u), mv(w)))
            out = jnp.moveaxis(outs, 0, 2).reshape(b, h, Lp, dv)[:, :, :L]
            return (out, S)

        def head_stats(x):
            mean = x.mean(-1)
            var = ((x - mean[..., None]) ** 2).mean(-1)
            am = jnp.abs(x).mean(-1)
            l2 = jnp.sqrt((x * x).sum(-1))
            return jnp.stack([mean, var, am, l2], -1).mean(2)

        def rmsnorm(x, w):
            return x * jax.lax.rsqrt((x * x).mean(-1, keepdims=True) + EPS) * w
        key = jax.random.key(seed)
        ks = jax.random.split(key, 20)
        B, L, D, H = (2, 512, 128, 4)
        dv = D // H
        f32 = jnp.float32
        rn = lambda k, shape, s: (jax.random.normal(k, shape) * s).astype(f32)
        fir = lambda k, shape: rn(k, shape, 0.02).at[..., -1].add(1.0)
        return {'hidden_states': jax.random.normal(ks[0], (B, L, D), f32), 'Wq': rn(ks[1], (D, D), 0.02), 'Wk': rn(ks[2], (D, D), 0.02), 'Wv': rn(ks[3], (D, D), 0.02), 'Wb': rn(ks[4], (D, H), 0.02), 'wq_conv': fir(ks[5], (D, 4)), 'wk_conv': fir(ks[6], (D, 4)), 'wv_conv': fir(ks[7], (D, 4)), 'fir_long': fir(ks[8], (H, dv, 64)), 'fir_short': fir(ks[9], (H, dv, 5)), 'Wg1': rn(ks[10], (D + 16, D), 0.02), 'bg1': jnp.zeros((D,), f32), 'Wg2': rn(ks[11], (D, 4), 0.02), 'bg2': jnp.array([-0.5, -0.5, 1.0, 3.0], f32), 'logit_temp': jnp.array([math.log(math.expm1(0.7))], f32), 'conv_res_logit': jnp.full((H,), -1.0, f32), 'Wres': rn(ks[12], (D, H), 0.02), 'bres': jnp.full((H,), -1.0, f32), 'Wog1': rn(ks[13], (D + 8, D // 2), 0.02), 'bog1': jnp.zeros((D // 2,), f32), 'Wog2': rn(ks[14], (D // 2, 1), 0.02), 'bog2': jnp.full((1,), -1.0986122886681098, f32), 'norm_w': jnp.ones((dv,), f32), 'Wo': rn(ks[15], (D, D), 0.02)}
    _L1_attn_in = _L1_attn_setup()

    def _L1_ffn_setup():
        import jax, jax.numpy as jnp
        import numpy as np
        DIM = 128
        EXPERT_DIM = 64
        N_EXPERTS = 16
        TOPK = 2
        SHARED_HIDDEN = EXPERT_DIM * TOPK
        B, T = (4, 128)

        def _moe_forward(x, router_w, router_bias, up_proj, gate_proj, down_proj, sh_gate, sh_up, sh_down):
            Bb, Tt, D = x.shape
            flat = x.reshape(Bb * Tt, D)
            N = flat.shape[0]
            logits = flat @ router_w.T
            topk_scores, topk_idx = jax.lax.top_k(logits + router_bias, TOPK)
            topk_scores = jax.nn.softmax(topk_scores, axis=-1)
            combine = jnp.zeros((N, N_EXPERTS), flat.dtype)
            combine = combine.at[jnp.arange(N)[:, None], topk_idx].add(topk_scores)
            up_all = jnp.einsum('nd,kde->nke', flat, up_proj)
            gate_all = jnp.einsum('nd,kde->nke', flat, gate_proj)
            hidden = jax.nn.silu(gate_all) * up_all
            down_all = jnp.einsum('nke,ked->nkd', hidden, down_proj)
            out = jnp.einsum('nk,nkd->nd', combine, down_all)
            sh_hidden = jax.nn.silu(flat @ sh_gate.T) * (flat @ sh_up.T)
            out = out + sh_hidden @ sh_down.T
            return out.reshape(Bb, Tt, D)
        key = jax.random.key(seed)
        ks = jax.random.split(key, 9)
        std = 0.02
        return {'x': jax.random.normal(ks[0], (B, T, DIM), jnp.float32), 'router_w': jax.random.normal(ks[1], (N_EXPERTS, DIM), jnp.float32) * std, 'router_bias': jnp.zeros((N_EXPERTS,), jnp.float32), 'up_proj': jax.random.normal(ks[2], (N_EXPERTS, DIM, EXPERT_DIM), jnp.float32) * std, 'gate_proj': jax.random.normal(ks[3], (N_EXPERTS, DIM, EXPERT_DIM), jnp.float32) * std, 'down_proj': jax.random.normal(ks[4], (N_EXPERTS, EXPERT_DIM, DIM), jnp.float32) * std, 'sh_gate': jax.random.normal(ks[5], (SHARED_HIDDEN, DIM), jnp.float32) * std, 'sh_up': jax.random.normal(ks[6], (SHARED_HIDDEN, DIM), jnp.float32) * std, 'sh_down': jax.random.normal(ks[7], (DIM, SHARED_HIDDEN), jnp.float32) * std}
    _L1_ffn_in = _L1_ffn_setup()

    def _L2_attn_setup():
        import jax, jax.numpy as jnp
        import numpy as np
        D_MODEL = 128
        NHEAD = 16
        HEAD_DIM = D_MODEL // NHEAD
        LN_EPS = 1e-05

        def _retention_scan(v, lam_h):
            B, L, H, DH = v.shape
            a = jnp.broadcast_to(lam_h[None, None, :, None], v.shape)

            def combine(x, y):
                a1, b1 = x
                a2, b2 = y
                return (a1 * a2, a2 * b1 + b2)
            _, states = jax.lax.associative_scan(combine, (a, v), axis=1)
            return states
        key = jax.random.key(seed)
        ks = jax.random.split(key, 6)
        B, L, D = (4, 512, D_MODEL)
        s = 1.0 / np.sqrt(D)
        return {'x': jax.random.normal(ks[0], (B, L, D), jnp.float32), 'Wq': jax.random.normal(ks[1], (D, D), jnp.float32) * s, 'Wv': jax.random.normal(ks[2], (D, D), jnp.float32) * s, 'Wg': jax.random.normal(ks[3], (D, D), jnp.float32) * s, 'Wo': jax.random.normal(ks[4], (D, D), jnp.float32) * s, 'beta': jnp.full((NHEAD,), -0.2, jnp.float32), 'ln_gamma': jnp.ones((D_MODEL,), jnp.float32), 'ln_beta': jnp.zeros((D_MODEL,), jnp.float32)}
    _L2_attn_in = _L2_attn_setup()

    def _L2_ffn_setup():
        import jax, jax.numpy as jnp
        import numpy as np
        B, S, D = (1, 256, 128)
        E, K, F = (64, 8, 96)
        SF = 96
        C = 64
        ROUTED_SCALE = 1.0

        def _moe_forward(x, router_w, w_gate, w_up, w_down, ws_gate_up, ws_down):
            T = x.shape[0]
            logits = x.astype(jnp.float32) @ router_w.T
            probs = jax.nn.softmax(logits, axis=-1)
            topk_w, topk_ids = jax.lax.top_k(probs, K)
            topk_w = topk_w / jnp.sum(topk_w, axis=-1, keepdims=True)
            topk_w = topk_w.astype(x.dtype)
            N = T * K
            flat_e = topk_ids.reshape(-1)
            flat_w = topk_w.reshape(-1)
            tok = jnp.arange(N) // K
            onehot = flat_e[:, None] == jnp.arange(E)[None, :]
            pos = jnp.cumsum(onehot, axis=0)[jnp.arange(N), flat_e] - 1
            valid = pos < C
            idx = jnp.where(valid, flat_e * C + pos, E * C)
            x_buf = jnp.zeros((E * C + 1, x.shape[1]), x.dtype).at[idx].set(x[tok])
            xb = x_buf[:E * C].reshape(E, C, -1)
            g = jnp.einsum('ecd,edf->ecf', xb, w_gate)
            u = jnp.einsum('ecd,edf->ecf', xb, w_up)
            h = jax.nn.silu(g) * u
            y = jnp.einsum('ecf,efd->ecd', h, w_down).reshape(E * C, -1)
            safe = jnp.where(valid, idx, 0)
            contrib = y[safe] * (flat_w * valid.astype(flat_w.dtype))[:, None]
            routed = jax.ops.segment_sum(contrib, tok, num_segments=T)
            routed = routed * ROUTED_SCALE
            gu = x @ ws_gate_up
            sg, su = (gu[:, :SF], gu[:, SF:])
            shared = jax.nn.silu(sg) * su @ ws_down
            return routed + shared
        key = jax.random.key(seed)
        ks = jax.random.split(key, 7)
        w = 0.02
        return {'hidden_states': jax.random.normal(ks[0], (B, S, D), jnp.float32), 'router_w': jax.random.normal(ks[1], (E, D), jnp.float32) * w, 'w_gate': jax.random.normal(ks[2], (E, D, F), jnp.float32) * w, 'w_up': jax.random.normal(ks[3], (E, D, F), jnp.float32) * w, 'w_down': jax.random.normal(ks[4], (E, F, D), jnp.float32) * w, 'ws_gate_up': jax.random.normal(ks[5], (D, 2 * SF), jnp.float32) * w, 'ws_down': jax.random.normal(ks[6], (SF, D), jnp.float32) * w}
    _L2_ffn_in = _L2_ffn_setup()

    def _L3_attn_setup():
        import jax, jax.numpy as jnp
        import numpy as np
        BATCH, SEQ, DMODEL, DHID = (4, 512, 128, 128)
        R_MIN, R_MAX = (0.9, 0.99)
        MAX_PHASE = np.pi / 50
        EPS = 1e-05
        key = jax.random.key(seed)
        ks = jax.random.split(key, 8)
        u1 = jax.random.uniform(ks[0], (DHID,)) * (1 - EPS) + EPS
        mag_sq = u1 * (R_MAX ** 2 - R_MIN ** 2) + R_MIN ** 2
        nu_log = jnp.log(-0.5 * jnp.log(mag_sq + EPS))
        u2 = jax.random.uniform(ks[1], (DHID,)) * (1 - EPS) + EPS
        theta_log = jnp.log(MAX_PHASE * u2)
        B_re = jax.random.normal(ks[2], (DHID, DMODEL)) / np.sqrt(2 * DMODEL)
        B_im = jax.random.normal(ks[3], (DHID, DMODEL)) / np.sqrt(2 * DMODEL)
        C_re = jax.random.normal(ks[4], (DMODEL, DHID)) / np.sqrt(DHID)
        C_im = jax.random.normal(ks[5], (DMODEL, DHID)) / np.sqrt(DHID)
        D_skip = jax.random.normal(ks[6], (DMODEL,))
        inputs = jax.random.normal(ks[7], (BATCH, SEQ, DMODEL), dtype=jnp.float32)
        return {'inputs': inputs, 'nu_log': nu_log, 'theta_log': theta_log, 'B_re': B_re, 'B_im': B_im, 'C_re': C_re, 'C_im': C_im, 'D_skip': D_skip}
    _L3_attn_in = _L3_attn_setup()

    def _L3_ffn_setup():
        import jax, jax.numpy as jnp
        import numpy as np
        B, S, D, FF, E, L = (8, 256, 128, 512, 16, 4)

        def _unipool_layer(xt, router, W1, W2):
            logits = xt @ router
            probs = jax.nn.softmax(logits, axis=-1)
            w = jnp.max(probs, axis=-1)
            idx = jnp.argmax(probs, axis=-1)

            def body(acc, params):
                w1, w2, i = params
                h = jax.nn.silu(xt @ w1) @ w2
                sel = jnp.where(idx == i, w, 0.0)
                return (acc + sel[:, None] * h, None)
            out, _ = jax.lax.scan(body, jnp.zeros_like(xt), (W1, W2, jnp.arange(W1.shape[0])))
            return out
        key = jax.random.key(seed)
        k0, k1, k2, k3 = jax.random.split(key, 4)
        x = jax.random.normal(k0, (B, S, D), dtype=jnp.float32)
        routers = jax.random.normal(k1, (L, D, E), dtype=jnp.float32) * 0.02
        W1 = jax.random.normal(k2, (E, D, FF), dtype=jnp.float32) * 0.02
        W2 = jax.random.normal(k3, (E, FF, D), dtype=jnp.float32) * 0.02
        return {'x': x, 'routers': routers, 'W1': W1, 'W2': W2}
    _L3_ffn_in = _L3_ffn_setup()
    _d = {'L0_attn_x': _L0_attn_in['x'], 'L0_attn_W_Q': _L0_attn_in['W_Q'], 'L0_attn_W_K': _L0_attn_in['W_K'], 'L0_attn_W_V': _L0_attn_in['W_V'], 'L0_attn_W_O': _L0_attn_in['W_O'], 'L0_ffn_Wg': _L0_ffn_in['Wg'], 'L0_ffn_W1': _L0_ffn_in['W1'], 'L0_ffn_b1': _L0_ffn_in['b1'], 'L0_ffn_W2': _L0_ffn_in['W2'], 'L0_ffn_b2': _L0_ffn_in['b2'], 'L0_ffn_W3': _L0_ffn_in['W3'], 'L0_ffn_b3': _L0_ffn_in['b3'], 'L1_attn_Wq': _L1_attn_in['Wq'], 'L1_attn_Wk': _L1_attn_in['Wk'], 'L1_attn_Wv': _L1_attn_in['Wv'], 'L1_attn_Wb': _L1_attn_in['Wb'], 'L1_attn_wq_conv': _L1_attn_in['wq_conv'], 'L1_attn_wk_conv': _L1_attn_in['wk_conv'], 'L1_attn_wv_conv': _L1_attn_in['wv_conv'], 'L1_attn_fir_long': _L1_attn_in['fir_long'], 'L1_attn_fir_short': _L1_attn_in['fir_short'], 'L1_attn_Wg1': _L1_attn_in['Wg1'], 'L1_attn_bg1': _L1_attn_in['bg1'], 'L1_attn_Wg2': _L1_attn_in['Wg2'], 'L1_attn_bg2': _L1_attn_in['bg2'], 'L1_attn_logit_temp': _L1_attn_in['logit_temp'], 'L1_attn_conv_res_logit': _L1_attn_in['conv_res_logit'], 'L1_attn_Wres': _L1_attn_in['Wres'], 'L1_attn_bres': _L1_attn_in['bres'], 'L1_attn_Wog1': _L1_attn_in['Wog1'], 'L1_attn_bog1': _L1_attn_in['bog1'], 'L1_attn_Wog2': _L1_attn_in['Wog2'], 'L1_attn_bog2': _L1_attn_in['bog2'], 'L1_attn_norm_w': _L1_attn_in['norm_w'], 'L1_attn_Wo': _L1_attn_in['Wo'], 'L1_ffn_router_w': _L1_ffn_in['router_w'], 'L1_ffn_router_bias': _L1_ffn_in['router_bias'], 'L1_ffn_up_proj': _L1_ffn_in['up_proj'], 'L1_ffn_gate_proj': _L1_ffn_in['gate_proj'], 'L1_ffn_down_proj': _L1_ffn_in['down_proj'], 'L1_ffn_sh_gate': _L1_ffn_in['sh_gate'], 'L1_ffn_sh_up': _L1_ffn_in['sh_up'], 'L1_ffn_sh_down': _L1_ffn_in['sh_down'], 'L2_attn_Wq': _L2_attn_in['Wq'], 'L2_attn_Wv': _L2_attn_in['Wv'], 'L2_attn_Wg': _L2_attn_in['Wg'], 'L2_attn_Wo': _L2_attn_in['Wo'], 'L2_attn_beta': _L2_attn_in['beta'], 'L2_attn_ln_gamma': _L2_attn_in['ln_gamma'], 'L2_attn_ln_beta': _L2_attn_in['ln_beta'], 'L2_ffn_router_w': _L2_ffn_in['router_w'], 'L2_ffn_w_gate': _L2_ffn_in['w_gate'], 'L2_ffn_w_up': _L2_ffn_in['w_up'], 'L2_ffn_w_down': _L2_ffn_in['w_down'], 'L2_ffn_ws_gate_up': _L2_ffn_in['ws_gate_up'], 'L2_ffn_ws_down': _L2_ffn_in['ws_down'], 'L3_attn_nu_log': _L3_attn_in['nu_log'], 'L3_attn_theta_log': _L3_attn_in['theta_log'], 'L3_attn_B_re': _L3_attn_in['B_re'], 'L3_attn_B_im': _L3_attn_in['B_im'], 'L3_attn_C_re': _L3_attn_in['C_re'], 'L3_attn_C_im': _L3_attn_in['C_im'], 'L3_attn_D_skip': _L3_attn_in['D_skip'], 'L3_ffn_routers': _L3_ffn_in['routers'], 'L3_ffn_W1': _L3_ffn_in['W1'], 'L3_ffn_W2': _L3_ffn_in['W2']}
    _x0 = _d['L0_attn_x']
    _d['L0_attn_x'] = jax.random.normal(jax.random.fold_in(jax.random.key(seed), 1), (8, 256, 128), dtype=_x0.dtype)
    del _x0
    return _d

def reference(L0_attn_x, L0_attn_W_Q, L0_attn_W_K, L0_attn_W_V, L0_attn_W_O, L0_ffn_Wg, L0_ffn_W1, L0_ffn_b1, L0_ffn_W2, L0_ffn_b2, L0_ffn_W3, L0_ffn_b3, L1_attn_Wq, L1_attn_Wk, L1_attn_Wv, L1_attn_Wb, L1_attn_wq_conv, L1_attn_wk_conv, L1_attn_wv_conv, L1_attn_fir_long, L1_attn_fir_short, L1_attn_Wg1, L1_attn_bg1, L1_attn_Wg2, L1_attn_bg2, L1_attn_logit_temp, L1_attn_conv_res_logit, L1_attn_Wres, L1_attn_bres, L1_attn_Wog1, L1_attn_bog1, L1_attn_Wog2, L1_attn_bog2, L1_attn_norm_w, L1_attn_Wo, L1_ffn_router_w, L1_ffn_router_bias, L1_ffn_up_proj, L1_ffn_gate_proj, L1_ffn_down_proj, L1_ffn_sh_gate, L1_ffn_sh_up, L1_ffn_sh_down, L2_attn_Wq, L2_attn_Wv, L2_attn_Wg, L2_attn_Wo, L2_attn_beta, L2_attn_ln_gamma, L2_attn_ln_beta, L2_ffn_router_w, L2_ffn_w_gate, L2_ffn_w_up, L2_ffn_w_down, L2_ffn_ws_gate_up, L2_ffn_ws_down, L3_attn_nu_log, L3_attn_theta_log, L3_attn_B_re, L3_attn_B_im, L3_attn_C_re, L3_attn_C_im, L3_attn_D_skip, L3_ffn_routers, L3_ffn_W1, L3_ffn_W2):

    def _L0_attn_ref(x, W_Q, W_K, W_V, W_O):
        import jax, jax.numpy as jnp
        import numpy as np
        B, S, D, H = (2, 256, 128, 16)
        HD = D // H
        b, s, d = x.shape
        Q = (x @ W_Q.T).reshape(b, s, H, HD).transpose(0, 2, 1, 3)
        K = (x @ W_K.T).reshape(b, s, H, HD).transpose(0, 2, 1, 3)
        V = (x @ W_V.T).reshape(b, s, H, HD).transpose(0, 2, 1, 3)
        attn = jnp.einsum('bhqd,bhkd->bhqk', Q, K) / jnp.sqrt(jnp.float32(HD))
        slopes = 1.0 / (2.0 ** 8) ** ((jnp.arange(H, dtype=jnp.float32) + 1) / H)
        pos = jnp.arange(s)
        rel = jnp.minimum(pos[None, :] - pos[:, None], 0).astype(jnp.float32)
        bias = slopes[:, None, None] * rel[None, :, :]
        causal = pos[None, :] <= pos[:, None]
        attn = jnp.where(causal[None, None], attn + bias[None], -jnp.inf)
        attn = jax.nn.softmax(attn, axis=-1)
        out = jnp.einsum('bhqk,bhkd->bhqd', attn, V)
        out = out.transpose(0, 2, 1, 3).reshape(b, s, d)
        return out @ W_O.T

    def _L0_ffn_ref(x, Wg, W1, b1, W2, b2, W3, b3):
        import jax, jax.numpy as jnp
        import numpy as np
        B, S, H, DFF, E, K = (2, 256, 128, 256, 8, 2)

        def _moe(x, Wg, W1, b1, W2, b2, W3, b3):
            Bm, Sm, Hm = x.shape
            xt = x.reshape(-1, Hm)
            gout = xt @ Wg.T
            topv, topi = jax.lax.top_k(gout, K)
            w = jax.nn.softmax(topv, axis=-1)
            comb = jnp.einsum('tke,tk->te', jax.nn.one_hot(topi, E, dtype=x.dtype), w)
            g = jnp.einsum('th,efh->etf', xt, W1) + b1[:, None, :]
            v = jnp.einsum('th,efh->etf', xt, W2) + b2[:, None, :]
            h = jax.nn.silu(g) * v
            eo = jnp.einsum('etf,ehf->eth', h, W3) + b3[:, None, :]
            out = jnp.einsum('eth,te->th', eo, comb)
            return out.reshape(Bm, Sm, Hm)
        return _moe(x, Wg, W1, b1, W2, b2, W3, b3)

    def _L1_attn_ref(hidden_states, Wq, Wk, Wv, Wb, wq_conv, wk_conv, wv_conv, fir_long, fir_short, Wg1, bg1, Wg2, bg2, logit_temp, conv_res_logit, Wres, bres, Wog1, bog1, Wog2, bog2, norm_w, Wo):
        import math
        import jax, jax.numpy as jnp
        import numpy as np
        CHUNK = 32
        PROB_FLOOR = 0.02
        EPS = 1e-05

        def l2norm(x):
            return x * jax.lax.rsqrt(jnp.sum(x * x, -1, keepdims=True) + 1e-06)

        def causal_dwconv(x, w):
            B, L, C = x.shape
            K = w.shape[-1]
            y = jax.lax.conv_general_dilated(jnp.transpose(x, (0, 2, 1)), w[:, None, :], (1,), [(K - 1, 0)], feature_group_count=C)
            return jnp.transpose(y, (0, 2, 1))

        def delta_rule_chunkwise(q, k, v, beta, chunk=CHUNK):
            b, h, L, dk = q.shape
            dv = v.shape[-1]
            pad = -L % chunk
            if pad:
                q = jnp.pad(q, ((0, 0), (0, 0), (0, pad), (0, 0)))
                k = jnp.pad(k, ((0, 0), (0, 0), (0, pad), (0, 0)))
                v = jnp.pad(v, ((0, 0), (0, 0), (0, pad), (0, 0)))
                beta = jnp.pad(beta, ((0, 0), (0, 0), (0, pad)))
            Lp = L + pad
            n = Lp // chunk
            q = l2norm(q)
            k = l2norm(k)
            v = v * beta[..., None]
            kb = k * beta[..., None]
            r = lambda t: t.reshape(b, h, n, chunk, t.shape[-1])
            q, k, v, kb = (r(q), r(k), r(v), r(kb))
            i_ = jnp.arange(chunk)
            strict_lower = (i_[:, None] > i_[None, :]).astype(q.dtype)
            lower_incl = (i_[:, None] >= i_[None, :]).astype(q.dtype)
            inv = -(kb @ jnp.swapaxes(k, -1, -2)) * strict_lower
            for i in range(1, chunk):
                inv = inv.at[..., i, :].add(jnp.einsum('...j,...jk->...k', inv[..., i, :], inv))
            inv = inv + jnp.eye(chunk, dtype=q.dtype)
            u = inv @ v
            w = inv @ kb
            mv = lambda t: jnp.moveaxis(t, 2, 0)

            def step(S, xs):
                qi, ki, ui, wi = xs
                attn = qi @ jnp.swapaxes(ki, -1, -2) * lower_incl
                ui2 = ui - wi @ S
                oi = qi @ S + attn @ ui2
                return (S + jnp.swapaxes(ki, -1, -2) @ ui2, oi)
            S0 = jnp.zeros((b, h, dk, dv), q.dtype)
            S, outs = jax.lax.scan(step, S0, (mv(q), mv(k), mv(u), mv(w)))
            out = jnp.moveaxis(outs, 0, 2).reshape(b, h, Lp, dv)[:, :, :L]
            return (out, S)

        def head_stats(x):
            mean = x.mean(-1)
            var = ((x - mean[..., None]) ** 2).mean(-1)
            am = jnp.abs(x).mean(-1)
            l2 = jnp.sqrt((x * x).sum(-1))
            return jnp.stack([mean, var, am, l2], -1).mean(2)

        def rmsnorm(x, w):
            return x * jax.lax.rsqrt((x * x).mean(-1, keepdims=True) + EPS) * w
        B, L, D = hidden_states.shape
        H = Wb.shape[-1]
        silu = jax.nn.silu
        q_in = silu(causal_dwconv(hidden_states @ Wq, wq_conv))
        k_in = silu(causal_dwconv(hidden_states @ Wk, wk_conv))
        v_in = silu(causal_dwconv(hidden_states @ Wv, wv_conv))
        dk = q_in.shape[-1] // H
        dv = v_in.shape[-1] // H
        q = q_in.reshape(B, L, H, dk)
        k = k_in.reshape(B, L, H, dk)
        v_direct = v_in.reshape(B, L, H, dv)
        beta = jax.nn.sigmoid(hidden_states @ Wb)
        do, S = delta_rule_chunkwise(jnp.transpose(q, (0, 2, 1, 3)), jnp.transpose(k, (0, 2, 1, 3)), jnp.transpose(v_direct, (0, 2, 1, 3)), jnp.transpose(beta, (0, 2, 1)))
        delta_out = jnp.transpose(do, (0, 2, 1, 3))
        local_long = causal_dwconv(v_in, fir_long.reshape(-1, fir_long.shape[-1])).reshape(B, L, H, dv)
        local_short = causal_dwconv(v_in, fir_short.reshape(-1, fir_short.shape[-1])).reshape(B, L, H, dv)
        stats = jnp.concatenate([head_stats(t) for t in (local_short, local_long, delta_out, v_direct)], -1)
        gate_in = jnp.concatenate([hidden_states, stats], -1)
        logits = (jax.nn.gelu(gate_in @ Wg1 + bg1, approximate=False) @ Wg2 + bg2) / jax.nn.softplus(logit_temp)
        p = jax.nn.softmax(logits, -1)
        p = jnp.clip(p, PROB_FLOOR, None)
        p = p / p.sum(-1, keepdims=True)
        pw = p[:, :, None, :]
        o = pw[..., 0:1] * local_short + pw[..., 1:2] * local_long + pw[..., 2:3] * delta_out + pw[..., 3:4] * v_direct
        res_gate = jax.nn.sigmoid(hidden_states @ Wres + bres)
        static = jax.nn.sigmoid(conv_res_logit)
        o = o + (static[None, None, :] * res_gate)[..., None] * local_short
        og_stats = jnp.concatenate([head_stats(o), head_stats(v_direct)], -1)
        og_in = jnp.concatenate([hidden_states, og_stats], -1)
        og = jax.nn.sigmoid(jax.nn.gelu(og_in @ Wog1 + bog1, approximate=False) @ Wog2 + bog2)
        o = o * og[:, :, :, None]
        o = rmsnorm(o, norm_w)
        return o.reshape(B, L, -1) @ Wo

    def _L1_ffn_ref(x, router_w, router_bias, up_proj, gate_proj, down_proj, sh_gate, sh_up, sh_down):
        import jax, jax.numpy as jnp
        import numpy as np
        DIM = 128
        EXPERT_DIM = 64
        N_EXPERTS = 16
        TOPK = 2
        SHARED_HIDDEN = EXPERT_DIM * TOPK
        B, T = (4, 128)

        def _moe_forward(x, router_w, router_bias, up_proj, gate_proj, down_proj, sh_gate, sh_up, sh_down):
            Bb, Tt, D = x.shape
            flat = x.reshape(Bb * Tt, D)
            N = flat.shape[0]
            logits = flat @ router_w.T
            topk_scores, topk_idx = jax.lax.top_k(logits + router_bias, TOPK)
            topk_scores = jax.nn.softmax(topk_scores, axis=-1)
            combine = jnp.zeros((N, N_EXPERTS), flat.dtype)
            combine = combine.at[jnp.arange(N)[:, None], topk_idx].add(topk_scores)
            up_all = jnp.einsum('nd,kde->nke', flat, up_proj)
            gate_all = jnp.einsum('nd,kde->nke', flat, gate_proj)
            hidden = jax.nn.silu(gate_all) * up_all
            down_all = jnp.einsum('nke,ked->nkd', hidden, down_proj)
            out = jnp.einsum('nk,nkd->nd', combine, down_all)
            sh_hidden = jax.nn.silu(flat @ sh_gate.T) * (flat @ sh_up.T)
            out = out + sh_hidden @ sh_down.T
            return out.reshape(Bb, Tt, D)
        return _moe_forward(x, router_w, router_bias, up_proj, gate_proj, down_proj, sh_gate, sh_up, sh_down)

    def _L2_attn_ref(x, Wq, Wv, Wg, Wo, beta, ln_gamma, ln_beta):
        import jax, jax.numpy as jnp
        import numpy as np
        D_MODEL = 128
        NHEAD = 16
        HEAD_DIM = D_MODEL // NHEAD
        LN_EPS = 1e-05

        def _retention_scan(v, lam_h):
            B, L, H, DH = v.shape
            a = jnp.broadcast_to(lam_h[None, None, :, None], v.shape)

            def combine(x, y):
                a1, b1 = x
                a2, b2 = y
                return (a1 * a2, a2 * b1 + b2)
            _, states = jax.lax.associative_scan(combine, (a, v), axis=1)
            return states
        B, L, D = x.shape
        H, DH = (NHEAD, HEAD_DIM)
        q = (x @ Wq.T).reshape(B, L, H, DH)
        v = (x @ Wv.T).reshape(B, L, H, DH)
        lam_h = jax.nn.sigmoid(beta)
        state = _retention_scan(v, lam_h)
        y = (q * state).reshape(B, L, D)
        mu = jnp.mean(y, axis=-1, keepdims=True)
        var = jnp.mean((y - mu) ** 2, axis=-1, keepdims=True)
        y = (y - mu) * jax.lax.rsqrt(var + LN_EPS) * ln_gamma + ln_beta
        gate = jax.nn.silu(x @ Wg.T)
        y = y * gate
        return y @ Wo.T

    def _L2_ffn_ref(hidden_states, router_w, w_gate, w_up, w_down, ws_gate_up, ws_down):
        import jax, jax.numpy as jnp
        import numpy as np
        B, S, D = (1, 256, 128)
        E, K, F = (64, 8, 96)
        SF = 96
        C = 64
        ROUTED_SCALE = 1.0

        def _moe_forward(x, router_w, w_gate, w_up, w_down, ws_gate_up, ws_down):
            T = x.shape[0]
            logits = x.astype(jnp.float32) @ router_w.T
            probs = jax.nn.softmax(logits, axis=-1)
            topk_w, topk_ids = jax.lax.top_k(probs, K)
            topk_w = topk_w / jnp.sum(topk_w, axis=-1, keepdims=True)
            topk_w = topk_w.astype(x.dtype)
            N = T * K
            flat_e = topk_ids.reshape(-1)
            flat_w = topk_w.reshape(-1)
            tok = jnp.arange(N) // K
            onehot = flat_e[:, None] == jnp.arange(E)[None, :]
            pos = jnp.cumsum(onehot, axis=0)[jnp.arange(N), flat_e] - 1
            valid = pos < C
            idx = jnp.where(valid, flat_e * C + pos, E * C)
            x_buf = jnp.zeros((E * C + 1, x.shape[1]), x.dtype).at[idx].set(x[tok])
            xb = x_buf[:E * C].reshape(E, C, -1)
            g = jnp.einsum('ecd,edf->ecf', xb, w_gate)
            u = jnp.einsum('ecd,edf->ecf', xb, w_up)
            h = jax.nn.silu(g) * u
            y = jnp.einsum('ecf,efd->ecd', h, w_down).reshape(E * C, -1)
            safe = jnp.where(valid, idx, 0)
            contrib = y[safe] * (flat_w * valid.astype(flat_w.dtype))[:, None]
            routed = jax.ops.segment_sum(contrib, tok, num_segments=T)
            routed = routed * ROUTED_SCALE
            gu = x @ ws_gate_up
            sg, su = (gu[:, :SF], gu[:, SF:])
            shared = jax.nn.silu(sg) * su @ ws_down
            return routed + shared
        b, s, d = hidden_states.shape
        x = hidden_states.reshape(-1, d)
        out = _moe_forward(x, router_w, w_gate, w_up, w_down, ws_gate_up, ws_down)
        return out.reshape(b, s, d)

    def _L3_attn_ref(inputs, nu_log, theta_log, B_re, B_im, C_re, C_im, D_skip):
        import jax, jax.numpy as jnp
        import numpy as np
        BATCH, SEQ, DMODEL, DHID = (4, 512, 128, 128)
        R_MIN, R_MAX = (0.9, 0.99)
        MAX_PHASE = np.pi / 50
        EPS = 1e-05
        nu = jnp.exp(nu_log)
        theta = jnp.exp(theta_log)
        diag_lambda = jnp.exp(-nu + 1j * theta)
        gamma_log = 0.5 * jnp.log(1 - jnp.exp(-2 * jnp.exp(nu_log)) + EPS)
        B_norm = (B_re + 1j * B_im) * jnp.exp(gamma_log)[:, None]
        inputs_c = inputs.astype(jnp.complex64)
        Bu = jnp.einsum('hd,btd->bth', B_norm, inputs_c)

        def step(h, bu_t):
            h = diag_lambda * h + bu_t
            return (h, h)
        h0 = jnp.zeros((inputs.shape[0], diag_lambda.shape[0]), dtype=Bu.dtype)
        _, hs = jax.lax.scan(step, h0, jnp.swapaxes(Bu, 0, 1))
        hs = jnp.swapaxes(hs, 0, 1)
        C_complex = C_re + 1j * C_im
        out = jnp.einsum('bth,dh->btd', hs, C_complex).real + inputs * D_skip
        return out.astype(jnp.float32)

    def _L3_ffn_ref(x, routers, W1, W2):
        import jax, jax.numpy as jnp
        import numpy as np
        B, S, D, FF, E, L = (8, 256, 128, 512, 16, 4)

        def _unipool_layer(xt, router, W1, W2):
            logits = xt @ router
            probs = jax.nn.softmax(logits, axis=-1)
            w = jnp.max(probs, axis=-1)
            idx = jnp.argmax(probs, axis=-1)

            def body(acc, params):
                w1, w2, i = params
                h = jax.nn.silu(xt @ w1) @ w2
                sel = jnp.where(idx == i, w, 0.0)
                return (acc + sel[:, None] * h, None)
            out, _ = jax.lax.scan(body, jnp.zeros_like(xt), (W1, W2, jnp.arange(W1.shape[0])))
            return out
        b, s, d = x.shape
        xt = x.reshape(-1, d)

        def step(carry, router):
            return (_unipool_layer(carry, router, W1, W2), None)
        xt, _ = jax.lax.scan(step, xt, routers)
        return xt.reshape(b, s, d)
    x = L0_attn_x
    x = _layernorm(x + _L0_attn_ref(x, L0_attn_W_Q, L0_attn_W_K, L0_attn_W_V, L0_attn_W_O), axis=-1)
    x = _layernorm(x + _L0_ffn_ref(x, L0_ffn_Wg, L0_ffn_W1, L0_ffn_b1, L0_ffn_W2, L0_ffn_b2, L0_ffn_W3, L0_ffn_b3), axis=-1)
    x = _layernorm(x + _L1_attn_ref(x, L1_attn_Wq, L1_attn_Wk, L1_attn_Wv, L1_attn_Wb, L1_attn_wq_conv, L1_attn_wk_conv, L1_attn_wv_conv, L1_attn_fir_long, L1_attn_fir_short, L1_attn_Wg1, L1_attn_bg1, L1_attn_Wg2, L1_attn_bg2, L1_attn_logit_temp, L1_attn_conv_res_logit, L1_attn_Wres, L1_attn_bres, L1_attn_Wog1, L1_attn_bog1, L1_attn_Wog2, L1_attn_bog2, L1_attn_norm_w, L1_attn_Wo), axis=-1)
    x = _layernorm(x + _L1_ffn_ref(x, L1_ffn_router_w, L1_ffn_router_bias, L1_ffn_up_proj, L1_ffn_gate_proj, L1_ffn_down_proj, L1_ffn_sh_gate, L1_ffn_sh_up, L1_ffn_sh_down), axis=-1)
    x = _layernorm(x + _L2_attn_ref(x, L2_attn_Wq, L2_attn_Wv, L2_attn_Wg, L2_attn_Wo, L2_attn_beta, L2_attn_ln_gamma, L2_attn_ln_beta), axis=-1)
    x = _layernorm(x + _L2_ffn_ref(x, L2_ffn_router_w, L2_ffn_w_gate, L2_ffn_w_up, L2_ffn_w_down, L2_ffn_ws_gate_up, L2_ffn_ws_down), axis=-1)
    x = _layernorm(x + _L3_attn_ref(x, L3_attn_nu_log, L3_attn_theta_log, L3_attn_B_re, L3_attn_B_im, L3_attn_C_re, L3_attn_C_im, L3_attn_D_skip), axis=-1)
    x = _layernorm(x + _L3_ffn_ref(x, L3_ffn_routers, L3_ffn_W1, L3_ffn_W2), axis=-1)
    return x

_drawn_inputs = setup_inputs


def setup_inputs(seed=0):
    import zlib

    import numpy as np

    out = dict(_drawn_inputs(seed))
    spreads = {'L1_attn_bg1': (0.0, 0.8),
     'L1_attn_conv_res_logit': (-1.0, 0.6),
     'L1_attn_bres': (-1.0, 0.6),
     'L1_attn_bog1': (0.0, 2.0),
     'L1_attn_norm_w': (1.0, 0.2),
     'L1_ffn_router_bias': (0.0, 0.8),
     'L2_attn_beta': (-0.20000000298023224, 0.6),
     'L2_attn_ln_gamma': (1.0, 0.2),
     'L2_attn_ln_beta': (0.0, 0.1)}
    factors = {'L0_ffn_b1': 6.798,
     'L0_ffn_b2': 6.29,
     'L1_attn_Wq': 6.375,
     'L1_attn_Wk': 6.236,
     'L1_attn_Wb': 8.0,
     'L1_attn_wq_conv': 7.128,
     'L1_attn_wk_conv': 6.768,
     'L1_attn_fir_long': 8.0,
     'L1_attn_fir_short': 2.675,
     'L1_attn_Wg1': 8.0,
     'L1_attn_Wg2': 8.0,
     'L1_attn_Wres': 8.0,
     'L1_attn_Wog1': 8.0,
     'L1_attn_Wog2': 8.0,
     'L1_ffn_router_w': 8.0,
     'L1_ffn_up_proj': 8.0,
     'L1_ffn_gate_proj': 8.0,
     'L1_ffn_down_proj': 8.0,
     'L1_ffn_sh_gate': 7.745,
     'L1_ffn_sh_up': 7.656,
     'L1_ffn_sh_down': 7.668,
     'L2_ffn_router_w': 8.0,
     'L2_ffn_w_gate': 8.0,
     'L2_ffn_w_up': 8.0,
     'L2_ffn_w_down': 8.0,
     'L2_ffn_ws_gate_up': 8.0,
     'L2_ffn_ws_down': 8.0}
    for name, (base, spread) in spreads.items():
        noise = np.random.default_rng([zlib.crc32(name.encode()), seed]).standard_normal(out[name].shape)
        drawn = base * np.exp(spread * noise) if base else spread * noise
        out[name] = jnp.asarray(drawn.astype(out[name].dtype))
    for name, factor in factors.items():
        out[name] = (out[name] * factor).astype(out[name].dtype)
    return out
```

```python
from contextlib import ExitStack

import numpy as np
import concourse.bass as bass
from concourse import mybir

F32 = mybir.dt.float32
ALU = mybir.AluOpType
ACT = mybir.ActivationFunctionType
AX = mybir.AxisListType

P = 128
D = 128
BATCH = 8
SEQ = 256
N = BATCH * SEQ
T = N // P
NBLK = N // 512
LN_EPS = 1e-5
MASKED = -1e30


class Tally:

    def __init__(self, sem):
        self.sem, self.before = sem, 0

    def wait(self, eng, n):
        eng.wait_ge(self.sem, self.before + n)

    def close(self, total):
        self.before += total


class Core:

    def __init__(self, nc, ctx):
        self.nc, self.ctx, self.tallies = nc, ctx, {}
        self.X = self.keep("X", [P, T, D])
        self.XT = self.keep("XT", [P, N])
        self.ident = self.keep("ident", [P, P])
        self.ones = self.keep("ones", [P, P])

    def keep(self, name, shape, dt=F32):
        return self.ctx.enter_context(self.nc.sbuf_tensor(name, shape, dt))

    def tally(self, name):
        if name not in self.tallies:
            self.tallies[name] = Tally(self.ctx.enter_context(self.nc.semaphore(name)))
        return self.tallies[name]


def setup_stage(k, x_in):
    nc = k.nc
    loaded, made, turned, copied = (k.tally(n) for n in ("loaded", "made", "ln_turned", "ln_copied"))
    with nc.psum_tensor("ps_setup", [P, 4, 512], F32) as ps, nc.Block() as block:
        @block.sync
        def _(sp):
            sp.dma_start(k.X[:], x_in.rearrange("b (t p) d -> p (b t) d", p=P)).then_inc(loaded.sem, 16)

        @block.gpsimd
        def _(pool):
            nc.gpsimd.memset(k.ident[:], 0.0).then_inc(made.sem, 1)
            made.wait(pool, 1)
            nc.gpsimd.affine_select(out=k.ident[:], in_=k.ident[:], compare_op=ALU.not_equal, fill=1.0,
                                    base=0, pattern=[[-1, P]], channel_multiplier=1).then_inc(made.sem, 1)
            nc.gpsimd.memset(k.ones[:], 1.0).then_inc(made.sem, 1)
            made.wait(pool, 3)

        @block.tensor
        def _(pe):
            loaded.wait(pe, 16)
            made.wait(pe, 2)
            for g in range(4):
                for j in range(4):
                    t = nc.tensor.transpose(ps[:, g, j * P:(j + 1) * P], k.X[:, 4 * g + j, :], k.ident[:])
                t.then_inc(turned.sem, 1)

        @block.scalar
        def _(act):
            for g in range(4):
                turned.wait(act, g + 1)
                nc.scalar.activation(k.XT[:, g * 512:(g + 1) * 512], ps[:, g, :], ACT.Copy).then_inc(copied.sem, 1)
    loaded.close(16)
    made.close(3)
    turned.close(4)
    copied.close(4)


def layernorm_stage(k, name, turn=True):
    nc = k.nc
    asked, rooted, scaled, turned, copied = (
        k.tally(n) for n in ("ln_asked", "ln_rooted", "ln_scaled", "ln_turned", "ln_copied"))
    with ExitStack() as s:
        stats = s.enter_context(nc.sbuf_tensor(f"{name}_stats", [P, T, 6], F32))
        agg = s.enter_context(nc.sbuf_tensor(f"{name}_agg", [P, T, 2], F32))
        vare = s.enter_context(nc.sbuf_tensor(f"{name}_vare", [P, T], F32))
        root = s.enter_context(nc.sbuf_tensor(f"{name}_root", [P, T], F32))
        rstd = s.enter_context(nc.sbuf_tensor(f"{name}_rstd", [P, T], F32))
        t0 = s.enter_context(nc.sbuf_tensor(f"{name}_t0", [P, T], F32))
        ps = s.enter_context(nc.psum_tensor(f"{name}_ps", [P, 4, 512], F32))
        block = s.enter_context(nc.Block())

        @block.vector
        def _(dve):
            for t in range(T):
                nc.vector.bn_stats(stats[:, t, :], k.X[:, t, :])
            dve.drain()
            for t in range(T):
                nc.vector.bn_aggr(agg[:, t, :], stats[:, t, :])
            dve.drain()
            nc.vector.tensor_scalar(vare[:], agg[:, :, 1], LN_EPS, None, ALU.add).then_inc(asked.sem, 1)
            rooted.wait(dve, 1)
            inverse_root(nc, dve, rstd[:], root[:], vare[:], t0[:])
            for t in range(T):
                ins = nc.vector.tensor_scalar(k.X[:, t, :], k.X[:, t, :], agg[:, t, 0:1], rstd[:, t:t + 1],
                                              ALU.subtract, ALU.mult)
                if t % 4 == 3:
                    ins.then_inc(scaled.sem, 1)

        @block.scalar
        def _(act):
            asked.wait(act, 1)
            nc.scalar.activation(root[:], vare[:], ACT.Sqrt).then_inc(rooted.sem, 1)
            if turn:
                for g in range(4):
                    turned.wait(act, g + 1)
                    nc.scalar.activation(k.XT[:, g * 512:(g + 1) * 512], ps[:, g, :], ACT.Copy)\
                        .then_inc(copied.sem, 1)

        if turn:
            @block.tensor
            def _(pe):
                for g in range(4):
                    scaled.wait(pe, g + 1)
                    for j in range(4):
                        t = nc.tensor.transpose(ps[:, g, j * P:(j + 1) * P], k.X[:, 4 * g + j, :], k.ident[:])
                    t.then_inc(turned.sem, 1)
    asked.close(1)
    rooted.close(1)
    scaled.close(4)
    if turn:
        turned.close(4)
        copied.close(4)


HEADS = 16
HD = D // HEADS


def attention_stage(k, w_q, w_k, w_v, w_o):
    nc = k.nc
    KC = SEQ // P
    SC = P + SEQ
    slopes = (np.float32(1.0) / np.power(np.float32(256.0), (np.arange(HEADS, dtype=np.float32) + 1) / HEADS)).astype(np.float32)
    with ExitStack() as s:
        sb = lambda n, shape: s.enter_context(nc.sbuf_tensor(f"at_{n}", shape, F32))
        wq, wk, wv, wo = (sb(n, [P, D]) for n in ("wq", "wk", "wv", "wo"))
        QT, KT = sb("QT", [P, N]), sb("KT", [P, N])
        V = sb("V", [P, T, D])
        rel = sb("rel", [P, SEQ])
        bias = sb("bias", [P, HEADS, SEQ])
        hmask = sb("hmask", [P, HEADS])
        qm = sb("qm", [P, HEADS, SEQ])
        S = sb("S", [P, 2, SC])
        nmax = sb("nmax", [P, HEADS, KC])
        rsum = sb("rsum", [P, HEADS, KC])
        rinv = sb("rinv", [P, HEADS, KC])
        Pr = sb("Pr", [P, 2, SC])
        PT = sb("PT", [P, 2, SC])
        O = sb("O", [P, T, D])
        OT = sb("OT", [P, N])
        sem = lambda n: k.tally(f"at_{n}")
        w_in, biased, masked, projected, proj_out, v_out = map(sem, ("w_in", "biased", "masked", "projected", "proj_out", "v_out"))
        psA_cm = nc.psum_tensor("at_psA", [P, 8, 512], F32)
        with psA_cm as psA, nc.Block() as block:
            @block.sync
            def _(sp):
                for t, w in ((wq, w_q), (wk, w_k), (wv, w_v), (wo, w_o)):
                    sp.dma_start(t[:], w).then_inc(w_in.sem, 16)

            @block.gpsimd
            def _(pool):
                nc.gpsimd.iota(rel[:], [[1, SEQ]], base=-P, channel_multiplier=-1,
                               allow_small_or_imprecise_dtypes=True).then_inc(biased.sem, 1)
                nc.gpsimd.memset(hmask[:], 1.0).then_inc(masked.sem, 1)
                masked.wait(pool, 1)
                nc.gpsimd.affine_select(out=hmask[:], in_=hmask[:], compare_op=ALU.is_ge, fill=0.0, base=0,
                                        pattern=[[-HD, HEADS]], channel_multiplier=1).then_inc(masked.sem, 1)
                masked.wait(pool, 2)
                nc.gpsimd.affine_select(out=hmask[:], in_=hmask[:], compare_op=ALU.is_ge, fill=0.0, base=HD - 1,
                                        pattern=[[HD, HEADS]], channel_multiplier=-1).then_inc(masked.sem, 1)
                biased.wait(pool, 2)
                nc.gpsimd.affine_select(out=bias[:], in_=bias[:], compare_op=ALU.is_ge, fill=MASKED, base=P,
                                        pattern=[[0, HEADS], [-1, SEQ]], channel_multiplier=1)\
                    .then_inc(biased.sem, 1)

            @block.tensor
            def _(pe):
                w_in.wait(pe, 64)
                for g in range(4):
                    nc.tensor.matmul(psA[:, g, :], wq[:], k.XT[:, g * 512:(g + 1) * 512], start=True, stop=True)\
                        .then_inc(projected.sem, 1)
                    nc.tensor.matmul(psA[:, 4 + g, :], wk[:], k.XT[:, g * 512:(g + 1) * 512], start=True, stop=True)\
                        .then_inc(projected.sem, 1)
                for g in range(4):
                    proj_out.wait(pe, g + 1)
                    for j in range(4):
                        t = 4 * g + j
                        m = nc.tensor.matmul(psA[:, g, j * P:(j + 1) * P], k.XT[:, t * P:(t + 1) * P], wv[:],
                                             start=True, stop=True)
                    m.then_inc(projected.sem, 1)

            @block.scalar
            def _(act):
                for g in range(4):
                    projected.wait(act, 2 * g + 1)
                    nc.scalar.activation(QT[:, g * 512:(g + 1) * 512], psA[:, g, :], ACT.Copy,
                                         scale=float(1.0 / np.sqrt(np.float32(HD)))).then_inc(proj_out.sem, 1)
                for g in range(4):
                    projected.wait(act, 8 + g + 1)
                    nc.scalar.activation(V[:, 4 * g:4 * g + 4, :], psA[:, g, :].rearrange("p (t d) -> p t d", d=D),
                                         ACT.Copy).then_inc(v_out.sem, 1)

            @block.vector
            def _(dve):
                biased.wait(dve, 1)
                for h in range(HEADS):
                    m = nc.vector.tensor_scalar(bias[:, h, :], rel[:], float(slopes[h]), None, ALU.mult)
                m.then_inc(biased.sem, 1)
                for g in range(4):
                    projected.wait(dve, 2 * g + 2)
                    nc.vector.tensor_copy(KT[:, g * 512:(g + 1) * 512], psA[:, 4 + g, :])

        scored, biasd, expd, turned, tcopied, weighted, normed, qmasked, begun, groups_begun = map(
            sem, ("scored", "biasd", "expd", "turned", "tcopied", "weighted", "normed", "qmasked", "begun",
                  "groups_begun"))
        QG = 4
        NG = HEADS // QG
        with ExitStack() as ps_ctx:
            psS = [ps_ctx.enter_context(nc.psum_tensor(f"at_psS{i}", [P, 512], F32)) for i in range(2)]
            psT = [ps_ctx.enter_context(nc.psum_tensor(f"at_psT{i}", [P, 512], F32)) for i in range(2)]
            psO = ps_ctx.enter_context(nc.psum_tensor("at_psO", [P, 512], F32))
            block = ps_ctx.enter_context(nc.Block())

            @block.gpsimd
            def _(pool):
                with pool.Fori(0, BATCH) as b:
                    for g in range(NG):
                        pool.wait_ge(scored.sem, HEADS * b + (g + 1) * QG)
                        pool.sem_inc(groups_begun.sem, 1)
                        nc.gpsimd.tensor_tensor(
                            qm[:, g * QG:(g + 1) * QG, :],
                            QT[:, bass.ds(b * SEQ, SEQ)].unsqueeze(1).to_broadcast([P, QG, SEQ]),
                            hmask[:, g * QG:(g + 1) * QG].unsqueeze(2).to_broadcast([P, QG, SEQ]),
                            ALU.mult).then_inc(qmasked.sem, 1)

            @block.tensor
            def _(pe):
                pe.sem_inc(scored.sem, HEADS)
                with pe.Fori(0, BATCH) as b:
                    def scores(h):
                        if h % QG == 0:
                            pe.wait_ge(qmasked.sem, NG * b + (h // QG + 1))
                        if h >= 2:
                            pe.wait_ge(biasd.sem, HEADS * b + (h - 1))
                        nc.tensor.matmul(psS[h % 2][:, 0:P], qm[:, h, 0:P], KT[:, bass.ds(b * SEQ, P)],
                                         start=True, stop=True)
                        nc.tensor.matmul(psS[h % 2][:, P:SC], qm[:, h, P:SEQ], KT[:, bass.ds(b * SEQ, SEQ)],
                                         start=True, stop=True).then_inc(scored.sem, 1)

                    def turn(h):
                        pe.wait_ge(expd.sem, HEADS * b + (h + 1))
                        if h >= 2:
                            pe.wait_ge(tcopied.sem, HEADS * b + (h - 1))
                        for j in range(3):
                            m = nc.tensor.transpose(psT[h % 2][:, j * P:(j + 1) * P], Pr[:, h % 2, j * P:(j + 1) * P],
                                                    k.ident[:])
                        m.then_inc(turned.sem, 1)

                    def weigh(h):
                        pe.wait_ge(tcopied.sem, HEADS * b + (h + 1))
                        if h == 0:
                            pe.wait_ge(normed.sem, b + 1)
                        o0 = psO[:, h * HD:(h + 1) * HD]
                        o1 = psO[:, D + h * HD:D + (h + 1) * HD]
                        v0 = V[:, bass.ds(b * KC, 1), h * HD:(h + 1) * HD].rearrange("p a d -> p (a d)")
                        v1 = V[:, bass.ds(b * KC + 1, 1), h * HD:(h + 1) * HD].rearrange("p a d -> p (a d)")
                        nc.tensor.matmul(o0, PT[:, h % 2, 0:P], v0, start=True, stop=True)
                        nc.tensor.matmul(o1, PT[:, h % 2, P:2 * P], v0, start=True, stop=False)
                        nc.tensor.matmul(o1, PT[:, h % 2, 2 * P:SC], v1, start=False, stop=True)\
                            .then_inc(weighted.sem, 1)

                    for h in range(HEADS + 2):
                        if h < HEADS:
                            scores(h)
                        if 1 <= h <= HEADS:
                            turn(h - 1)
                        if h >= 2:
                            weigh(h - 2)

            @block.vector
            def _(dve):
                dve.sem_inc(normed.sem, 1)
                with dve.Fori(0, BATCH) as b:
                    def add_bias(h):
                        dve.wait_ge(scored.sem, HEADS * b + (HEADS + h + 1))
                        if h >= 2:
                            dve.wait_ge(expd.sem, HEADS * b + (h - 1))
                        dve.sem_inc(begun.sem, 1)
                        nc.vector.tensor_tensor_reduce(S[:, h % 2, 0:P], psS[h % 2][:, 0:P], bias[:, h, P:SEQ], -1.0,
                                                       -MASKED, ALU.add, ALU.min, nmax[:, h, 0:1])
                        nc.vector.tensor_tensor_reduce(S[:, h % 2, P:SC], psS[h % 2][:, P:SC], bias[:, h, :], -1.0,
                                                       -MASKED, ALU.add, ALU.min, nmax[:, h, 1:2])\
                            .then_inc(biasd.sem, 1)

                    def copy_turned(h):
                        dve.wait_ge(turned.sem, HEADS * b + (h + 1))
                        if h >= 2:
                            dve.wait_ge(weighted.sem, HEADS * b + (h - 1))
                        nc.vector.tensor_copy(PT[:, h % 2, :], psT[h % 2][:, 0:SC]).then_inc(tcopied.sem, 1)

                    for h in range(HEADS + 1):
                        if h < HEADS:
                            add_bias(h)
                        if h >= 1:
                            copy_turned(h - 1)
                    nc.vector.reciprocal(rinv[:], rsum[:])
                    dve.drain()
                    dve.wait_ge(weighted.sem, HEADS * b + HEADS)
                    for qt in range(KC):
                        m = nc.vector.tensor_tensor(
                            O[:, bass.ds(b * KC + qt, 1), :].rearrange("p a (h e) -> p (a h) e", e=HD),
                            psO[:, qt * D:(qt + 1) * D].rearrange("p (h e) -> p h e", e=HD),
                            rinv[:, :, qt:qt + 1].to_broadcast([P, HEADS, HD]), ALU.mult)
                    m.then_inc(normed.sem, 1)

            @block.scalar
            def _(act):
                with act.Fori(0, BATCH) as b:
                    for h in range(HEADS):
                        act.wait_ge(biasd.sem, HEADS * b + (h + 1))
                        if h >= 2:
                            act.wait_ge(turned.sem, HEADS * b + (h - 1))
                        if h == 0:
                            act.wait_ge(normed.sem, b + 1)
                        nc.scalar.activation(Pr[:, h % 2, 0:P], S[:, h % 2, 0:P], ACT.Exp, scale=-1.0,
                                             bias=nmax[:, h, 0:1], accum_out=rsum[:, h, 0:1])
                        nc.scalar.activation(Pr[:, h % 2, P:SC], S[:, h % 2, P:SC], ACT.Exp, scale=-1.0,
                                             bias=nmax[:, h, 1:2], accum_out=rsum[:, h, 1:2]).then_inc(expd.sem, 1)

        project_and_add_stage(k, "at", O, OT, wo)
        w_in.close(64)
        biased.close(3)
        masked.close(3)
        projected.close(12)
        proj_out.close(4)
        v_out.close(4)


def project_and_add_stage(k, name, O, OT, w):
    nc = k.nc
    turned, copied, projected = (k.tally(f"pr_{n}") for n in ("turned", "copied", "projected"))
    with nc.psum_tensor(f"{name}_pr_psT", [P, 4, 512], F32) as psT, \
            nc.psum_tensor(f"{name}_pr_psR", [P, 4, 512], F32) as psR, nc.Block() as block:
        @block.tensor
        def _(pe):
            if O is not None:
                for g in range(4):
                    for j in range(4):
                        m = nc.tensor.transpose(psT[:, g, j * P:(j + 1) * P], O[:, 4 * g + j, :], k.ident[:])
                    m.then_inc(turned.sem, 1)
            for g in range(4):
                if O is not None:
                    copied.wait(pe, g + 1)
                for j in range(4):
                    t = 4 * g + j
                    m = nc.tensor.matmul(psR[:, g, j * P:(j + 1) * P], OT[:, t * P:(t + 1) * P], w[:],
                                         start=True, stop=True)
                m.then_inc(projected.sem, 1)

        if O is not None:
            @block.scalar
            def _(act):
                for g in range(4):
                    turned.wait(act, g + 1)
                    nc.scalar.activation(OT[:, g * 512:(g + 1) * 512], psT[:, g, :], ACT.Copy).then_inc(copied.sem, 1)

        @block.vector
        def _(dve):
            for g in range(4):
                projected.wait(dve, g + 1)
                x = k.X[:, 4 * g:4 * g + 4, :]
                nc.vector.tensor_tensor(x, x, psR[:, g, :].rearrange("p (t d) -> p t d", d=D), ALU.add)
    projected.close(4)
    if O is not None:
        turned.close(4)
        copied.close(4)


PAD = -3e38
TAKEN = -1e38
ROUND = float(1.5 * 2 ** 23)


def route_stage(k, name, comb, w_r, r_bias, experts, top, of_probs, renormed, always=0, capacity=None,
                sort=None):
    nc = k.nc
    E = experts
    w_in, made, logits, asked, exped, counted, counts = (
        k.tally(f"rt_{n}") for n in ("w_in", "made", "logits", "asked", "exped", "counted", "counts"))
    with ExitStack() as s:
        sb = lambda n, shape: s.enter_context(nc.sbuf_tensor(f"{name}_rt_{n}", shape, F32))
        wr = sb("wr", [P, E])
        rb = sb("rb", [P, E])
        L = sb("L", [P, T, E + 8])
        R = sb("R", [P, T, E + 8])
        m8, rep8 = sb("m8", [P, T, 8]), sb("rep8", [P, T, 8])
        ex, sel = sb("ex", [P, T, E]), sb("sel", [P, T, E])
        total, inv = sb("total", [P, T]), sb("inv", [P, T])
        psL = s.enter_context(nc.psum_tensor(f"{name}_psL", [P, T, E], F32))
        ranked = capacity or sort
        if sort:
            weight, slot, tile_expert = sort
            tiles = tile_expert.shape[1]
            count, first, last = (sb(n, [P, E]) for n in ("count", "first", "last"))
            place = sb("place", [P, T])
            tile_no = sb("tile_no", [1, tiles])
            past = sb("past", [1, tiles, E])
            psN = s.enter_context(nc.psum_tensor(f"{name}_psN", [P, E], F32))
        if ranked:
            before, tri = sb("before", [P, T, E]), sb("tri", [P, P])
            psC = s.enter_context(nc.psum_tensor(f"{name}_psC", [P, T, E], F32))
        block = s.enter_context(nc.Block())
        bc = lambda ap, n: ap.unsqueeze(2).to_broadcast([P, T, n])

        @block.sync
        def _(sp):
            sp.dma_start(wr[:], w_r).then_inc(w_in.sem, 16)
            if r_bias is not None:
                sp.dma_start(rb[:], r_bias.partition_broadcast(P)).then_inc(w_in.sem, 16)

        @block.gpsimd
        def _(pool):
            if sort:
                nc.gpsimd.iota(tile_no[:], [[1, tiles]], base=0, channel_multiplier=0,
                               allow_small_or_imprecise_dtypes=True)
            if ranked:
                nc.gpsimd.affine_select(out=tri[:], in_=k.ones[:], compare_op=ALU.is_ge, fill=0.0, base=-1,
                                        pattern=[[1, P]], channel_multiplier=-1).then_inc(made.sem, 1)

        @block.tensor
        def _(pe):
            w_in.wait(pe, 32 if r_bias is not None else 16)
            for t in range(T):
                m = nc.tensor.matmul(psL[:, t, :], k.XT[:, t * P:(t + 1) * P], wr[:], start=True, stop=True)
            m.then_inc(logits.sem, 1)
            if ranked:
                made.wait(pe, 1)
                counted.wait(pe, 1)
                half = min(T, 512 // E)
                for j in range(T // half):
                    o = psC[:, j * half:(j + 1) * half, :].rearrange("p t e -> p (t e)")
                    nc.tensor.matmul(o, tri[:], sel[:, j * half:(j + 1) * half, :].rearrange("p t e -> p (t e)"),
                                     start=True, stop=False)
                    m = nc.tensor.matmul(o, k.ones[:],
                                         before[:, j * half:(j + 1) * half, :].rearrange("p t e -> p (t e)"),
                                         start=False, stop=True)
                if sort:
                    nc.tensor.matmul(psN[:], k.ones[:], before[:, T - 1, :], start=True, stop=False)
                    m = nc.tensor.matmul(psN[:], k.ones[:], sel[:, T - 1, :], start=False, stop=True)
                m.then_inc(counts.sem, 1)

        @block.scalar
        def _(act):
            asked.wait(act, 1)
            nc.scalar.activation(ex[:], ex[:], ACT.Exp).then_inc(exped.sem, 1)

        @block.vector
        def _(dve):
            nc.vector.memset(L[:, :, E:E + 8], PAD)
            if always:
                nc.vector.memset(comb[:, :, E:E + always], 1.0)
            logits.wait(dve, 1)
            if r_bias is not None:
                nc.vector.tensor_tensor(L[:, :, 0:E], psL[:], rb[:].unsqueeze(1).to_broadcast([P, T, E]), ALU.add)
            else:
                nc.vector.tensor_copy(L[:, :, 0:E], psL[:])
            dve.drain()
            for t in range(T):
                nc.vector.max(m8[:, t, :], L[:, t, 0:E])
            dve.drain()
            nc.vector.tensor_tensor(ex[:], L[:, :, 0:E], m8[:, :, 0:1].to_broadcast([P, T, E]), ALU.subtract)\
                .then_inc(asked.sem, 1)
            exped.wait(dve, 1)
            if of_probs:
                nc.vector.tensor_reduce(total[:], ex[:], AX.X, ALU.add)
                dve.drain()
                nc.vector.reciprocal(inv[:], total[:])
                dve.drain()
                nc.vector.tensor_tensor(ex[:], ex[:], bc(inv[:], E), ALU.mult)
                dve.drain()
                nc.vector.tensor_copy(L[:, :, 0:E], ex[:])
                dve.drain()
                for t in range(T):
                    nc.vector.max(m8[:, t, :], L[:, t, 0:E])
                dve.drain()
            nc.vector.tensor_copy(rep8[:], m8[:])
            if top < 8:
                dve.drain()
                nc.vector.memset(rep8[:, :, top:8], PAD)
            dve.drain()
            for t in range(T):
                nc.vector.match_replace(R[:, t, :], rep8[:, t, :], L[:, t, :], TAKEN)
            dve.drain()
            nc.vector.tensor_tensor(sel[:], R[:, :, 0:E], L[:, :, 0:E], ALU.not_equal)
            dve.drain()
            c = comb[:, :, 0:E]
            nc.vector.tensor_tensor(c, ex[:], sel[:], ALU.mult)
            dve.drain()
            if renormed:
                nc.vector.tensor_reduce(total[:], c, AX.X, ALU.add)
                dve.drain()
                nc.vector.reciprocal(inv[:], total[:])
                dve.drain()
                nc.vector.tensor_tensor(c, c, bc(inv[:], E), ALU.mult)
                dve.drain()
            if ranked:
                nc.vector.memset(before[:, 0, :], 0.0)
                for t in range(1, T):
                    dve.drain()
                    m = nc.vector.tensor_tensor(before[:, t, :], before[:, t - 1, :], sel[:, t - 1, :], ALU.add)
                m.then_inc(counted.sem, 1)
                counts.wait(dve, 1)
            if capacity:
                nc.vector.scalar_tensor_tensor(out=c, in0=psC[:], scalar=float(capacity), in1=c,
                                               op0=ALU.is_lt, op1=ALU.mult)
            if sort:
                made.wait(dve, 1)
                nc.vector.tensor_copy(weight[:], m8[:, :, 0])
                nc.vector.tensor_scalar(count[:], psN[:], 1.0 / P, 63.5 / P, ALU.mult, ALU.add)
                dve.drain()
                nc.vector.tensor_scalar(count[:], count[:], ROUND, None, ALU.add)
                dve.drain()
                nc.vector.tensor_scalar(count[:], count[:], -ROUND, None, ALU.add)
                dve.drain()
                nc.vector.tensor_tensor_scan(last[:], k.ones[:, 0:E], count[:], 0.0, ALU.mult, ALU.add)
                dve.drain()
                nc.vector.tensor_tensor(first[:], last[:], count[:], ALU.subtract)
                dve.drain()
                nc.vector.tensor_scalar(first[:], first[:], float(P), None, ALU.mult)
                dve.drain()
                nc.vector.tensor_tensor(before[:], psC[:], first[:].unsqueeze(1).to_broadcast([P, T, E]), ALU.add)
                dve.drain()
                nc.vector.tensor_tensor(before[:], before[:], sel[:], ALU.mult)
                dve.drain()
                nc.vector.tensor_reduce(place[:], before[:], AX.X, ALU.add)
                dve.drain()
                nc.vector.tensor_copy(slot[:], place[:])
                nc.vector.tensor_tensor(past[:], tile_no[:].unsqueeze(2).to_broadcast([1, tiles, E]),
                                        last[0:1, :].unsqueeze(1).to_broadcast([1, tiles, E]), ALU.is_ge)
                dve.drain()
                nc.vector.tensor_reduce(tile_no[:], past[:], AX.X, ALU.add)
                dve.drain()
                nc.vector.tensor_scalar(tile_expert[:], tile_no[:], float(E - 1), None, ALU.min)
    w_in.close(32 if r_bias is not None else 16)
    logits.close(1)
    asked.close(1)
    exped.close(1)
    if ranked:
        for t in (made, counted, counts):
            t.close(1)


def experts_stage(k, name, comb, w_up, w_down, count, chunk, chunks, gated, biased, acc, clear=False):
    nc = k.nc
    WU = chunks * chunk * (2 if gated else 1) + (2 * chunks if biased else 0)
    UNITS = NBLK * chunks
    up_done, silu_done, hid_done, down_done, acc_done = (
        k.tally(f"ex_{n}") for n in ("up_done", "silu_done", "hid_done", "down_done", "acc_done"))
    w_in = [k.tally(f"ex_w_in{i}") for i in range(2)]
    pairs = count // 2
    odd = count % 2
    looped = pairs if odd else pairs - 1
    with ExitStack() as s:
        wu = [s.enter_context(nc.sbuf_tensor(f"{name}_wu{i}", [P, WU], F32)) for i in range(2)]
        wd = [s.enter_context(nc.sbuf_tensor(f"{name}_wd{i}", [chunk, chunks * D], F32)) for i in range(2)]
        sg = s.enter_context(nc.sbuf_tensor(f"{name}_sg", [chunk, 2, 512], F32))
        hid = s.enter_context(nc.sbuf_tensor(f"{name}_hid", [chunk, 2, 512], F32))
        psG = s.enter_context(nc.psum_tensor(f"{name}_psG", [P, 2, 512], F32))
        psU = s.enter_context(nc.psum_tensor(f"{name}_psU", [P, 2, 512], F32)) if gated else None
        psD = s.enter_context(nc.psum_tensor(f"{name}_psD", [P, 2, 512], F32))
        block = s.enter_context(nc.Block())

        def steps(first, experts, follow):
            u = [(e, b, c) for e in range(experts) for b in range(NBLK) for c in range(chunks)]
            for j, unit in enumerate(u):
                nxt = u[j + 1] if j + 1 < len(u) else ((0, 0, 0) if follow else None)
                yield j, unit, nxt

        def engine(eng, body):
            if looped:
                with eng.Fori(0, looped) as i:
                    body(i, 2, True)
            if odd:
                body(pairs, 1, False)
            else:
                body(pairs - 1, 2, False)

        @block.sync
        def _(sp):
            def load(e, half):
                sp.dma_start(wu[half][:], w_up[bass.ds(e, 1), :, :].rearrange("a p f -> p (a f)"))\
                    .then_inc(w_in[half].sem, 16)
                sp.dma_start(wd[half][:], w_down[bass.ds(e, 1), :, :].rearrange("a p f -> p (a f)"))\
                    .then_inc(w_in[half].sem, 16)

            load(0, 0)
            if count > 1:
                load(1, 1)
            if pairs > 1:
                with sp.Fori(1, pairs) as i:
                    for half in range(2):
                        sp.wait_ge(down_done.sem, 2 * NBLK * i + (down_done.before + NBLK * (half - 1)))
                        load(2 * i + half, half)
            if odd:
                down_done.wait(sp, NBLK * (count - 2))
                load(count - 1, 0)

        @block.tensor
        def _(pe):
            def up(i, j, unit):
                half, b, c = unit
                if b == 0 and c == 0:
                    pe.wait_ge(w_in[half].sem, 32 * i + (w_in[half].before + 32))
                pe.wait_ge(hid_done.sem, 2 * UNITS * i + (hid_done.before + j + 1))
                x = k.XT[:, b * 512:(b + 1) * 512]
                w = wu[half]
                m = nc.tensor.matmul(psG[0:chunk, j % 2, :], w[:, c * chunk:(c + 1) * chunk], x, start=True, stop=True)
                if gated:
                    o = (chunks + c) * chunk
                    m = nc.tensor.matmul(psU[0:chunk, j % 2, :], w[:, o:o + chunk], x, start=True, stop=True)
                m.then_inc(up_done.sem, 1)

            def down(i, j, unit):
                half, b, c = unit
                pe.wait_ge(hid_done.sem, 2 * UNITS * i + (hid_done.before + j + 3))
                if c == 0:
                    pe.wait_ge(acc_done.sem, 2 * NBLK * i + (acc_done.before + NBLK * half + b + 1))
                for t in range(4):
                    m = nc.tensor.matmul(psD[:, b % 2, t * P:(t + 1) * P], hid[:, j % 2, t * P:(t + 1) * P],
                                         wd[half][:, c * D:(c + 1) * D], start=(c == 0 and t == 0),
                                         stop=(c == chunks - 1 and t == 3), skip_group_check=True)
                if c == chunks - 1:
                    m.then_inc(down_done.sem, 1)

            def body(i, experts, follow):
                for j, unit, nxt in steps(i, experts, follow):
                    if nxt is not None:
                        if j + 1 < experts * UNITS:
                            up(i, j + 1, nxt)
                        else:
                            up(i + 1, 0, nxt)
                    down(i, j, unit)

            up(0, 0, (0, 0, 0))
            engine(pe, body)

        @block.scalar
        def _(act):
            def body(i, experts, follow):
                for j, (half, b, c), _ in steps(i, experts, follow):
                    act.wait_ge(up_done.sem, 2 * UNITS * i + (up_done.before + j + 1))
                    w = wu[half]
                    o = chunks * chunk * 2 + c
                    bias = {"bias": w[0:chunk, o:o + 1]} if biased else {}
                    if gated:
                        nc.scalar.activation(sg[:, j % 2, :], psG[0:chunk, j % 2, :], ACT.Silu, **bias)\
                            .then_inc(silu_done.sem, 1)
                    else:
                        nc.scalar.activation(hid[:, j % 2, :], psG[0:chunk, j % 2, :], ACT.Silu, **bias)\
                            .then_inc(hid_done.sem, 1)

            if not gated:
                act.sem_inc(hid_done.sem, 2)
            engine(act, body)

        @block.vector
        def _(dve):
            def hide(i, j, unit):
                half, b, c = unit
                dve.wait_ge(silu_done.sem, 2 * UNITS * i + (silu_done.before + j + 1))
                w = wu[half]
                o = chunks * chunk * 2 + chunks + c
                if biased:
                    m = nc.vector.scalar_tensor_tensor(out=hid[:, j % 2, :], in0=psU[0:chunk, j % 2, :],
                                                       scalar=w[0:chunk, o:o + 1], in1=sg[:, j % 2, :],
                                                       op0=ALU.add, op1=ALU.mult)
                else:
                    m = nc.vector.tensor_tensor(hid[:, j % 2, :], psU[0:chunk, j % 2, :], sg[:, j % 2, :], ALU.mult)
                m.then_inc(hid_done.sem, 1)

            def add(i, unit):
                half, b, c = unit
                dve.wait_ge(down_done.sem, 2 * NBLK * i + (down_done.before + NBLK * half + b + 1))
                for t in range(4):
                    a = acc[:, 4 * b + t, :]
                    m = nc.vector.scalar_tensor_tensor(out=a, in0=psD[:, b % 2, t * P:(t + 1) * P],
                                                       scalar=comb[:, 4 * b + t, bass.ds(2 * i + half, 1)], in1=a,
                                                       op0=ALU.mult, op1=ALU.add)
                m.then_inc(acc_done.sem, 1)

            def body(i, experts, follow):
                for j, unit, nxt in steps(i, experts, follow):
                    if gated and nxt is not None:
                        if j + 1 < experts * UNITS:
                            hide(i, j + 1, nxt)
                        else:
                            hide(i + 1, 0, nxt)
                    if unit[2] == chunks - 1:
                        add(i, unit)

            if clear:
                nc.vector.memset(acc[:], 0.0)
                dve.drain()
            dve.sem_inc(acc_done.sem, 2)
            if gated:
                dve.sem_inc(hid_done.sem, 2)
                hide(0, 0, (0, 0, 0))
            engine(dve, body)
    up_done.close(count * UNITS)
    if gated:
        silu_done.close(count * UNITS)
    hid_done.close(count * UNITS + 2)
    down_done.close(count * NBLK)
    acc_done.close(count * NBLK + 2)
    w_in[0].close(32 * (pairs + odd))
    w_in[1].close(32 * pairs)


def moe_l0_stage(k, a):
    E, F = 8, 256
    nc = k.nc
    with nc.sbuf_tensor("m0_comb", [P, T, E], F32) as comb:
        route_stage(k, "m0", comb, a["L0_ffn_router"], None, E, top=2, of_probs=False, renormed=True)
        with nc.sbuf_tensor("m0_combT", [E, N], F32) as combT, nc.sbuf_tensor("m0_b3", [E, D], F32) as b3:
            turn_comb_stage(k, "m0", comb, combT, b3, a["L0_ffn_b3"])
            project_and_add_stage(k, "m0", None, combT, b3)
        experts_stage(k, "m0", comb, a["L0_ffn_up"], a["L0_ffn_down"], E, P, F // P, True, True, k.X)


def turn_comb_stage(k, name, comb, combT, b3_sb, b3):
    nc = k.nc
    loaded, turned, copied = (k.tally(f"tc_{n}") for n in ("loaded", "turned", "copied"))
    E = combT.shape[0]
    with nc.psum_tensor(f"{name}_psTC", [P, 4, 512], F32) as ps, nc.Block() as block:
        @block.sync
        def _(sp):
            sp.dma_start(b3_sb[:], b3).then_inc(loaded.sem, 16)
            loaded.wait(sp, 16)

        @block.tensor
        def _(pe):
            for g in range(4):
                for j in range(4):
                    m = nc.tensor.transpose(ps[0:E, g, j * P:(j + 1) * P], comb[:, 4 * g + j, :], k.ident[:])
                m.then_inc(turned.sem, 1)

        @block.scalar
        def _(act):
            for g in range(4):
                turned.wait(act, g + 1)
                nc.scalar.activation(combT[:, g * 512:(g + 1) * 512], ps[0:E, g, :], ACT.Copy).then_inc(copied.sem, 1)
    loaded.close(16)
    turned.close(4)
    copied.close(4)


def moe_l1_stage(k, a):
    E, F, S = 16, 64, 2
    with k.nc.sbuf_tensor("m1_comb", [P, T, E + S], F32) as comb:
        route_stage(k, "m1", comb, a["L1_ffn_router"], a["L1_ffn_router_bias"], E, top=2, of_probs=False,
                    renormed=True, always=S)
        experts_stage(k, "m1", comb, a["L1_ffn_up"], a["L1_ffn_down"], E + S, F, 1, True, False, k.X)


def moe_l2_stage(k, a):
    E, F, S = 64, 96, 1
    with k.nc.sbuf_tensor("m2_comb", [P, T, E + S], F32) as comb:
        route_stage(k, "m2", comb, a["L2_ffn_router"], None, E, top=8, of_probs=True, renormed=True,
                    always=S, capacity=64)
        experts_stage(k, "m2", comb, a["L2_ffn_up"], a["L2_ffn_down"], E + S, F, 1, True, False, k.X)


def turn_stage(k, name, Y):
    nc = k.nc
    turned, copied = k.tally("ln_turned"), k.tally("ln_copied")
    with nc.psum_tensor(f"{name}_psY", [P, 4, 512], F32) as ps, nc.Block() as block:
        @block.tensor
        def _(pe):
            for g in range(4):
                for j in range(4):
                    m = nc.tensor.transpose(ps[:, g, j * P:(j + 1) * P], Y[:, 4 * g + j, :], k.ident[:])
                m.then_inc(turned.sem, 1)

        @block.scalar
        def _(act):
            for g in range(4):
                turned.wait(act, g + 1)
                nc.scalar.activation(k.XT[:, g * 512:(g + 1) * 512], ps[:, g, :], ACT.Copy).then_inc(copied.sem, 1)
    turned.close(4)
    copied.close(4)


E3, F3, LAYERS = 16, 512, 4
SLOT_TILES = 32
UNROLL, AHEAD = 4, 7


def load_l3_weights(k, a):
    nc = k.nc
    k.W1, k.W2 = k.keep("W1", [P, E3, F3]), k.keep("W2", [P, E3, F3])
    k.sorted_x = nc.dram_tensor("sorted_x", (SLOT_TILES * P, D), F32).ap()
    k.sorted_y = nc.dram_tensor("sorted_y", (SLOT_TILES * P, D), F32).ap()
    loaded, zeroed, cleared = k.tally("l3_loaded"), k.tally("l3_zeroed"), k.tally("l3_cleared")
    zero = k.keep("zero", [P, D])
    with nc.Block() as block:
        @block.vector
        def _(dve):
            nc.vector.memset(zero[:], 0.0).then_inc(cleared.sem, 1)

        @block.sync
        def _(sp):
            for g in range(4):
                e = slice(4 * g, 4 * g + 4)
                sp.dma_start(k.W1[:, e, :], a["L3_ffn_up"][e].rearrange("e p f -> p e f")).then_inc(loaded.sem, 16)
                sp.dma_start(k.W2[:, e, :], a["L3_ffn_down"][e].rearrange("e p f -> p e f")).then_inc(loaded.sem, 16)
            cleared.wait(sp, 1)
            sp.dma_start(k.sorted_x.rearrange("(j p) d -> p j d", p=P),
                         zero[:].unsqueeze(1).to_broadcast([P, SLOT_TILES, D])).then_inc(zeroed.sem, 16)


def sorted_experts_stage(k, name, Y, slot, tile_expert):
    nc = k.nc
    C = F3 // P
    scattered, loaded_w, zeroed = k.tally("so_scattered"), k.tally("l3_loaded"), k.tally("l3_zeroed")
    x_in = [k.tally(f"so_x_in{i}") for i in range(4)]
    stored = [k.tally(f"so_stored{i}") for i in range(4)]
    turned_x, x_out, up_done, silu_done, turned_h, h_out, down_done, y_out = (
        k.tally(f"so_{n}") for n in
        ("turned_x", "x_out", "up_done", "silu_done", "turned_h", "h_out", "down_done", "y_out"))
    with ExitStack() as s:
        sb = lambda n, shape: s.enter_context(nc.sbuf_tensor(f"{name}_{n}", shape, F32))
        xs = [sb(f"xs{i}", [P, D]) for i in range(4)]
        ys = [sb(f"ys{i}", [P, D]) for i in range(4)]
        xT = [sb(f"xT{i}", [P, P]) for i in range(2)]
        h = [sb(f"h{i}", [P, F3]) for i in range(2)]
        hT = [sb(f"hT{i}", [P, F3]) for i in range(2)]
        pb = lambda n: s.enter_context(nc.psum_tensor(f"{name}_{n}", [P, 512], F32))
        psX, psH, psT, psY = ([pb(f"ps{n}{i}") for i in range(2)] for n in "XHTY")
        block = s.enter_context(nc.Block())
        tile_rows = lambda t, j: t.rearrange("(j p) d -> j p d", p=P)[bass.ds(j, 1), :, :]\
            .rearrange("a p d -> (a p) d")

        def steps(eng, step, last):
            for v in range(AHEAD):
                step(v, v % UNROLL)
            trips = (SLOT_TILES - AHEAD) // UNROLL
            with eng.Fori(0, trips) as i:
                for c in range(UNROLL):
                    step(i * UNROLL + (AHEAD + c), (AHEAD + c) % UNROLL)
            for v in range(AHEAD + trips * UNROLL, last):
                step(v, v % UNROLL)

        def inside(j):
            return not isinstance(j, int) or 0 <= j < SLOT_TILES

        def wait(eng, tally, n, per=1):
            if not isinstance(n, int) or n > 0:
                eng.wait_ge(tally.sem, n * per + tally.before)

        def round_wait(eng, tally, v, m, off=0):
            if isinstance(v, int):
                n = (v - m) // 4 + 1 - off
                if n > 0:
                    eng.wait_ge(tally.sem, 16 * n + tally.before)
            else:
                eng.wait_ge(tally.sem, v * 4 + (16 - 4 * m - 16 * off + tally.before))

        @block.gpsimd
        def _(pool):
            zeroed.wait(pool, 0) if zeroed.before else pool.wait_ge(zeroed.sem, 16)
            for t in range(T):
                pool.indirect_dma_start(k.sorted_x, bass.IndirectOffsetOnAxis(slot[:, t:t + 1], 0), Y[:, t, :], None)\
                    .then_inc(scattered.sem, 16)

        @block.sync
        def _(sp):
            scattered.wait(sp, 16 * T)

            def step(v, m):
                if inside(v):
                    wait(sp, turned_x, v - 3)
                    sp.dma_start(xs[m][:], tile_rows(k.sorted_x, v)).then_inc(x_in[m].sem, 16)
                j = v - 6
                if inside(j):
                    wait(sp, y_out, j + 1)
                    sp.dma_start(tile_rows(k.sorted_y, j), ys[(m - 6) % 4][:]).then_inc(stored[(m - 6) % 4].sem, 16)

            steps(sp, step, SLOT_TILES + 6)
            for t in stored:
                t.wait(sp, 16 * SLOT_TILES // 4)

        @block.tensor
        def _(pe):
            if loaded_w.before == 0:
                pe.wait_ge(loaded_w.sem, 128)

            def expert(j):
                return pe.value_load(tile_expert[0:1, bass.ds(j, 1)], min_val=0, max_val=E3 - 1)

            def step(v, m):
                j = v
                if inside(j):
                    round_wait(pe, x_in[m], v, m)
                    wait(pe, x_out, j - 1)
                    nc.tensor.transpose(psX[m % 2][:, 0:P], xs[m][:], k.ident[:]).then_inc(turned_x.sem, 1)
                j, b = v - 1, (m - 1) % 2
                if inside(j):
                    e = expert(j)
                    wait(pe, x_out, j + 1)
                    wait(pe, silu_done, j - 1)
                    nc.tensor.matmul(psH[b][:], xT[b][:], k.W1[:, bass.ds(e, 1), :].rearrange("p a f -> p (a f)"),
                                     start=True, stop=True).then_inc(up_done.sem, 1)
                j, b = v - 2, (m - 2) % 2
                if inside(j):
                    wait(pe, silu_done, j + 1)
                    wait(pe, h_out, j - 1)
                    for c in range(C):
                        i = nc.tensor.transpose(psT[b][:, c * P:(c + 1) * P], h[b][:, c * P:(c + 1) * P], k.ident[:])
                    i.then_inc(turned_h.sem, 1)
                j, b = v - 3, (m - 3) % 2
                if inside(j):
                    e = expert(j)
                    wait(pe, h_out, j + 1)
                    wait(pe, y_out, j - 1)
                    for c in range(C):
                        i = nc.tensor.matmul(psY[b][:, 0:D], hT[b][:, c * P:(c + 1) * P],
                                             k.W2[:, bass.ds(e, 1), c * D:(c + 1) * D].rearrange("p a f -> p (a f)"),
                                             start=(c == 0), stop=(c == C - 1))
                    i.then_inc(down_done.sem, 1)

            steps(pe, step, SLOT_TILES + 3)

        @block.scalar
        def _(act):
            def step(v, m):
                j, b = v - 1, (m - 1) % 2
                if inside(j):
                    wait(act, up_done, j + 1)
                    nc.scalar.activation(h[b][:], psH[b][:], ACT.Silu).then_inc(silu_done.sem, 1)
                j, b = v - 3, (m - 3) % 2
                if inside(j):
                    wait(act, down_done, j + 1)
                    q = (m - 3) % 4
                    round_wait(act, stored[q], j, q, off=1)
                    nc.scalar.activation(ys[q][:], psY[b][:, 0:D], ACT.Copy).then_inc(y_out.sem, 1)

            steps(act, step, SLOT_TILES + 3)

        @block.vector
        def _(dve):
            def step(v, m):
                j = v
                if inside(j):
                    wait(dve, turned_x, j + 1)
                    nc.vector.tensor_copy(xT[m % 2][:], psX[m % 2][:, 0:P]).then_inc(x_out.sem, 1)
                j, b = v - 2, (m - 2) % 2
                if inside(j):
                    wait(dve, turned_h, j + 1)
                    nc.vector.tensor_copy(hT[b][:], psT[b][:]).then_inc(h_out.sem, 1)

            steps(dve, step, SLOT_TILES + 2)
    scattered.close(16 * T)
    for t in x_in + stored:
        t.close(16 * SLOT_TILES // 4)
    for t in (turned_x, x_out, up_done, silu_done, turned_h, h_out, down_done, y_out):
        t.close(SLOT_TILES)
    loaded_w.close(128) if loaded_w.before == 0 else None
    zeroed.close(16) if zeroed.before == 0 else None


def gather_stage(k, name, G, Y, weight, slot, last):
    nc = k.nc
    gathered, weighed, turned, copied = (k.tally(f"ga_{n}") for n in ("gathered", "weighed", "turned", "copied"))
    gathered = [k.tally(f"ga_gathered{g}") for g in range(4)]
    with nc.psum_tensor(f"{name}_psY", [P, 4, 512], F32) as ps, nc.Block() as block:
        @block.gpsimd
        def _(pool):
            for t in range(T):
                pool.indirect_dma_start(G[:, t, :], None, k.sorted_y, bass.IndirectOffsetOnAxis(slot[:, t:t + 1], 0))\
                    .then_inc(gathered[t // 4].sem, 16)

        @block.vector
        def _(dve):
            for g in range(4):
                gathered[g].wait(dve, 64)
                for t in range(4 * g, 4 * g + 4):
                    if last:
                        m = nc.vector.scalar_tensor_tensor(out=k.X[:, t, :], in0=G[:, t, :], scalar=weight[:, t:t + 1],
                                                           in1=k.X[:, t, :], op0=ALU.mult, op1=ALU.add)
                    else:
                        m = nc.vector.tensor_scalar(Y[:, t, :], G[:, t, :], weight[:, t:t + 1], None, ALU.mult)
                m.then_inc(weighed.sem, 1)

        if not last:
            @block.tensor
            def _(pe):
                for g in range(4):
                    weighed.wait(pe, g + 1)
                    for j in range(4):
                        m = nc.tensor.transpose(ps[:, g, j * P:(j + 1) * P], Y[:, 4 * g + j, :], k.ident[:])
                    m.then_inc(turned.sem, 1)

            @block.scalar
            def _(act):
                for g in range(4):
                    turned.wait(act, g + 1)
                    nc.scalar.activation(k.XT[:, g * 512:(g + 1) * 512], ps[:, g, :], ACT.Copy).then_inc(copied.sem, 1)
    for t in gathered:
        t.close(64)
    weighed.close(4)
    if not last:
        turned.close(4)
        copied.close(4)


def moe_l3_stage(k, a):
    nc = k.nc
    with ExitStack() as s:
        sb = lambda n, shape, dt=F32: s.enter_context(nc.sbuf_tensor(f"m3_{n}", shape, dt))
        comb, G, Y, weight = sb("comb", [P, T, E3]), sb("G", [P, T, D]), sb("Y", [P, T, D]), sb("weight", [P, T])
        slot, tile_expert = sb("slot", [P, T], mybir.dt.uint32), sb("tile_expert", [1, SLOT_TILES], mybir.dt.int32)
        for layer in range(LAYERS):
            n = f"m3{layer}"
            route_stage(k, n, comb, a["L3_ffn_routers"][layer], None, E3, top=1, of_probs=True, renormed=False,
                        sort=(weight, slot, tile_expert))
            sorted_experts_stage(k, n, Y if layer else k.X, slot, tile_expert)
            gather_stage(k, n, G, Y, weight, slot, layer == LAYERS - 1)


def inverse_root(nc, dve, out, root, v, scratch):
    nc.vector.reciprocal(out, root)
    dve.drain()
    nc.vector.tensor_tensor(scratch, out, out, ALU.mult)
    dve.drain()
    nc.vector.tensor_tensor(scratch, scratch, v, ALU.mult)
    dve.drain()
    nc.vector.tensor_scalar(scratch, scratch, -0.5, 1.5, ALU.mult, ALU.add)
    dve.drain()
    nc.vector.tensor_tensor(out, out, scratch, ALU.mult)
    dve.drain()


CH = 32
DHEADS = D // CH
UN = N // CH
CPS = SEQ // CH
PE_TAPS = 25
LONG, SHORT, CONV = 64, 5, 4
EPS_L2 = 1e-6
FLOOR = 0.02



def delta_stage(k, a):
    nc = k.nc
    with ExitStack() as s:
        sb = lambda n, shape: s.enter_context(nc.sbuf_tensor(f"de_{n}", shape, F32))
        f = {n: sb(n, [P, N]) for n in (
            "qT", "kT", "short", "long", "qH", "kH", "vH", "sq", "kbH", "vbH", "attn", "delta")}
        pads = [sb(f"pad{i}", [P, BATCH, SEQ + CONV - 1]) for i in range(3)]
        vpad = sb("vpad", [P, BATCH, SEQ + LONG - 1])
        r1, r2, r3 = (t[:].rearrange("p b s -> p (b s)")[:, 0:N] for t in pads)
        w = {n: sb(n, [P, D]) for n in ("Wq", "Wk", "Wv", "Wxg", "Wg1x", "Wg1s", "Wg2", "Wo")}
        w["Wog1x"], w["Wog1s"], w["Wog2"] = sb("Wog1x", [P, D // 2]), sb("Wog1s", [P, D // 2]), sb("Wog2", [D // 2, D])
        taps = sb("taps", [P, 3 * CONV + SHORT + LONG])
        cols = sb("cols", [P, 6])
        rows = sb("rows", [P, 5])
        delta_filters(k, a, f, pads, vpad, w, taps, cols, rows)
        v = vpad[:, :, LONG - 1:]
        small = {n: sb(n, [P, UN]) for n in ("beta", "res", "ssk", "ssq", "rt", "rk", "rq", "t0")}
        delta_heads(k, f, v, w, cols, small, r1, r2, r3)
        delta_scan(k, f, r1, r2, r3)
        delta_gate(k, f, w, cols, rows, small, r1, r2, r3)
        project_and_add_stage(k, "de", None, r1, w["Wo"])


def delta_filters(k, a, f, pads, vpad, w, taps, cols, rows):
    nc = k.nc
    w_in, made, projected, padded, convd, silud, longed, diags = (
        k.tally(f"df_{n}") for n in ("w_in", "made", "projected", "padded", "convd", "silud", "longed", "diags"))
    T0 = 3 * CONV
    T1 = T0 + SHORT
    with nc.sbuf_tensor("df_diag", [P, PE_TAPS, P], F32) as diag, nc.psum_tensor("df_ps", [P, 2, 4, 512], F32) as ps, \
            nc.Block() as block:
        ahead = CONV - 1

        @block.sync
        def _(sp):
            for n in ("Wv", "Wq", "Wk"):
                sp.dma_start(w[n][:], a[f"L1_attn_{n}"]).then_inc(w_in.sem, 16)
            sp.dma_start(taps[:], a["L1_attn_taps"]).then_inc(w_in.sem, 16)
            rest = [(w[n], a[f"L1_attn_{n}"]) for n in
                    ("Wxg", "Wg1x", "Wg1s", "Wg2", "Wo", "Wog1x", "Wog1s", "Wog2", "cols")
                    if n != "cols"] + [(cols, a["L1_attn_cols"]), (rows, a["L1_attn_rows"].partition_broadcast(P))]
            for t, d in rest:
                sp.dma_start(t[:], d).then_inc(w_in.sem, 16)
            w_in.wait(sp, 16 * (4 + len(rest)))

        @block.gpsimd
        def _(pool):
            for t in pads:
                nc.gpsimd.memset(t[:, :, 0:ahead], 0.0)
            nc.gpsimd.memset(vpad[:, :, 0:LONG - 1], 0.0).then_inc(made.sem, 1)
            w_in.wait(pool, 16 * 14)
            for j in range(PE_TAPS):
                nc.gpsimd.tensor_scalar(diag[:, j, :], k.ident[:], taps[:, T1 + j:T1 + j + 1], None, ALU.mult)\
                    .then_inc(diags.sem, 1)

        @block.tensor
        def _(pe):
            w_in.wait(pe, 16 * 14)
            for i, n in enumerate(("Wv", "Wq", "Wk")):
                if i == 2:
                    padded.wait(pe, 1)
                for g in range(4):
                    m = nc.tensor.matmul(ps[:, i % 2, g, :], w[n][:], k.XT[:, g * 512:(g + 1) * 512],
                                         start=True, stop=True)
                m.then_inc(projected.sem, 1)
            padded.wait(pe, 2)
            silud.wait(pe, 1)
            diags.wait(pe, PE_TAPS)
            for g in range(4):
                for j in range(PE_TAPS):
                    m = nc.tensor.matmul(ps[:, 1, g, :], diag[:, j, :], vpad[:, 2 * g:2 * g + 2, j:j + SEQ],
                                         start=(j == 0), stop=(j == PE_TAPS - 1))
            m.then_inc(longed.sem, 1)

        @block.scalar
        def _(act):
            for i in range(3):
                projected.wait(act, i + 1)
                nc.scalar.activation(pads[(i + 2) % 3][:, :, ahead:], ps[:, i % 2, :, :].rearrange(
                    "p g (b s) -> p (g b) s", s=SEQ), ACT.Copy).then_inc(padded.sem, 1)
            outs = (vpad[:, :, LONG - 1:], f["qT"][:].rearrange("p (b s) -> p b s", b=BATCH),
                    f["kT"][:].rearrange("p (b s) -> p b s", b=BATCH))
            srcs = (f["sq"], f["qH"], f["kH"])
            made.wait(act, 1)
            for i in range(3):
                convd.wait(act, i + 1)
                nc.scalar.activation(outs[i], srcs[i][:].rearrange("p (b s) -> p b s", b=BATCH), ACT.Silu)\
                    .then_inc(silud.sem, 1)

        @block.vector
        def _(dve):
            def fir(out, src, first, n, start, only_add=False):
                o = out[:].rearrange("p (b s) -> p b s", b=BATCH)
                for j in range(n):
                    x, t = src[:, :, start + j:start + j + SEQ], taps[:, first + j:first + j + 1]
                    if j == 0:
                        m = nc.vector.tensor_scalar(o, x, t, None, ALU.mult)
                    else:
                        dve.drain()
                        m = nc.vector.scalar_tensor_tensor(out=o, in0=x, scalar=t, in1=o, op0=ALU.mult, op1=ALU.add)
                return m

            w_in.wait(dve, 16 * 14)
            made.wait(dve, 1)
            for i, (tile, pad) in enumerate(((f["sq"], pads[2]), (f["qH"], pads[0]), (f["kH"], pads[1]))):
                padded.wait(dve, i + 1)
                fir(tile, pad, CONV * ((i + 2) % 3), CONV, 0).then_inc(convd.sem, 1)
            silud.wait(dve, 1)
            fir(f["short"], vpad, T0, SHORT, LONG - SHORT)
            fir(f["long"], vpad, T1 + PE_TAPS, LONG - PE_TAPS, PE_TAPS)
            longed.wait(dve, 1)
            dve.drain()
            l = f["long"][:]
            nc.vector.tensor_tensor(l, l, ps[:, 1, :, :].rearrange("p g c -> p (g c)"), ALU.add)


def delta_heads(k, f, v, w, cols, small, r1, r2, r3):
    nc = k.nc
    gates, gout, turned, squared, summed, rooted, asked, sig = (
        k.tally(f"dh_{n}") for n in ("gates", "gout", "turned", "squared", "summed", "rooted", "asked", "sig"))
    H = lambda ap: ap.rearrange("p (u d) -> p u d", d=CH)
    bc = lambda t: t[:].unsqueeze(2).to_broadcast([P, UN, CH])
    with nc.psum_tensor("dh_ps", [P, 4, 512], F32) as ps, nc.Block() as block:
        @block.tensor
        def _(pe):
            for g in range(4):
                m = nc.tensor.matmul(ps[:, g, :], w["Wxg"][:], k.XT[:, g * 512:(g + 1) * 512], start=True, stop=True)
            m.then_inc(gates.sem, 1)

        @block.scalar
        def _(act):
            gates.wait(act, 1)
            nc.scalar.activation(r3, ps[:].rearrange("p g c -> p (g c)"), ACT.Copy).then_inc(gout.sem, 1)
            for i, n in enumerate(("qH", "kH")):
                turned.wait(act, i + 1)
                if i == 1:
                    summed.wait(act, 1)
                nc.scalar.activation(f["sq"][:], f[n][:], ACT.Square).then_inc(squared.sem, 1)
            for i, (t, o) in enumerate((("ssq", "rt"), ("ssk", "t0"))):
                asked.wait(act, 1)
                m = nc.scalar.activation(small[o][:], small[t][:], ACT.Sqrt)
            m.then_inc(rooted.sem, 1)
            turned.wait(act, 3)
            g = r2.rearrange("p (u s) -> p u s", s=CH)
            nc.scalar.activation(small["beta"][:], g[:, :, 0], ACT.Sigmoid)
            nc.scalar.activation(small["res"][:], g[:, :, 1], ACT.Sigmoid, bias=cols[:, 0:1]).then_inc(sig.sem, 1)

        @block.vector
        def _(dve):
            nc.vector.transpose(f["qH"][:], f["qT"][:]).then_inc(turned.sem, 1)
            nc.vector.transpose(f["kH"][:], f["kT"][:]).then_inc(turned.sem, 1)
            for b in range(BATCH):
                nc.vector.transpose(f["vH"][:, b * SEQ:(b + 1) * SEQ], v[:, b, :])
            gout.wait(dve, 1)
            nc.vector.transpose(r2, r3).then_inc(turned.sem, 1)
            for i, n in enumerate(("ssq", "ssk")):
                squared.wait(dve, i + 1)
                m = nc.vector.tensor_reduce(small[n][:], H(f["sq"][:]), AX.X, ALU.add)
                m.then_inc(summed.sem, 1)
                dve.drain()
                m = nc.vector.tensor_scalar(small[n][:], small[n][:], EPS_L2, None, ALU.add)
            m.then_inc(asked.sem, 1)
            rooted.wait(dve, 1)
            for ss, rt, r in (("ssq", "rt", "rq"), ("ssk", "t0", "rk")):
                inverse_root(nc, dve, small[r][:], small[rt][:], small[ss][:], small[rt][:])
            nc.vector.tensor_tensor(H(f["qH"][:]), H(f["qH"][:]), bc(small["rq"]), ALU.mult)
            nc.vector.tensor_tensor(H(f["kH"][:]), H(f["kH"][:]), bc(small["rk"]), ALU.mult)
            sig.wait(dve, 1)
            nc.vector.tensor_tensor(H(f["vbH"][:]), H(f["vH"][:]), bc(small["beta"]), ALU.mult)
            dve.drain()
            nc.vector.tensor_tensor(H(f["kbH"][:]), H(f["kH"][:]), bc(small["beta"]), ALU.mult)
            nc.vector.transpose(f["qT"][:], f["qH"][:])
            nc.vector.transpose(f["kT"][:], f["kH"][:])
            dve.drain()
            nc.vector.transpose(r1, f["kbH"][:])
    gates.close(1); gout.close(1); turned.close(3); squared.close(2); summed.close(2)
    rooted.close(1); asked.close(1); sig.close(1)


def delta_scan(k, f, r1, r2, r3):
    nc = k.nc
    blocked, multiplied, masked, opened, cleared = (
        k.tally(f"ds_{n}") for n in ("blocked", "multiplied", "masked", "opened", "cleared"))
    with ExitStack() as s:
        sb = lambda n, shape: s.enter_context(nc.sbuf_tensor(f"ds_{n}", shape, F32))
        bd = {n: sb(f"bd_{n}", [P, BATCH, D]) for n in ("kbT", "kT", "qT", "kH", "U", "attn")}
        strict, incl = sb("strict", [P, CH]), sb("incl", [P, CH])
        tmp = sb("tmp", [P, 2, CH * CH // 4 + CH])
        state, r, u2 = (sb(n, [P, BATCH, CH]) for n in ("state", "r", "u2"))
        at = lambda t, n: t.rearrange("p (b n i) -> p b n i", b=BATCH, n=CPS)[:, :, bass.ds(n, 1), :]\
            .rearrange("p b a i -> p b (a i)")
        src = {"kbT": r1, "kT": f["kT"][:], "qT": f["qT"][:], "kH": f["kH"][:], "U": r2, "attn": f["attn"][:]}

        def expand(copy, name, n):
            for h in range(DHEADS):
                p = slice(CH * h, CH * (h + 1))
                m = copy(bd[name][p, :, CH * h:CH * (h + 1)], at(src[name], n)[p])
            return m

        with nc.psum_tensor("ds_psA", [P, N], F32) as psA, nc.psum_tensor("ds_psB", [P, N], F32) as psB, \
                nc.Block() as block:
            @block.gpsimd
            def _(pool):
                for n in ("U", "attn", "kH"):
                    m = nc.gpsimd.memset(bd[n][:], 0.0)
                m.then_inc(cleared.sem, 1)
                cleared.wait(pool, 1)
                for h in range(DHEADS):
                    p = slice(CH * h, CH * (h + 1))
                    nc.gpsimd.affine_select(out=strict[p, :], in_=k.ones[p, 0:CH], compare_op=ALU.is_ge, fill=0.0,
                                            base=-1, pattern=[[-1, CH]], channel_multiplier=1)
                    m = nc.gpsimd.affine_select(out=incl[p, :], in_=k.ones[p, 0:CH], compare_op=ALU.is_ge, fill=0.0,
                                                base=0, pattern=[[1, CH]], channel_multiplier=-1)
                m.then_inc(masked.sem, 1)

            @block.vector
            def _(dve):
                nc.vector.memset(bd["kbT"][:], 0.0)
                dve.drain()
                with dve.Fori(0, CPS) as n:
                    dve.wait_ge(multiplied.sem, n + (multiplied.before + 1))
                    expand(nc.vector.tensor_copy, "kbT", n).then_inc(blocked.sem, 1)
                masked.wait(dve, 1)
                multiplied.wait(dve, CPS + 1)
                g = lambda t: t.rearrange("p (u j) -> p u j", j=CH)
                m3 = lambda t: t[:].unsqueeze(1).to_broadcast([P, UN, CH])
                nc.vector.tensor_tensor(g(r3), g(psA[:]), m3(strict), ALU.mult)
                nc.vector.tensor_tensor(g(f["attn"][:]), g(psB[:]), m3(incl), ALU.mult)
                dve.drain()
                nc.vector.transpose(r2.rearrange("p (g j i) -> p g j i", g=2, j=CH),
                                    r3.rearrange("p (g u j) -> p g j u", g=2, j=CH))
                Tm = f["sq"][:].rearrange("p (g i c) -> p g i c", g=2, i=CH)
                L = r2.rearrange("p (g j i) -> p g j i", g=2, j=CH)
                nc.vector.memset(f["sq"][:], 0.0)
                dve.drain()
                nc.vector.memset(f["sq"][:].rearrange("p (g x) -> p g x", g=2)[:, :, 0:CH * CH:CH + 1], 1.0)
                dve.drain()
                for j in range(CH - 1):
                    ni, nk = CH - 1 - j, j + 1
                    t = tmp[:, :, 0:ni * nk].rearrange("p g (i c) -> p g i c", c=nk)
                    nc.vector.tensor_tensor(t, L[:, :, j, j + 1:].unsqueeze(3).to_broadcast([P, 2, ni, nk]),
                                            Tm[:, :, j:j + 1, 0:nk].to_broadcast([P, 2, ni, nk]), ALU.mult)
                    dve.drain()
                    rows = Tm[:, :, j + 1:, 0:nk]
                    nc.vector.tensor_tensor(rows, rows, t, ALU.subtract)
                    dve.drain()
                nc.vector.transpose(r2.rearrange("p (g u i) -> p g i u", g=2, i=CH),
                                    f["sq"][:].rearrange("p (g i c) -> p g i c", g=2, i=CH))

            @block.scalar
            def _(act):
                nc.scalar.memzero(bd["kT"][:])
                act.drain()
                with act.Fori(0, CPS) as n:
                    act.wait_ge(multiplied.sem, n + (multiplied.before + 1))
                    expand(nc.scalar.copy, "kT", n).then_inc(opened.sem, 1)
                nc.scalar.memzero(bd["qT"][:])

            @block.tensor
            def _(pe):
                pe.sem_inc(multiplied.sem, 1)
                with pe.Fori(0, CPS) as n:
                    pe.wait_ge(blocked.sem, n + (blocked.before + 1))
                    pe.wait_ge(opened.sem, n + (opened.before + 1))
                    for b in range(BATCH):
                        c = bass.ds(n * CH + b * SEQ, CH)
                        nc.tensor.matmul(psA[:, c], bd["kbT"][:, b, :], f["kT"][:, c], start=True, stop=True)
                        m = nc.tensor.matmul(psB[:, c], bd["kT"][:, b, :], f["qT"][:, c], start=True, stop=True)
                    m.then_inc(multiplied.sem, 1)

        opened_k, read, carried, less, solved, solved_out, out_done, out_copied, added = (
            k.tally(f"dt_{n}") for n in
            ("opened", "read", "carried", "less", "solved", "solved_out", "out_done", "out_copied", "added"))
        opened_d, opened_p = k.tally("dt_opened_d"), k.tally("dt_opened_p")
        with ExitStack() as pc:
            ps1, ps2, ps3, ps4 = (pc.enter_context(nc.psum_tensor(f"dt_ps{i}", [P, 512], F32)) for i in range(1, 5))
            block = pc.enter_context(nc.Block())
            b3 = lambda t: t[:, 0:BATCH * CH].rearrange("p (b c) -> p b c", c=CH)

            @block.gpsimd
            def _(pool):
                with pool.Fori(0, CPS) as n:
                    pool.wait_ge(added.sem, n + (added.before + 1))
                    expand(nc.gpsimd.tensor_copy, "kH", n)
                    expand(nc.gpsimd.tensor_copy, "attn", n).then_inc(opened_p.sem, 1)

            @block.scalar
            def _(act):
                with act.Fori(0, CPS) as n:
                    act.wait_ge(added.sem, n + (added.before + 1))
                    expand(nc.scalar.copy, "kbT", n).then_inc(opened_k.sem, 1)
                    expand(nc.scalar.copy, "qT", n).then_inc(opened_k.sem, 1)
                    act.wait_ge(solved.sem, n + (solved.before + 1))
                    nc.scalar.copy(u2[:], b3(ps2)).then_inc(solved_out.sem, 1)
                    act.wait_ge(out_done.sem, n + (out_done.before + 1))
                    nc.scalar.copy(at(f["delta"][:], n), b3(ps3)).then_inc(out_copied.sem, 1)

            @block.tensor
            def _(pe):
                with pe.Fori(0, CPS) as n:
                    pe.wait_ge(added.sem, n + (added.before + 1))
                    pe.wait_ge(opened_k.sem, 2 * n + (opened_k.before + 1))
                    for b in range(BATCH):
                        m = nc.tensor.matmul(ps1[:, b * CH:(b + 1) * CH], bd["kbT"][:, b, :], state[:, b, :],
                                             start=True, stop=True)
                    m.then_inc(carried.sem, 1)
                    pe.wait_ge(opened_k.sem, 2 * n + (opened_k.before + 2))
                    pe.wait_ge(out_copied.sem, n + (out_copied.before + 1))
                    for b in range(BATCH):
                        nc.tensor.matmul(ps3[:, b * CH:(b + 1) * CH], bd["qT"][:, b, :], state[:, b, :],
                                         start=(b == 0), stop=False, skip_group_check=True)
                    pe.wait_ge(opened_d.sem, n + (opened_d.before + 1))
                    pe.wait_ge(less.sem, n + (less.before + 1))
                    for b in range(BATCH):
                        m = nc.tensor.matmul(ps2[:, b * CH:(b + 1) * CH], bd["U"][:, b, :], r[:, b, :],
                                             start=True, stop=True)
                    m.then_inc(solved.sem, 1)
                    pe.wait_ge(opened_p.sem, n + (opened_p.before + 1))
                    pe.wait_ge(solved_out.sem, n + (solved_out.before + 1))
                    for b in range(BATCH):
                        m = nc.tensor.matmul(ps4[:, b * CH:(b + 1) * CH], bd["kH"][:, b, :], u2[:, b, :],
                                             start=True, stop=True)
                    m.then_inc(read.sem, 1)
                    for b in range(BATCH):
                        m = nc.tensor.matmul(ps3[:, b * CH:(b + 1) * CH], bd["attn"][:, b, :], u2[:, b, :],
                                             start=False, stop=(b == BATCH - 1), skip_group_check=True)
                    m.then_inc(out_done.sem, 1)

            @block.vector
            def _(dve):
                nc.vector.memset(state[:], 0.0).then_inc(added.sem, 1)
                dve.sem_inc(out_copied.sem, 1)
                with dve.Fori(0, CPS) as n:
                    expand(nc.vector.tensor_copy, "U", n).then_inc(opened_d.sem, 1)
                    dve.wait_ge(carried.sem, n + (carried.before + 1))
                    nc.vector.tensor_tensor(r[:], at(f["vbH"][:], n), b3(ps1), ALU.subtract).then_inc(less.sem, 1)
                    dve.wait_ge(read.sem, n + (read.before + 1))
                    dve.wait_ge(out_done.sem, n + (out_done.before + 1))
                    nc.vector.tensor_tensor(state[:], state[:], b3(ps4), ALU.add).then_inc(added.sem, 1)


def delta_gate(k, f, w, cols, rows, small, r1, r2, r3):
    nc = k.nc
    H = lambda ap: ap.rearrange("p (u d) -> p u d", d=CH)
    with ExitStack() as s:
        sb = lambda n, shape: s.enter_context(nc.sbuf_tensor(f"dg_{n}", shape, F32))
        Z = sb("Z", [P, UN, CH])
        ss = sb("ss", [P, 4, UN])
        l2 = sb("l2", [P, 4, UN])
        su, t1 = sb("su", [P, UN]), sb("t1", [P, UN])
        lg, pr = sb("lg", [P, UN, 4]), sb("pr", [P, UN, 4])
        one = sb("one", [P, 4])
        og, fac = sb("og", [P, UN]), sb("fac", [P, UN])
        sqd, sumd, ask, rt, zt, hid, gel, lgt, lgc, ex, asko, cons = (
            k.tally(f"dg_{n}") for n in ("sqd", "sumd", "ask", "rt", "zt", "hid", "gel", "lgt", "lgc", "ex", "asko", "cons"))
        hpart = {"short": r2, "long": r3, "delta": f["delta"][:], "v": f["vH"][:]}
        ZT = f["qT"][:]
        G = f["kT"]
        o = f["qH"][:]
        tmp = f["kbH"][:]

        def stats(dve, x, n, col, squares):
            nc.vector.tensor_reduce(su[:], H(x), AX.X, ALU.add)
            nc.vector.tensor_reduce(t1[:], H(x), AX.X, ALU.add, apply_absolute_value=True)
            sqd.wait(dve, squares)
            nc.vector.tensor_reduce(ss[:, n, :], H(f["sq"][:]), AX.X, ALU.add).then_inc(sumd.sem, 1)
            dve.drain()
            nc.vector.tensor_scalar(Z[:, :, col], su[:], 1.0 / D, None, ALU.mult)
            nc.vector.tensor_scalar(Z[:, :, col + 2], t1[:], 1.0 / D, None, ALU.mult)
            nc.vector.tensor_tensor(su[:], su[:], su[:], ALU.mult)
            dve.drain()
            nc.vector.tensor_scalar(su[:], su[:], -1.0 / (D * CH), None, ALU.mult)
            dve.drain()
            m = nc.vector.scalar_tensor_tensor(out=Z[:, :, col + 1], in0=ss[:, n, :], scalar=1.0 / D, in1=su[:],
                                               op0=ALU.mult, op1=ALU.add)
            dve.drain()
            return m

        with nc.psum_tensor("dg_ps", [P, 4, 512], F32) as ps, nc.psum_tensor("dg_ps2", [P, 4, 512], F32) as ps2, \
                nc.Block() as block:
            @block.vector
            def _(dve):
                nc.vector.memset(Z[:], 0.0)
                nc.vector.transpose(r2, f["short"][:])
                nc.vector.transpose(r3, f["long"][:])
                dve.drain()
                for i, (n, j) in enumerate((("v", 3), ("delta", 2), ("short", 0), ("long", 1))):
                    m = stats(dve, hpart[n], j, 4 * j, i + 1)
                m.then_inc(ask.sem, 1)
                rt.wait(dve, 1)
                for j in range(4):
                    m = nc.vector.tensor_scalar(Z[:, :, 4 * j + 3], l2[:, j, :], 1.0 / DHEADS, None, ALU.mult)
                dve.drain()
                nc.vector.transpose(ZT, Z[:].rearrange("p u s -> p (u s)")).then_inc(zt.sem, 1)
                lgc.wait(dve, 1)
                nc.vector.transpose(o, tmp)
                dve.drain()
                cons.wait(dve, 1)
                nc.vector.tensor_scalar(one[:, 2:3], rows[:, 4:5], 0.0, None, ALU.max)
                dve.drain()
                nc.vector.tensor_tensor(one[:, 2:3], one[:, 2:3], one[:, 1:2], ALU.add)
                dve.drain()
                nc.vector.reciprocal(one[:, 3:4], one[:, 2:3])
                nc.vector.tensor_tensor(lg[:], H(o)[:, :, 0:4], rows[:, 0:4].unsqueeze(1).to_broadcast([P, UN, 4]),
                                        ALU.add)
                dve.drain()
                nc.vector.tensor_scalar(lg[:], lg[:], one[:, 3:4], None, ALU.mult)
                dve.drain()
                nc.vector.tensor_reduce(su[:], lg[:], AX.X, ALU.max)
                dve.drain()
                b4 = lambda t: t[:].unsqueeze(2).to_broadcast([P, UN, 4])
                nc.vector.tensor_tensor(lg[:], lg[:], b4(su), ALU.subtract).then_inc(ask.sem, 1)
                rt.wait(dve, 2)
                for i in range(2):
                    nc.vector.tensor_reduce(su[:], pr[:], AX.X, ALU.add)
                    dve.drain()
                    nc.vector.reciprocal(t1[:], su[:])
                    dve.drain()
                    nc.vector.tensor_tensor(pr[:], pr[:], b4(t1), ALU.mult)
                    dve.drain()
                    if i == 0:
                        nc.vector.tensor_scalar(pr[:], pr[:], FLOOR, None, ALU.max)
                        dve.drain()
                nc.vector.scalar_tensor_tensor(out=pr[:, :, 0], in0=small["res"][:], scalar=one[:, 0:1],
                                               in1=pr[:, :, 0], op0=ALU.mult, op1=ALU.add)
                dve.drain()
                b32 = lambda t: t.unsqueeze(2).to_broadcast([P, UN, CH])
                for j, n in enumerate(("short", "long", "delta", "v")):
                    dst = o if j == 0 else tmp
                    nc.vector.tensor_tensor(H(dst), H(hpart[n]), b32(pr[:, :, j]), ALU.mult)
                    dve.drain()
                    if j:
                        m = nc.vector.tensor_tensor(o, o, tmp, ALU.add)
                        dve.drain()
                m.then_inc(ask.sem, 1)
                stats(dve, o, 0, 0, 5).then_inc(ask.sem, 1)
                rt.wait(dve, 3)
                nc.vector.tensor_scalar(Z[:, :, 3], l2[:, 0, :], 1.0 / DHEADS, None, ALU.mult)
                dve.drain()
                nc.vector.transpose(ZT, Z[:].rearrange("p u s -> p (u s)")).then_inc(zt.sem, 1)
                lgc.wait(dve, 2)
                nc.vector.transpose(r2, tmp).then_inc(asko.sem, 1)
                rt.wait(dve, 4)
                nc.vector.tensor_tensor(t1[:], og[:], og[:], ALU.mult)
                dve.drain()
                nc.vector.tensor_tensor(t1[:], t1[:], ss[:, 0, :], ALU.mult)
                dve.drain()
                nc.vector.tensor_scalar(t1[:], t1[:], 1.0 / CH, LN_EPS, ALU.mult, ALU.add).then_inc(asko.sem, 1)
                rt.wait(dve, 5)
                inverse_root(nc, dve, fac[:], su[:], t1[:], l2[:, 1, :])
                nc.vector.tensor_tensor(fac[:], fac[:], og[:], ALU.mult)
                dve.drain()
                nc.vector.tensor_tensor(H(o), H(o), b32(fac[:]), ALU.mult)
                dve.drain()
                nc.vector.transpose(r1, o)
                nc.vector.tensor_scalar(w["Wo"][:], w["Wo"][:], cols[:, 2:3], None, ALU.mult)

            @block.scalar
            def _(act):
                nc.scalar.activation(one[:, 0:1], cols[:, 1:2], ACT.Sigmoid)
                nc.scalar.activation(one[:, 1:2], rows[:, 4:5], ACT.Abs)
                act.drain()
                nc.scalar.activation(one[:, 1:2], one[:, 1:2], ACT.Exp, scale=-1.0)
                act.drain()
                nc.scalar.activation(one[:, 1:2], one[:, 1:2], ACT.Ln, bias=k.ones[:, 0:1]).then_inc(cons.sem, 1)
                for i, n in enumerate(("v", "delta", "short", "long")):
                    if i:
                        sumd.wait(act, i)
                    nc.scalar.activation(f["sq"][:], hpart[n], ACT.Square).then_inc(sqd.sem, 1)
                ask.wait(act, 1)
                nc.scalar.activation(l2[:], ss[:], ACT.Sqrt).then_inc(rt.sem, 1)
                for g in range(4):
                    hid.wait(act, g + 1)
                    nc.scalar.activation(G[:, g * 512:(g + 1) * 512], ps[:, g, :], ACT.Gelu, bias=cols[:, 3:4])\
                        .then_inc(gel.sem, 1)
                for g in range(4):
                    lgt.wait(act, g + 1)
                    m = nc.scalar.activation(tmp[:, g * 512:(g + 1) * 512], ps2[:, g, :], ACT.Copy)
                m.then_inc(lgc.sem, 1)
                ask.wait(act, 2)
                nc.scalar.activation(pr[:], lg[:], ACT.Exp).then_inc(rt.sem, 1)
                ask.wait(act, 3)
                nc.scalar.activation(f["sq"][:], o, ACT.Square).then_inc(sqd.sem, 1)
                ask.wait(act, 4)
                nc.scalar.activation(l2[:, 0, :], ss[:, 0, :], ACT.Sqrt).then_inc(rt.sem, 1)
                for g in range(4):
                    hid.wait(act, 4 + g + 1)
                    nc.scalar.activation(G[0:D // 2, g * 512:(g + 1) * 512], ps[0:D // 2, g, :], ACT.Gelu,
                                         bias=cols[0:D // 2, 4:5]).then_inc(gel.sem, 1)
                for g in range(4):
                    lgt.wait(act, 4 + g + 1)
                    m = nc.scalar.activation(tmp[:, g * 512:(g + 1) * 512], ps2[:, g, :], ACT.Copy)
                m.then_inc(lgc.sem, 1)
                asko.wait(act, 1)
                nc.scalar.activation(og[:], H(r2)[:, :, 0], ACT.Sigmoid, bias=cols[:, 5:6]).then_inc(rt.sem, 1)
                asko.wait(act, 2)
                nc.scalar.activation(su[:], t1[:], ACT.Sqrt).then_inc(rt.sem, 1)

            @block.tensor
            def _(pe):
                for i, (wx, ws, w2, M) in enumerate((("Wg1x", "Wg1s", "Wg2", P), ("Wog1x", "Wog1s", "Wog2", D // 2))):
                    if i == 1:
                        lgc.wait(pe, 1)
                    zt.wait(pe, i + 1)
                    for g in range(4):
                        c = slice(g * 512, (g + 1) * 512)
                        nc.tensor.matmul(ps[0:M, g, :], w[wx][:], k.XT[:, c], start=True, stop=False)
                        nc.tensor.matmul(ps[0:M, g, :], w[ws][:], ZT[:, c], start=False, stop=True)\
                            .then_inc(hid.sem, 1)
                    for g in range(4):
                        gel.wait(pe, 4 * i + g + 1)
                        nc.tensor.matmul(ps2[:, g, :], w[w2][:], G[0:M, g * 512:(g + 1) * 512], start=True, stop=True)\
                            .then_inc(lgt.sem, 1)


def retention_stage(k, a):
    nc = k.nc
    w_in, consts, made, projected, scanned, turned, gated, asked, rooted, scaled, tail = (
        k.tally(f"re_{n}") for n in
        ("w_in", "consts", "made", "projected", "scanned", "turned", "gated", "asked", "rooted", "scaled", "tail"))
    with ExitStack() as s:
        sb = lambda n, shape: s.enter_context(nc.sbuf_tensor(f"re_{n}", shape, F32))
        w = {n: sb(n, [P, D]) for n in ("wq", "wv", "wg", "wo")}
        col = sb("col", [P, 3])
        lam = sb("lam", [P, 1])
        decay = sb("decay", [P, BATCH, SEQ])
        state, yT, gate, y2T = (sb(n, [P, N]) for n in ("state", "yT", "gate", "y2T"))
        Y = sb("Y", [P, T, D])
        stats, agg = sb("stats", [P, T, 6]), sb("agg", [P, T, 2])
        vare, root, rstd, scratch = (sb(n, [P, T]) for n in ("vare", "root", "rstd", "scratch"))
        with nc.psum_tensor("re_psQ", [P, N], F32) as psQ, nc.psum_tensor("re_psV", [P, N], F32) as psV, \
                nc.Block() as block:
            @block.sync
            def _(sp):
                sp.dma_start(col[:], a["L2_attn_cols"]).then_inc(consts.sem, 16)
                for n in ("wv", "wq", "wg", "wo"):
                    sp.dma_start(w[n][:], a[f"L2_attn_{n}"]).then_inc(w_in.sem, 16)
                w_in.wait(sp, 64)

            @block.tensor
            def _(pe):
                w_in.wait(pe, 64)
                for n, ps in (("wv", psV), ("wq", psQ)):
                    for g in range(4):
                        m = nc.tensor.matmul(ps[:, g * 512:(g + 1) * 512], w[n][:], k.XT[:, g * 512:(g + 1) * 512],
                                             start=True, stop=True)
                    m.then_inc(projected.sem, 1)

            @block.scalar
            def _(act):
                consts.wait(act, 16)
                nc.scalar.activation(lam[:], col[:, 0:1], ACT.Sigmoid).then_inc(made.sem, 1)

            @block.vector
            def _(dve):
                nc.vector.memset(decay[:], 1.0)
                made.wait(dve, 1)
                dve.drain()
                nc.vector.tensor_scalar(decay[:], decay[:], lam[:, 0:1], None, ALU.mult)
                dve.drain()
                nc.vector.memset(decay[:, :, 0:1], 0.0)
                dve.drain()
                projected.wait(dve, 1)
                nc.vector.tensor_tensor_scan(state[:], decay[:].rearrange("p b s -> p (b s)"), psV[:], 0.0,
                                             ALU.mult, ALU.add)
                dve.drain()
                projected.wait(dve, 2)
                nc.vector.tensor_tensor(yT[:], psQ[:], state[:], ALU.mult)

        with nc.psum_tensor("re_psY", [P, T, D], F32) as psY, nc.psum_tensor("re_psG", [P, 4, 512], F32) as psG, \
                nc.Block() as block:
            @block.tensor
            def _(pe):
                for t in range(T):
                    m = nc.tensor.transpose(psY[:, t, :], yT[:, t * P:(t + 1) * P], k.ident[:])
                    if t % 4 == 3:
                        m.then_inc(turned.sem, 1)
                for g in range(4):
                    nc.tensor.matmul(psG[:, g, :], w["wg"][:], k.XT[:, g * 512:(g + 1) * 512], start=True, stop=True)\
                        .then_inc(gated.sem, 1)

            @block.scalar
            def _(act):
                asked.wait(act, 1)
                nc.scalar.activation(root[:], vare[:], ACT.Sqrt).then_inc(rooted.sem, 1)
                for g in range(4):
                    gated.wait(act, g + 1)
                    nc.scalar.activation(gate[:, g * 512:(g + 1) * 512], psG[:, g, :], ACT.Silu)

            @block.vector
            def _(dve):
                for t in range(T):
                    if t % 4 == 0:
                        turned.wait(dve, t // 4 + 1)
                    nc.vector.bn_stats(stats[:, t, :], psY[:, t, :])
                dve.drain()
                for t in range(T):
                    nc.vector.bn_aggr(agg[:, t, :], stats[:, t, :])
                dve.drain()
                nc.vector.tensor_scalar(vare[:], agg[:, :, 1], LN_EPS, None, ALU.add).then_inc(asked.sem, 1)
                rooted.wait(dve, 1)
                inverse_root(nc, dve, rstd[:], root[:], vare[:], scratch[:])
                for t in range(T):
                    nc.vector.tensor_scalar(Y[:, t, :], psY[:, t, :], agg[:, t, 0:1], rstd[:, t:t + 1],
                                            ALU.subtract, ALU.mult)

        with nc.psum_tensor("re_psN", [P, 4, 512], F32) as psN, nc.Block() as block:
            @block.tensor
            def _(pe):
                for g in range(4):
                    for j in range(4):
                        m = nc.tensor.transpose(psN[:, g, j * P:(j + 1) * P], Y[:, 4 * g + j, :], k.ident[:])
                    m.then_inc(tail.sem, 1)

            @block.scalar
            def _(act):
                for g in range(4):
                    tail.wait(act, g + 1)
                    nc.scalar.activation(y2T[:, g * 512:(g + 1) * 512], psN[:, g, :], ACT.Identity,
                                         scale=col[:, 1:2], bias=col[:, 2:3]).then_inc(scaled.sem, 1)

            @block.vector
            def _(dve):
                for g in range(4):
                    scaled.wait(dve, g + 1)
                    c = slice(g * 512, (g + 1) * 512)
                    nc.vector.tensor_tensor(y2T[:, c], y2T[:, c], gate[:, c], ALU.mult)
        project_and_add_stage(k, "re", None, y2T, w["wo"])


def lru_stage(k, a):
    nc = k.nc
    w_in, iotad, exped, prepared, sined, halved, projected, scaled, rotated, out_done = (
        k.tally(f"lr_{n}") for n in
        ("w_in", "iotad", "exped", "prepared", "sined", "halved", "projected", "scaled", "rotated", "out_done"))
    TURN_HI, TURN_LO = 6.28125, float(2 * np.pi - 6.28125)
    with ExitStack() as s:
        sb = lambda n, shape: s.enter_context(nc.sbuf_tensor(f"lr_{n}", shape, F32))
        w = {n: sb(n, [P, D]) for n in ("Br", "Bi", "Cr", "Ci")}
        col = sb("col", [P, 3])
        nu, th, mag, mag2, gamma, g1 = (sb(n, [P, 1]) for n in ("nu", "th", "mag", "mag2", "gamma", "g1"))
        time, angle, turns, sin, half, cos = (sb(n, [P, SEQ]) for n in ("time", "angle", "turns", "sin", "half", "cos"))
        diag = sb("diag", [P, D])
        decay, br, bi, m1, m2, hr, hi = (sb(n, [P, BATCH, SEQ]) for n in ("decay", "br", "bi", "m1", "m2", "hr", "hi"))
        gr, gi = sb("gr", [P, BATCH, SEQ]), sb("gi", [P, BATCH, SEQ])
        all_seqs = lambda t: t[:].unsqueeze(1).to_broadcast([P, BATCH, SEQ])
        flat = lambda t: t[:].rearrange("p b s -> p (b s)")
        with nc.psum_tensor("lr_psR", [P, N], F32) as psR, nc.psum_tensor("lr_psI", [P, N], F32) as psI, \
                nc.Block() as block:
            @block.sync
            def _(sp):
                sp.dma_start(col[:], a["L3_attn_cols"]).then_inc(w_in.sem, 16)
                for n in w:
                    sp.dma_start(w[n][:], a[f"L3_attn_{n}"]).then_inc(w_in.sem, 16)

            @block.gpsimd
            def _(pool):
                nc.gpsimd.iota(time[:], [[1, SEQ]], base=0, channel_multiplier=0,
                               allow_small_or_imprecise_dtypes=True).then_inc(iotad.sem, 1)

            @block.tensor
            def _(pe):
                w_in.wait(pe, 80)
                for n, ps in (("Br", psR), ("Bi", psI)):
                    for g in range(4):
                        m = nc.tensor.matmul(ps[:, g * 512:(g + 1) * 512], w[n][:], k.XT[:, g * 512:(g + 1) * 512],
                                             start=True, stop=True)
                    m.then_inc(projected.sem, 1)

            @block.scalar
            def _(act):
                w_in.wait(act, 80)
                nc.scalar.activation(nu[:], col[:, 0:1], ACT.Exp)
                nc.scalar.activation(th[:], col[:, 1:2], ACT.Exp)
                act.drain()
                nc.scalar.activation(mag[:], nu[:], ACT.Exp, scale=-1.0)
                nc.scalar.activation(mag2[:], nu[:], ACT.Exp, scale=-2.0).then_inc(exped.sem, 1)
                prepared.wait(act, 1)
                nc.scalar.activation(gamma[:], g1[:], ACT.Sqrt)
                act.drain()
                projected.wait(act, 1)
                nc.scalar.activation(flat(br), psR[:], ACT.Copy, scale=gamma[:, 0:1])
                projected.wait(act, 2)
                nc.scalar.activation(flat(bi), psI[:], ACT.Copy, scale=gamma[:, 0:1]).then_inc(scaled.sem, 1)
                prepared.wait(act, 2)
                nc.scalar.activation(sin[:], angle[:], ACT.Sin)
                nc.scalar.activation(half[:], angle[:], ACT.Sin, scale=0.5).then_inc(sined.sem, 1)

            @block.vector
            def _(dve):
                exped.wait(dve, 1)
                nc.vector.tensor_scalar(g1[:], mag2[:], -1.0, 1.0, ALU.mult, ALU.add)
                dve.drain()
                nc.vector.tensor_scalar(g1[:], g1[:], LN_EPS, None, ALU.add).then_inc(prepared.sem, 1)
                iotad.wait(dve, 1)
                nc.vector.tensor_scalar(angle[:], time[:], th[:, 0:1], None, ALU.mult)
                dve.drain()
                nc.vector.tensor_scalar(turns[:], angle[:], float(1 / (2 * np.pi)), ROUND, ALU.mult, ALU.add)
                dve.drain()
                nc.vector.tensor_scalar(turns[:], turns[:], -ROUND, None, ALU.add)
                dve.drain()
                nc.vector.scalar_tensor_tensor(out=angle[:], in0=turns[:], scalar=-TURN_HI, in1=angle[:],
                                               op0=ALU.mult, op1=ALU.add)
                dve.drain()
                nc.vector.scalar_tensor_tensor(out=angle[:], in0=turns[:], scalar=-TURN_LO, in1=angle[:],
                                               op0=ALU.mult, op1=ALU.add)
                dve.drain()
                nc.vector.tensor_scalar(angle[:], angle[:], 3.1415925, -3.1415925, ALU.min, ALU.max)\
                    .then_inc(prepared.sem, 1)
                nc.vector.memset(decay[:], 1.0)
                dve.drain()
                nc.vector.tensor_scalar(decay[:], decay[:], mag[:, 0:1], None, ALU.mult)
                dve.drain()
                nc.vector.memset(decay[:, :, 0:1], 0.0)
                w_in.wait(dve, 80)
                nc.vector.tensor_scalar(diag[:], k.ident[:], col[:, 2:3], None, ALU.mult)
                nc.vector.tensor_scalar(w["Ci"][:], w["Ci"][:], -1.0, None, ALU.mult)
                sined.wait(dve, 1)
                nc.vector.tensor_tensor(cos[:], half[:], half[:], ALU.mult)
                dve.drain()
                nc.vector.tensor_scalar(cos[:], cos[:], -2.0, 1.0, ALU.mult, ALU.add)
                dve.drain()
                scaled.wait(dve, 1)
                C, S = all_seqs(cos), all_seqs(sin)
                nc.vector.tensor_tensor(gr[:], br[:], C, ALU.mult)
                nc.vector.tensor_tensor(m1[:], bi[:], S, ALU.mult)
                nc.vector.tensor_tensor(gi[:], bi[:], C, ALU.mult)
                nc.vector.tensor_tensor(m2[:], br[:], S, ALU.mult)
                dve.drain()
                nc.vector.tensor_tensor(gr[:], gr[:], m1[:], ALU.add)
                nc.vector.tensor_tensor(gi[:], gi[:], m2[:], ALU.subtract)
                dve.drain()
                nc.vector.tensor_tensor_scan(flat(br), flat(decay), flat(gr), 0.0, ALU.mult, ALU.add)
                nc.vector.tensor_tensor_scan(flat(bi), flat(decay), flat(gi), 0.0, ALU.mult, ALU.add)
                dve.drain()
                nc.vector.tensor_tensor(hr[:], br[:], C, ALU.mult)
                nc.vector.tensor_tensor(m1[:], bi[:], S, ALU.mult)
                nc.vector.tensor_tensor(hi[:], br[:], S, ALU.mult)
                nc.vector.tensor_tensor(m2[:], bi[:], C, ALU.mult)
                dve.drain()
                nc.vector.tensor_tensor(hr[:], hr[:], m1[:], ALU.subtract)
                nc.vector.tensor_tensor(hi[:], hi[:], m2[:], ALU.add)

        with nc.psum_tensor("lr_psO", [P, 4, 512], F32) as psO, nc.Block() as block:
            @block.tensor
            def _(pe):
                for g in range(4):
                    for j in range(4):
                        t = 4 * g + j
                        o, c = psO[:, g, j * P:(j + 1) * P], slice(t * P, (t + 1) * P)
                        nc.tensor.matmul(o, flat(hr)[:, c], w["Cr"][:], start=True, stop=False)
                        nc.tensor.matmul(o, flat(hi)[:, c], w["Ci"][:], start=False, stop=False)
                        m = nc.tensor.matmul(o, k.XT[:, c], diag[:], start=False, stop=True)
                    m.then_inc(out_done.sem, 1)

            @block.vector
            def _(dve):
                for g in range(4):
                    out_done.wait(dve, g + 1)
                    x = k.X[:, 4 * g:4 * g + 4, :]
                    nc.vector.tensor_tensor(x, x, psO[:, g, :].rearrange("p (t d) -> p t d", d=D), ALU.add)


def store_stage(k, out):
    nc = k.nc
    stored = k.tally("stored")
    with nc.Block() as block:
        @block.sync
        def _(sp):
            sp.dma_start(out.rearrange("b (t p) d -> p (b t) d", p=P), k.X[:]).then_inc(stored.sem, 16)
            stored.wait(sp, 16)


def program(nc, a, out, upto=8, start=0):
    with ExitStack() as ctx:
        k = Core(nc, ctx)
        setup_stage(k, a["L0_attn_x"])
        stages = [
            lambda: attention_stage(k, a["L0_attn_W_Q"], a["L0_attn_W_K"], a["L0_attn_W_V"], a["L0_attn_W_O"]),
            lambda: moe_l0_stage(k, a),
            lambda: delta_stage(k, a),
            lambda: moe_l1_stage(k, a),
            lambda: retention_stage(k, a),
            lambda: moe_l2_stage(k, a),
            lambda: lru_stage(k, a),
            lambda: moe_l3_stage(k, a),
        ]
        for n in range(start, upto):
            if n == max(start, 6) and upto == 8:
                load_l3_weights(k, a)
            stages[n]()
            layernorm_stage(k, f"ln{n}", turn=n < 7)
        store_stage(k, out)


def lay_out(v):
    r = {}
    r["L0_attn_x"] = v["L0_attn_x"]
    for n in "QKVO":
        r[f"L0_attn_W_{n}"] = v[f"L0_attn_W_{n}"].T
    cat = lambda *x: np.concatenate(x, axis=2)
    E, F = v["L0_ffn_b1"].shape
    cols = lambda b: b.reshape(E, F // P, P).transpose(0, 2, 1)
    down = lambda w: w.reshape(w.shape[0], -1, P, D).transpose(0, 2, 1, 3).reshape(w.shape[0], P, -1)
    r["L0_ffn_router"] = v["L0_ffn_Wg"].T
    r["L0_ffn_up"] = cat(v["L0_ffn_W1"].transpose(0, 2, 1), v["L0_ffn_W2"].transpose(0, 2, 1),
                         cols(v["L0_ffn_b1"]), cols(v["L0_ffn_b2"]))
    r["L0_ffn_down"] = down(v["L0_ffn_W3"].transpose(0, 2, 1))
    r["L0_ffn_b3"] = v["L0_ffn_b3"]
    for n in "qkvo":
        r[f"L1_attn_W{n}"] = v[f"L1_attn_W{n}"]
    r["L1_attn_taps"] = np.concatenate(
        [v["L1_attn_wq_conv"], v["L1_attn_wk_conv"], v["L1_attn_wv_conv"], v["L1_attn_fir_short"].reshape(D, -1),
         v["L1_attn_fir_long"].reshape(D, -1)], axis=1)

    def spread(rows, columns):
        out = np.zeros((rows, DHEADS, CH), np.float32)
        for s, c in columns.items():
            out[:, :, s] = c if c.ndim == 2 else c[:, None]
        return out.reshape(rows, D)

    wg1, wg2, wog1, wog2 = (v[f"L1_attn_{n}"] for n in ("Wg1", "Wg2", "Wog1", "Wog2"))
    r["L1_attn_Wxg"] = spread(D, {0: v["L1_attn_Wb"], 1: v["L1_attn_Wres"]})
    r["L1_attn_Wg1x"], r["L1_attn_Wog1x"] = wg1[:D], wog1[:D]
    r["L1_attn_Wg1s"] = spread(D, {i: wg1[D + i] for i in range(16)}).T
    r["L1_attn_Wog1s"] = spread(D // 2, {(i if i < 4 else 8 + i): wog1[D + i] for i in range(8)}).T
    r["L1_attn_Wg2"] = spread(D, {i: wg2[:, i] for i in range(4)})
    r["L1_attn_Wog2"] = spread(D // 2, {0: wog2[:, 0]})
    r["L1_attn_cols"] = np.stack(
        [np.repeat(v["L1_attn_bres"], CH), np.repeat(v["L1_attn_conv_res_logit"], CH),
         np.tile(v["L1_attn_norm_w"], DHEADS), v["L1_attn_bg1"],
         np.concatenate([v["L1_attn_bog1"], np.zeros(D // 2, np.float32)]), np.repeat(v["L1_attn_bog2"], D)], axis=1)
    r["L1_attn_rows"] = np.concatenate([v["L1_attn_bg2"], v["L1_attn_logit_temp"]])
    r["L1_ffn_router"] = v["L1_ffn_router_w"].T
    r["L1_ffn_router_bias"] = v["L1_ffn_router_bias"]
    halves = lambda w: w.T.reshape(D, 2, -1).transpose(1, 0, 2)
    r["L1_ffn_up"] = np.concatenate([cat(v["L1_ffn_gate_proj"], v["L1_ffn_up_proj"]),
                                     cat(halves(v["L1_ffn_sh_gate"]), halves(v["L1_ffn_sh_up"]))])
    r["L1_ffn_down"] = np.concatenate([v["L1_ffn_down_proj"], v["L1_ffn_sh_down"].T.reshape(2, -1, D)])
    r["L2_ffn_router"] = v["L2_ffn_router_w"].T
    r["L2_ffn_up"] = np.concatenate([cat(v["L2_ffn_w_gate"], v["L2_ffn_w_up"]), v["L2_ffn_ws_gate_up"][None]])
    r["L2_ffn_down"] = np.concatenate([v["L2_ffn_w_down"], v["L2_ffn_ws_down"][None]])
    c = lambda *x: np.stack(x, axis=1)
    r["L2_attn_cols"] = c(np.repeat(v["L2_attn_beta"], HD), v["L2_attn_ln_gamma"], v["L2_attn_ln_beta"])
    for n in "qvgo":
        r[f"L2_attn_w{n}"] = v[f"L2_attn_W{n}"].T
    r["L3_attn_cols"] = c(v["L3_attn_nu_log"], v["L3_attn_theta_log"], v["L3_attn_D_skip"])
    for n, m in (("Br", "B_re"), ("Bi", "B_im"), ("Cr", "C_re"), ("Ci", "C_im")):
        r[f"L3_attn_{n}"] = v[f"L3_attn_{m}"].T
    r["L3_ffn_routers"] = v["L3_ffn_routers"]
    r["L3_ffn_up"] = v["L3_ffn_W1"]
    r["L3_ffn_down"] = down(v["L3_ffn_W2"])
    return r


def kernel(**inputs):
    import concourse.bacc as bacc
    from concourse.bass_utils import run_bass_kernel_spmd

    laid = {n: np.ascontiguousarray(x) for n, x in lay_out({n: np.asarray(x) for n, x in inputs.items()}).items()}
    nc = bacc.Bacc("TRN2", target_bir_lowering=False, num_devices=1)
    aps = {n: nc.dram_tensor(f"in_{n}", x.shape, mybir.dt.from_np(x.dtype), kind="ExternalInput").ap()
           for n, x in laid.items()}
    out = nc.dram_tensor("out", (BATCH, SEQ, D), F32, kind="ExternalOutput").ap()
    program(nc, aps, out)
    r = run_bass_kernel_spmd(nc, [{f"in_{n}": x for n, x in laid.items()}], core_ids=[0])
    return r.results[0]["out"]
```

```python
from contextlib import ExitStack

import numpy as np
import concourse.bass as bass
from concourse import mybir

F32, F16, BF16 = mybir.dt.float32, mybir.dt.float16, mybir.dt.bfloat16
ALU = mybir.AluOpType
ACT = mybir.ActivationFunctionType
AX = mybir.AxisListType

P = 128
D = 128
BATCH = 8
SEQ = 256
N = BATCH * SEQ
T = N // P
NBLK = N // 512
LN_EPS = 1e-5
MASKED = -1e30


class Tally:

    def __init__(self, sem):
        self.sem, self.before = sem, 0

    def at(self, n):
        return self.sem, n + self.before

    def close(self, total):
        self.before += total


class Core:

    def __init__(self, nc, ctx):
        self.nc, self.ctx, self.tallies = nc, ctx, {}
        self.X = self.keep("X", [P, T, D])
        self.XT = self.keep("XT", [P, N])
        self.ident = self.keep("ident", [P, P])
        self.ones = self.keep("ones", [P, P])

    def keep(self, name, shape, dt=F32):
        return self.ctx.enter_context(self.nc.sbuf_tensor(name, shape, dt))

    def tally(self, name):
        if name not in self.tallies:
            self.tallies[name] = Tally(self.ctx.enter_context(self.nc.semaphore(name)))
        return self.tallies[name]


def setup_stage(k, x_in):
    nc = k.nc
    loaded, made, turned, copied = (k.tally(n) for n in ("loaded", "made", "ln_turned", "ln_copied"))
    with nc.psum_tensor("ps_setup", [P, 4, 512], F32) as ps, nc.Block() as block:
        @block.sync
        def _(sp):
            sp.dma_start(k.X[:], x_in.rearrange("b (t p) d -> p (b t) d", p=P)).then_inc(loaded.sem, 16)

        @block.gpsimd
        def _(pool):
            nc.gpsimd.memset(k.ident[:], 0.0).then_inc(made.sem, 1)
            pool.wait_ge(*made.at(1))
            nc.gpsimd.affine_select(out=k.ident[:], in_=k.ident[:], compare_op=ALU.not_equal, fill=1.0,
                                    base=0, pattern=[[-1, P]], channel_multiplier=1).then_inc(made.sem, 1)
            nc.gpsimd.memset(k.ones[:], 1.0).then_inc(made.sem, 1)
            pool.wait_ge(*made.at(3))

        @block.tensor
        def _(pe):
            pe.wait_ge(*loaded.at(16))
            pe.wait_ge(*made.at(2))
            for g in range(4):
                for j in range(4):
                    t = nc.tensor.transpose(ps[:, g, j * P:(j + 1) * P], k.X[:, 4 * g + j, :], k.ident[:])
                t.then_inc(turned.sem, 1)

        @block.scalar
        def _(act):
            for g in range(4):
                act.wait_ge(*turned.at(g + 1))
                nc.scalar.activation(k.XT[:, g * 512:(g + 1) * 512], ps[:, g, :], ACT.Copy).then_inc(copied.sem, 1)
    loaded.close(16)
    made.close(3)
    turned.close(4)
    copied.close(4)


def layernorm_stage(k, name, turn=True):
    nc = k.nc
    asked, rooted, scaled, turned, copied = (
        k.tally(n) for n in ("ln_asked", "ln_rooted", "ln_scaled", "ln_turned", "ln_copied"))
    with ExitStack() as s:
        stats = s.enter_context(nc.sbuf_tensor(f"{name}_stats", [P, T, 6], F32))
        agg = s.enter_context(nc.sbuf_tensor(f"{name}_agg", [P, T, 2], F32))
        vare = s.enter_context(nc.sbuf_tensor(f"{name}_vare", [P, T], F32))
        root = s.enter_context(nc.sbuf_tensor(f"{name}_root", [P, T], F32))
        rstd = s.enter_context(nc.sbuf_tensor(f"{name}_rstd", [P, T], F32))
        t0 = s.enter_context(nc.sbuf_tensor(f"{name}_t0", [P, T], F32))
        ps = s.enter_context(nc.psum_tensor(f"{name}_ps", [P, 4, 512], F32))
        block = s.enter_context(nc.Block())

        @block.vector
        def _(dve):
            for t in range(T):
                nc.vector.bn_stats(stats[:, t, :], k.X[:, t, :])
            dve.drain()
            for t in range(T):
                nc.vector.bn_aggr(agg[:, t, :], stats[:, t, :])
            dve.drain()
            nc.vector.tensor_scalar(vare[:], agg[:, :, 1], LN_EPS, None, ALU.add).then_inc(asked.sem, 1)
            dve.wait_ge(*rooted.at(1))
            inverse_root(nc, dve, rstd[:], root[:], vare[:], t0[:])
            for t in range(T):
                ins = nc.vector.tensor_scalar(k.X[:, t, :], k.X[:, t, :], agg[:, t, 0:1], rstd[:, t:t + 1],
                                              ALU.subtract, ALU.mult)
                if t % 4 == 3:
                    ins.then_inc(scaled.sem, 1)

        @block.scalar
        def _(act):
            act.wait_ge(*asked.at(1))
            nc.scalar.activation(root[:], vare[:], ACT.Sqrt).then_inc(rooted.sem, 1)
            if turn:
                for g in range(4):
                    act.wait_ge(*turned.at(g + 1))
                    nc.scalar.activation(k.XT[:, g * 512:(g + 1) * 512], ps[:, g, :], ACT.Copy)\
                        .then_inc(copied.sem, 1)

        if turn:
            @block.tensor
            def _(pe):
                for g in range(4):
                    pe.wait_ge(*scaled.at(g + 1))
                    for j in range(4):
                        t = nc.tensor.transpose(ps[:, g, j * P:(j + 1) * P], k.X[:, 4 * g + j, :], k.ident[:])
                    t.then_inc(turned.sem, 1)
    asked.close(1)
    rooted.close(1)
    scaled.close(4)
    if turn:
        turned.close(4)
        copied.close(4)


HEADS = 16
HD = D // HEADS


def attention_stage(k, w_q, w_k, w_v, w_o):
    nc = k.nc
    KC = SEQ // P
    SC = P + SEQ
    slopes = (np.float32(1.0) / np.power(np.float32(256.0), (np.arange(HEADS, dtype=np.float32) + 1) / HEADS)).astype(np.float32)
    with ExitStack() as s:
        sb = lambda n, shape: s.enter_context(nc.sbuf_tensor(f"at_{n}", shape, F32))
        wq, wk, wv, wo = (sb(n, [P, D]) for n in ("wq", "wk", "wv", "wo"))
        QT, KT = sb("QT", [P, N]), sb("KT", [P, N])
        V = sb("V", [P, T, D])
        rel = sb("rel", [P, SEQ])
        bias = sb("bias", [P, HEADS, SEQ])
        hmask = sb("hmask", [P, HEADS])
        qm = sb("qm", [P, HEADS, SEQ])
        S = sb("S", [P, 2, SC])
        nmax = sb("nmax", [P, HEADS, KC])
        rsum = sb("rsum", [P, HEADS, KC])
        rinv = sb("rinv", [P, HEADS, KC])
        Pr = sb("Pr", [P, 2, SC])
        PT = sb("PT", [P, 2, SC])
        O = sb("O", [P, T, D])
        OT = sb("OT", [P, N])
        sem = lambda n: k.tally(f"at_{n}")
        w_in, biased, masked, projected, proj_out, v_out = map(sem, ("w_in", "biased", "masked", "projected", "proj_out", "v_out"))
        psA_cm = nc.psum_tensor("at_psA", [P, 8, 512], F32)
        with psA_cm as psA, nc.Block() as block:
            @block.sync
            def _(sp):
                for t, w in ((wq, w_q), (wk, w_k), (wv, w_v), (wo, w_o)):
                    sp.dma_start(t[:], w).then_inc(w_in.sem, 16)

            @block.gpsimd
            def _(pool):
                nc.gpsimd.iota(rel[:], [[1, SEQ]], base=-P, channel_multiplier=-1,
                               allow_small_or_imprecise_dtypes=True).then_inc(biased.sem, 1)
                nc.gpsimd.memset(hmask[:], 1.0).then_inc(masked.sem, 1)
                pool.wait_ge(*masked.at(1))
                nc.gpsimd.affine_select(out=hmask[:], in_=hmask[:], compare_op=ALU.is_ge, fill=0.0, base=0,
                                        pattern=[[-HD, HEADS]], channel_multiplier=1).then_inc(masked.sem, 1)
                pool.wait_ge(*masked.at(2))
                nc.gpsimd.affine_select(out=hmask[:], in_=hmask[:], compare_op=ALU.is_ge, fill=0.0, base=HD - 1,
                                        pattern=[[HD, HEADS]], channel_multiplier=-1).then_inc(masked.sem, 1)
                pool.wait_ge(*biased.at(2))
                nc.gpsimd.affine_select(out=bias[:], in_=bias[:], compare_op=ALU.is_ge, fill=MASKED, base=P,
                                        pattern=[[0, HEADS], [-1, SEQ]], channel_multiplier=1)\
                    .then_inc(biased.sem, 1)

            @block.tensor
            def _(pe):
                pe.wait_ge(*w_in.at(64))
                for g in range(4):
                    nc.tensor.matmul(psA[:, g, :], wq[:], k.XT[:, g * 512:(g + 1) * 512], start=True, stop=True)\
                        .then_inc(projected.sem, 1)
                    nc.tensor.matmul(psA[:, 4 + g, :], wk[:], k.XT[:, g * 512:(g + 1) * 512], start=True, stop=True)\
                        .then_inc(projected.sem, 1)
                for g in range(4):
                    pe.wait_ge(*proj_out.at(g + 1))
                    for j in range(4):
                        t = 4 * g + j
                        m = nc.tensor.matmul(psA[:, g, j * P:(j + 1) * P], k.XT[:, t * P:(t + 1) * P], wv[:],
                                             start=True, stop=True)
                    m.then_inc(projected.sem, 1)

            @block.scalar
            def _(act):
                for g in range(4):
                    act.wait_ge(*projected.at(2 * g + 1))
                    nc.scalar.activation(QT[:, g * 512:(g + 1) * 512], psA[:, g, :], ACT.Copy,
                                         scale=float(1.0 / np.sqrt(np.float32(HD)))).then_inc(proj_out.sem, 1)
                for g in range(4):
                    act.wait_ge(*projected.at(8 + g + 1))
                    nc.scalar.activation(V[:, 4 * g:4 * g + 4, :], psA[:, g, :].rearrange("p (t d) -> p t d", d=D),
                                         ACT.Copy).then_inc(v_out.sem, 1)

            @block.vector
            def _(dve):
                dve.wait_ge(*biased.at(1))
                for h in range(HEADS):
                    m = nc.vector.tensor_scalar(bias[:, h, :], rel[:], float(slopes[h]), None, ALU.mult)
                m.then_inc(biased.sem, 1)
                for g in range(4):
                    dve.wait_ge(*projected.at(2 * g + 2))
                    nc.vector.tensor_copy(KT[:, g * 512:(g + 1) * 512], psA[:, 4 + g, :])

        scored, biasd, expd, turned, tcopied, weighted, normed, qmasked, begun, groups_begun = map(
            sem, ("scored", "biasd", "expd", "turned", "tcopied", "weighted", "normed", "qmasked", "begun",
                  "groups_begun"))
        QG = 4
        NG = HEADS // QG
        with ExitStack() as ps_ctx:
            psS = [ps_ctx.enter_context(nc.psum_tensor(f"at_psS{i}", [P, 512], F32)) for i in range(2)]
            psT = [ps_ctx.enter_context(nc.psum_tensor(f"at_psT{i}", [P, 512], F32)) for i in range(2)]
            psO = ps_ctx.enter_context(nc.psum_tensor("at_psO", [P, 512], F32))
            block = ps_ctx.enter_context(nc.Block())

            @block.gpsimd
            def _(pool):
                with pool.Fori(0, BATCH) as b:
                    for g in range(NG):
                        pool.wait_ge(scored.sem, HEADS * b + (g + 1) * QG)
                        pool.sem_inc(groups_begun.sem, 1)
                        nc.gpsimd.tensor_tensor(
                            qm[:, g * QG:(g + 1) * QG, :],
                            QT[:, bass.ds(b * SEQ, SEQ)].unsqueeze(1).to_broadcast([P, QG, SEQ]),
                            hmask[:, g * QG:(g + 1) * QG].unsqueeze(2).to_broadcast([P, QG, SEQ]),
                            ALU.mult).then_inc(qmasked.sem, 1)

            @block.tensor
            def _(pe):
                pe.sem_inc(scored.sem, HEADS)
                with pe.Fori(0, BATCH) as b:
                    def scores(h):
                        if h % QG == 0:
                            pe.wait_ge(qmasked.sem, NG * b + (h // QG + 1))
                        if h >= 2:
                            pe.wait_ge(biasd.sem, HEADS * b + (h - 1))
                        nc.tensor.matmul(psS[h % 2][:, 0:P], qm[:, h, 0:P], KT[:, bass.ds(b * SEQ, P)],
                                         start=True, stop=True)
                        nc.tensor.matmul(psS[h % 2][:, P:SC], qm[:, h, P:SEQ], KT[:, bass.ds(b * SEQ, SEQ)],
                                         start=True, stop=True).then_inc(scored.sem, 1)

                    def turn(h):
                        pe.wait_ge(expd.sem, HEADS * b + (h + 1))
                        if h >= 2:
                            pe.wait_ge(tcopied.sem, HEADS * b + (h - 1))
                        for j in range(3):
                            m = nc.tensor.transpose(psT[h % 2][:, j * P:(j + 1) * P], Pr[:, h % 2, j * P:(j + 1) * P],
                                                    k.ident[:])
                        m.then_inc(turned.sem, 1)

                    def weigh(h):
                        pe.wait_ge(tcopied.sem, HEADS * b + (h + 1))
                        if h == 0:
                            pe.wait_ge(normed.sem, b + 1)
                        o0 = psO[:, h * HD:(h + 1) * HD]
                        o1 = psO[:, D + h * HD:D + (h + 1) * HD]
                        v0 = V[:, bass.ds(b * KC, 1), h * HD:(h + 1) * HD].rearrange("p a d -> p (a d)")
                        v1 = V[:, bass.ds(b * KC + 1, 1), h * HD:(h + 1) * HD].rearrange("p a d -> p (a d)")
                        nc.tensor.matmul(o0, PT[:, h % 2, 0:P], v0, start=True, stop=True)
                        nc.tensor.matmul(o1, PT[:, h % 2, P:2 * P], v0, start=True, stop=False)
                        nc.tensor.matmul(o1, PT[:, h % 2, 2 * P:SC], v1, start=False, stop=True)\
                            .then_inc(weighted.sem, 1)

                    for h in range(HEADS + 2):
                        if h < HEADS:
                            scores(h)
                        if 1 <= h <= HEADS:
                            turn(h - 1)
                        if h >= 2:
                            weigh(h - 2)

            @block.vector
            def _(dve):
                dve.sem_inc(normed.sem, 1)
                with dve.Fori(0, BATCH) as b:
                    def add_bias(h):
                        dve.wait_ge(scored.sem, HEADS * b + (HEADS + h + 1))
                        if h >= 2:
                            dve.wait_ge(expd.sem, HEADS * b + (h - 1))
                        dve.sem_inc(begun.sem, 1)
                        nc.vector.tensor_tensor_reduce(S[:, h % 2, 0:P], psS[h % 2][:, 0:P], bias[:, h, P:SEQ], -1.0,
                                                       -MASKED, ALU.add, ALU.min, nmax[:, h, 0:1])
                        nc.vector.tensor_tensor_reduce(S[:, h % 2, P:SC], psS[h % 2][:, P:SC], bias[:, h, :], -1.0,
                                                       -MASKED, ALU.add, ALU.min, nmax[:, h, 1:2])\
                            .then_inc(biasd.sem, 1)

                    def copy_turned(h):
                        dve.wait_ge(turned.sem, HEADS * b + (h + 1))
                        if h >= 2:
                            dve.wait_ge(weighted.sem, HEADS * b + (h - 1))
                        nc.vector.tensor_copy(PT[:, h % 2, :], psT[h % 2][:, 0:SC]).then_inc(tcopied.sem, 1)

                    for h in range(HEADS + 1):
                        if h < HEADS:
                            add_bias(h)
                        if h >= 1:
                            copy_turned(h - 1)
                    nc.vector.reciprocal(rinv[:], rsum[:])
                    dve.drain()
                    dve.wait_ge(weighted.sem, HEADS * b + HEADS)
                    for qt in range(KC):
                        m = nc.vector.tensor_tensor(
                            O[:, bass.ds(b * KC + qt, 1), :].rearrange("p a (h e) -> p (a h) e", e=HD),
                            psO[:, qt * D:(qt + 1) * D].rearrange("p (h e) -> p h e", e=HD),
                            rinv[:, :, qt:qt + 1].to_broadcast([P, HEADS, HD]), ALU.mult)
                    m.then_inc(normed.sem, 1)

            @block.scalar
            def _(act):
                with act.Fori(0, BATCH) as b:
                    for h in range(HEADS):
                        act.wait_ge(biasd.sem, HEADS * b + (h + 1))
                        if h >= 2:
                            act.wait_ge(turned.sem, HEADS * b + (h - 1))
                        if h == 0:
                            act.wait_ge(normed.sem, b + 1)
                        nc.scalar.activation(Pr[:, h % 2, 0:P], S[:, h % 2, 0:P], ACT.Exp, scale=-1.0,
                                             bias=nmax[:, h, 0:1], accum_out=rsum[:, h, 0:1])
                        nc.scalar.activation(Pr[:, h % 2, P:SC], S[:, h % 2, P:SC], ACT.Exp, scale=-1.0,
                                             bias=nmax[:, h, 1:2], accum_out=rsum[:, h, 1:2]).then_inc(expd.sem, 1)

        project_and_add_stage(k, "at", O, OT, wo)
        w_in.close(64)
        biased.close(3)
        masked.close(3)
        projected.close(12)
        proj_out.close(4)
        v_out.close(4)


def project_and_add_stage(k, name, O, OT, w):
    nc = k.nc
    turned, copied, projected = (k.tally(f"pr_{n}") for n in ("turned", "copied", "projected"))
    with nc.psum_tensor(f"{name}_pr_psT", [P, 4, 512], F32) as psT, \
            nc.psum_tensor(f"{name}_pr_psR", [P, 4, 512], F32) as psR, nc.Block() as block:
        @block.tensor
        def _(pe):
            if O is not None:
                for g in range(4):
                    for j in range(4):
                        m = nc.tensor.transpose(psT[:, g, j * P:(j + 1) * P], O[:, 4 * g + j, :], k.ident[:])
                    m.then_inc(turned.sem, 1)
            for g in range(4):
                if O is not None:
                    pe.wait_ge(*copied.at(g + 1))
                for j in range(4):
                    t = 4 * g + j
                    m = nc.tensor.matmul(psR[:, g, j * P:(j + 1) * P], OT[:, t * P:(t + 1) * P], w[:],
                                         start=True, stop=True)
                m.then_inc(projected.sem, 1)

        if O is not None:
            @block.scalar
            def _(act):
                for g in range(4):
                    act.wait_ge(*turned.at(g + 1))
                    nc.scalar.activation(OT[:, g * 512:(g + 1) * 512], psT[:, g, :], ACT.Copy).then_inc(copied.sem, 1)

        @block.vector
        def _(dve):
            for g in range(4):
                dve.wait_ge(*projected.at(g + 1))
                x = k.X[:, 4 * g:4 * g + 4, :]
                nc.vector.tensor_tensor(x, x, psR[:, g, :].rearrange("p (t d) -> p t d", d=D), ALU.add)
    projected.close(4)
    if O is not None:
        turned.close(4)
        copied.close(4)


PAD = -3e38
TAKEN = -1e38
ROUND = float(1.5 * 2 ** 23)


def route_stage(k, name, comb, w_r, r_bias, experts, top, of_probs, renormed, always=0, chosen=None,
                sort=None):
    nc = k.nc
    E = experts
    w_in, made, logits, asked, exped, counted, counts = (
        k.tally(n) for n in ("w_in", "made", "logits", "asked", "exped", "counted", "counts"))
    with ExitStack() as s:
        sb = lambda n, shape: s.enter_context(nc.sbuf_tensor(f"{name}_rt_{n}", shape, F32))
        wr = sb("wr", [P, E])
        rb = sb("rb", [P, E])
        L = sb("L", [P, T, E + 8])
        R = sb("R", [P, T, E + 8])
        m8, rep8 = sb("m8", [P, T, 8]), sb("rep8", [P, T, 8])
        ex, sel = sb("ex", [P, T, E]), chosen or sb("sel", [P, T, E])
        total, inv = sb("total", [P, T]), sb("inv", [P, T])
        psL = s.enter_context(nc.psum_tensor(f"{name}_psL", [P, T, E], F32))
        if sort:
            weight, slot, tile_expert = sort
            tiles = tile_expert.shape[1]
            count, first, last = (sb(n, [P, E]) for n in ("count", "first", "last"))
            place = sb("place", [P, T])
            tile_no = sb("tile_no", [1, tiles])
            past = sb("past", [1, tiles, E])
            psN = s.enter_context(nc.psum_tensor(f"{name}_psN", [P, E], F32))
            before, tri = sb("before", [P, T, E]), sb("tri", [P, P])
            psC = s.enter_context(nc.psum_tensor(f"{name}_psC", [P, T, E], F32))
        block = s.enter_context(nc.Block())
        bc = lambda ap, n: ap.unsqueeze(2).to_broadcast([P, T, n])

        @block.sync
        def _(sp):
            sp.dma_start(wr[:], w_r).then_inc(w_in.sem, 16)
            if r_bias is not None:
                sp.dma_start(rb[:], r_bias.partition_broadcast(P)).then_inc(w_in.sem, 16)

        @block.gpsimd
        def _(pool):
            if sort:
                nc.gpsimd.iota(tile_no[:], [[1, tiles]], base=0, channel_multiplier=0,
                               allow_small_or_imprecise_dtypes=True)
            if sort:
                nc.gpsimd.affine_select(out=tri[:], in_=k.ones[:], compare_op=ALU.is_ge, fill=0.0, base=-1,
                                        pattern=[[1, P]], channel_multiplier=-1).then_inc(made.sem, 1)

        @block.tensor
        def _(pe):
            pe.wait_ge(*w_in.at(32 if r_bias is not None else 16))
            for t in range(T):
                m = nc.tensor.matmul(psL[:, t, :], k.XT[:, t * P:(t + 1) * P], wr[:], start=True, stop=True)
            m.then_inc(logits.sem, 1)
            if sort:
                pe.wait_ge(*made.at(1))
                pe.wait_ge(*counted.at(1))
                half = min(T, 512 // E)
                for j in range(T // half):
                    o = psC[:, j * half:(j + 1) * half, :].rearrange("p t e -> p (t e)")
                    nc.tensor.matmul(o, tri[:], sel[:, j * half:(j + 1) * half, :].rearrange("p t e -> p (t e)"),
                                     start=True, stop=False)
                    m = nc.tensor.matmul(o, k.ones[:],
                                         before[:, j * half:(j + 1) * half, :].rearrange("p t e -> p (t e)"),
                                         start=False, stop=True)
                nc.tensor.matmul(psN[:], k.ones[:], before[:, T - 1, :], start=True, stop=False)
                m = nc.tensor.matmul(psN[:], k.ones[:], sel[:, T - 1, :], start=False, stop=True)
                m.then_inc(counts.sem, 1)

        @block.scalar
        def _(act):
            act.wait_ge(*asked.at(1))
            nc.scalar.activation(ex[:], ex[:], ACT.Exp).then_inc(exped.sem, 1)

        @block.vector
        def _(dve):
            nc.vector.memset(L[:, :, E:E + 8], PAD)
            if always:
                nc.vector.memset(comb[:, :, E:E + always], 1.0)
            dve.wait_ge(*logits.at(1))
            if r_bias is not None:
                nc.vector.tensor_tensor(L[:, :, 0:E], psL[:], rb[:].unsqueeze(1).to_broadcast([P, T, E]), ALU.add)
            else:
                nc.vector.tensor_copy(L[:, :, 0:E], psL[:])
            dve.drain()
            for t in range(T):
                nc.vector.max(m8[:, t, :], L[:, t, 0:E])
            dve.drain()
            nc.vector.tensor_tensor(ex[:], L[:, :, 0:E], m8[:, :, 0:1].to_broadcast([P, T, E]), ALU.subtract)\
                .then_inc(asked.sem, 1)
            dve.wait_ge(*exped.at(1))
            if of_probs:
                nc.vector.tensor_reduce(total[:], ex[:], AX.X, ALU.add)
                dve.drain()
                nc.vector.reciprocal(inv[:], total[:])
                dve.drain()
                nc.vector.tensor_tensor(ex[:], ex[:], bc(inv[:], E), ALU.mult)
                dve.drain()
                nc.vector.tensor_copy(L[:, :, 0:E], ex[:])
                dve.drain()
                for t in range(T):
                    nc.vector.max(m8[:, t, :], L[:, t, 0:E])
                dve.drain()
            nc.vector.tensor_copy(rep8[:], m8[:])
            if top < 8:
                dve.drain()
                nc.vector.memset(rep8[:, :, top:8], PAD)
            dve.drain()
            for t in range(T):
                nc.vector.match_replace(R[:, t, :], rep8[:, t, :], L[:, t, :], TAKEN)
            dve.drain()
            nc.vector.tensor_tensor(sel[:], R[:, :, 0:E], L[:, :, 0:E], ALU.not_equal)
            dve.drain()
            c = comb[:, :, 0:E]
            nc.vector.tensor_tensor(c, ex[:], sel[:], ALU.mult)
            dve.drain()
            if renormed:
                nc.vector.tensor_reduce(total[:], c, AX.X, ALU.add)
                dve.drain()
                nc.vector.reciprocal(inv[:], total[:])
                dve.drain()
                nc.vector.tensor_tensor(c, c, bc(inv[:], E), ALU.mult)
                dve.drain()
            if sort:
                nc.vector.memset(before[:, 0, :], 0.0)
                for t in range(1, T):
                    dve.drain()
                    m = nc.vector.tensor_tensor(before[:, t, :], before[:, t - 1, :], sel[:, t - 1, :], ALU.add)
                m.then_inc(counted.sem, 1)
                dve.wait_ge(*counts.at(1))
                dve.wait_ge(*made.at(1))
                nc.vector.tensor_copy(weight[:], m8[:, :, 0])
                nc.vector.tensor_scalar(count[:], psN[:], 1.0 / P, 63.5 / P, ALU.mult, ALU.add)
                dve.drain()
                nc.vector.tensor_scalar(count[:], count[:], ROUND, None, ALU.add)
                dve.drain()
                nc.vector.tensor_scalar(count[:], count[:], -ROUND, None, ALU.add)
                dve.drain()
                nc.vector.tensor_tensor_scan(last[:], k.ones[:, 0:E], count[:], 0.0, ALU.mult, ALU.add)
                dve.drain()
                nc.vector.tensor_tensor(first[:], last[:], count[:], ALU.subtract)
                dve.drain()
                nc.vector.tensor_scalar(first[:], first[:], float(P), None, ALU.mult)
                dve.drain()
                nc.vector.tensor_tensor(before[:], psC[:], first[:].unsqueeze(1).to_broadcast([P, T, E]), ALU.add)
                dve.drain()
                nc.vector.tensor_tensor(before[:], before[:], sel[:], ALU.mult)
                dve.drain()
                nc.vector.tensor_reduce(place[:], before[:], AX.X, ALU.add)
                dve.drain()
                nc.vector.tensor_copy(slot[:], place[:])
                nc.vector.tensor_tensor(past[:], tile_no[:].unsqueeze(2).to_broadcast([1, tiles, E]),
                                        last[0:1, :].unsqueeze(1).to_broadcast([1, tiles, E]), ALU.is_ge)
                dve.drain()
                nc.vector.tensor_reduce(tile_no[:], past[:], AX.X, ALU.add)
                dve.drain()
                nc.vector.tensor_scalar(tile_expert[:], tile_no[:], float(E - 1), None, ALU.min)
    w_in.close(32 if r_bias is not None else 16)
    logits.close(1)
    asked.close(1)
    exped.close(1)
    if sort:
        for t in (made, counted, counts):
            t.close(1)


def experts_stage(k, name, comb, w_up, w_down, count, chunk, chunks, gated, biased, acc, clear=False):
    nc = k.nc
    WU = chunks * chunk * (2 if gated else 1) + (2 * chunks if biased else 0)
    UNITS = NBLK * chunks
    up_done, silu_done, hid_done, down_done, acc_done = (
        k.tally(n) for n in ("up_done", "silu_done", "hid_done", "down_done", "acc_done"))
    w_in = [k.tally(f"w_in{i}") for i in range(2)]
    pairs = count // 2
    odd = count % 2
    looped = pairs if odd else pairs - 1
    with ExitStack() as s:
        wu = [s.enter_context(nc.sbuf_tensor(f"{name}_wu{i}", [P, WU], F32)) for i in range(2)]
        wd = [s.enter_context(nc.sbuf_tensor(f"{name}_wd{i}", [chunk, chunks * D], F32)) for i in range(2)]
        sg = s.enter_context(nc.sbuf_tensor(f"{name}_sg", [chunk, 2, 512], F32))
        hid = s.enter_context(nc.sbuf_tensor(f"{name}_hid", [chunk, 2, 512], F32))
        psG = s.enter_context(nc.psum_tensor(f"{name}_psG", [P, 2, 512], F32))
        psU = s.enter_context(nc.psum_tensor(f"{name}_psU", [P, 2, 512], F32)) if gated else None
        psD = s.enter_context(nc.psum_tensor(f"{name}_psD", [P, 2, 512], F32))
        block = s.enter_context(nc.Block())

        def steps(first, experts, follow):
            u = [(e, b, c) for e in range(experts) for b in range(NBLK) for c in range(chunks)]
            for j, unit in enumerate(u):
                nxt = u[j + 1] if j + 1 < len(u) else ((0, 0, 0) if follow else None)
                yield j, unit, nxt

        def engine(eng, body):
            if looped:
                with eng.Fori(0, looped) as i:
                    body(i, 2, True)
            if odd:
                body(pairs, 1, False)
            else:
                body(pairs - 1, 2, False)

        @block.sync
        def _(sp):
            def load(e, half):
                sp.dma_start(wu[half][:], w_up[bass.ds(e, 1), :, :].rearrange("a p f -> p (a f)"))\
                    .then_inc(w_in[half].sem, 16)
                sp.dma_start(wd[half][:], w_down[bass.ds(e, 1), :, :].rearrange("a p f -> p (a f)"))\
                    .then_inc(w_in[half].sem, 16)

            load(0, 0)
            if count > 1:
                load(1, 1)
            if pairs > 1:
                with sp.Fori(1, pairs) as i:
                    for half in range(2):
                        sp.wait_ge(*down_done.at(2 * NBLK * i + (NBLK * (half - 1))))
                        load(2 * i + half, half)
            if odd:
                sp.wait_ge(*down_done.at(NBLK * (count - 2)))
                load(count - 1, 0)

        @block.tensor
        def _(pe):
            def up(i, j, unit):
                half, b, c = unit
                if b == 0 and c == 0:
                    pe.wait_ge(*w_in[half].at(32 * i + 32))
                pe.wait_ge(*hid_done.at(2 * UNITS * i + (j + 1)))
                x = k.XT[:, b * 512:(b + 1) * 512]
                w = wu[half]
                m = nc.tensor.matmul(psG[0:chunk, j % 2, :], w[:, c * chunk:(c + 1) * chunk], x, start=True, stop=True)
                if gated:
                    o = (chunks + c) * chunk
                    m = nc.tensor.matmul(psU[0:chunk, j % 2, :], w[:, o:o + chunk], x, start=True, stop=True)
                m.then_inc(up_done.sem, 1)

            def down(i, j, unit):
                half, b, c = unit
                pe.wait_ge(*hid_done.at(2 * UNITS * i + (j + 3)))
                if c == 0:
                    pe.wait_ge(*acc_done.at(2 * NBLK * i + (NBLK * half + b + 1)))
                for t in range(4):
                    m = nc.tensor.matmul(psD[:, b % 2, t * P:(t + 1) * P], hid[:, j % 2, t * P:(t + 1) * P],
                                         wd[half][:, c * D:(c + 1) * D], start=(c == 0 and t == 0),
                                         stop=(c == chunks - 1 and t == 3), skip_group_check=True)
                if c == chunks - 1:
                    m.then_inc(down_done.sem, 1)

            def body(i, experts, follow):
                for j, unit, nxt in steps(i, experts, follow):
                    if nxt is not None:
                        if j + 1 < experts * UNITS:
                            up(i, j + 1, nxt)
                        else:
                            up(i + 1, 0, nxt)
                    down(i, j, unit)

            up(0, 0, (0, 0, 0))
            engine(pe, body)

        @block.scalar
        def _(act):
            def body(i, experts, follow):
                for j, (half, b, c), _ in steps(i, experts, follow):
                    act.wait_ge(*up_done.at(2 * UNITS * i + (j + 1)))
                    w = wu[half]
                    o = chunks * chunk * 2 + c
                    bias = {"bias": w[0:chunk, o:o + 1]} if biased else {}
                    if gated:
                        nc.scalar.activation(sg[:, j % 2, :], psG[0:chunk, j % 2, :], ACT.Silu, **bias)\
                            .then_inc(silu_done.sem, 1)
                    else:
                        nc.scalar.activation(hid[:, j % 2, :], psG[0:chunk, j % 2, :], ACT.Silu, **bias)\
                            .then_inc(hid_done.sem, 1)

            if not gated:
                act.sem_inc(hid_done.sem, 2)
            engine(act, body)

        @block.vector
        def _(dve):
            def hide(i, j, unit):
                half, b, c = unit
                dve.wait_ge(*silu_done.at(2 * UNITS * i + (j + 1)))
                w = wu[half]
                o = chunks * chunk * 2 + chunks + c
                if biased:
                    m = nc.vector.scalar_tensor_tensor(out=hid[:, j % 2, :], in0=psU[0:chunk, j % 2, :],
                                                       scalar=w[0:chunk, o:o + 1], in1=sg[:, j % 2, :],
                                                       op0=ALU.add, op1=ALU.mult)
                else:
                    m = nc.vector.tensor_tensor(hid[:, j % 2, :], psU[0:chunk, j % 2, :], sg[:, j % 2, :], ALU.mult)
                m.then_inc(hid_done.sem, 1)

            def add(i, unit):
                half, b, c = unit
                dve.wait_ge(*down_done.at(2 * NBLK * i + (NBLK * half + b + 1)))
                for t in range(4):
                    a = acc[:, 4 * b + t, :]
                    m = nc.vector.scalar_tensor_tensor(out=a, in0=psD[:, b % 2, t * P:(t + 1) * P],
                                                       scalar=comb[:, 4 * b + t, bass.ds(2 * i + half, 1)], in1=a,
                                                       op0=ALU.mult, op1=ALU.add)
                m.then_inc(acc_done.sem, 1)

            def body(i, experts, follow):
                for j, unit, nxt in steps(i, experts, follow):
                    if gated and nxt is not None:
                        if j + 1 < experts * UNITS:
                            hide(i, j + 1, nxt)
                        else:
                            hide(i + 1, 0, nxt)
                    if unit[2] == chunks - 1:
                        add(i, unit)

            if clear:
                nc.vector.memset(acc[:], 0.0)
                dve.drain()
            dve.sem_inc(acc_done.sem, 2)
            if gated:
                dve.sem_inc(hid_done.sem, 2)
                hide(0, 0, (0, 0, 0))
            engine(dve, body)
    up_done.close(count * UNITS)
    if gated:
        silu_done.close(count * UNITS)
    hid_done.close(count * UNITS + 2)
    down_done.close(count * NBLK)
    acc_done.close(count * NBLK + 2)
    w_in[0].close(32 * (pairs + odd))
    w_in[1].close(32 * pairs)


def moe_l0_stage(k, a):
    E, F = 8, 256
    nc = k.nc
    with nc.sbuf_tensor("m0_comb", [P, T, E], F32) as comb:
        route_stage(k, "m0", comb, a["L0_ffn_router"], None, E, top=2, of_probs=False, renormed=True)
        with nc.sbuf_tensor("m0_combT", [E, N], F32) as combT, nc.sbuf_tensor("m0_b3", [E, D], F32) as b3:
            turn_comb_stage(k, "m0", comb, combT, b3, a["L0_ffn_b3"])
            project_and_add_stage(k, "m0", None, combT, b3)
        experts_stage(k, "m0", comb, a["L0_ffn_up"], a["L0_ffn_down"], E, P, F // P, True, True, k.X)


def turn_comb_stage(k, name, comb, combT, b3_sb, b3):
    nc = k.nc
    loaded, turned, copied = (k.tally(n) for n in ("loaded", "turned", "copied"))
    E = combT.shape[0]
    with nc.psum_tensor(f"{name}_psTC", [P, 4, 512], F32) as ps, nc.Block() as block:
        @block.sync
        def _(sp):
            sp.dma_start(b3_sb[:], b3).then_inc(loaded.sem, 16)
            sp.wait_ge(*loaded.at(16))

        @block.tensor
        def _(pe):
            for g in range(4):
                for j in range(4):
                    m = nc.tensor.transpose(ps[0:E, g, j * P:(j + 1) * P], comb[:, 4 * g + j, :], k.ident[:])
                m.then_inc(turned.sem, 1)

        @block.scalar
        def _(act):
            for g in range(4):
                act.wait_ge(*turned.at(g + 1))
                nc.scalar.activation(combT[:, g * 512:(g + 1) * 512], ps[0:E, g, :], ACT.Copy).then_inc(copied.sem, 1)
    loaded.close(16)
    turned.close(4)
    copied.close(4)


def moe_l1_stage(k, a):
    E, F, S = 16, 64, 2
    with k.nc.sbuf_tensor("m1_comb", [P, T, E + S], F32) as comb:
        route_stage(k, "m1", comb, a["L1_ffn_router"], a["L1_ffn_router_bias"], E, top=2, of_probs=False,
                    renormed=True, always=S)
        experts_stage(k, "m1", comb, a["L1_ffn_up"], a["L1_ffn_down"], E + S, F, 1, True, False, k.X)


SLOT_TILES = 32
UNROLL, AHEAD = 4, 7


def steps(eng, step, last):
    for v in range(AHEAD):
        step(v, v % UNROLL)
    trips = (SLOT_TILES - AHEAD) // UNROLL
    with eng.Fori(0, trips) as i:
        for c in range(UNROLL):
            step(i * UNROLL + (AHEAD + c), (AHEAD + c) % UNROLL)
    for v in range(AHEAD + trips * UNROLL, last):
        step(v, v % UNROLL)


def inside(j):
    return not isinstance(j, int) or 0 <= j < SLOT_TILES


def some(n):
    return not isinstance(n, int) or n > 0


def rounds(v, m, off=0, each=16):
    if isinstance(v, int):
        return each * ((v - m) // UNROLL + 1 - off)
    return v * (each // UNROLL) + (each - each // UNROLL * m - each * off)


E2, F2, SLOTS = 64, 96, 64
ROW = D + E2
LATER = 2.0 * N


def moe_l2_stage(k, a):
    nc = k.nc
    with ExitStack() as s:
        sb = lambda n, shape, dt=F32: s.enter_context(nc.sbuf_tensor(f"m2_{n}", shape, dt))
        comb, chosen = sb("comb", [P, T, E2]), sb("chosen", [P, T, E2])
        token, row = sb("token", [P, SLOT_TILES]), sb("row", [P, SLOT_TILES], mybir.dt.uint32)
        count = sb("count", [P, N], F16)
        k.token_rows = nc.dram_tensor("token_rows", (N, ROW), F32).ap()
        route_stage(k, "m2", comb, a["L2_ffn_router"], None, E2, top=8, of_probs=True, renormed=True, chosen=chosen)
        acc = s.enter_context(nc.psum_tensor("m2_acc", [P, NBLK, 512], F32))
        slots_stage(k, a, comb, chosen, acc, token, row, count)
        slot_experts_stage(k, a, acc, token, row, count)
        with nc.psum_tensor("m2_psA", [P, NBLK, 512], F32) as ps:
            add_turned_stage(k, acc, ps)


def slots_stage(k, a, comb, chosen, acc, token, row, count):
    nc = k.nc
    saved, w_in, made, turned, valued, listed, spread, up_done, silu_done, hid_done, down_done = (
        k.tally(n) for n in ("saved", "w_in", "made", "turned", "valued", "listed", "spread", "up_done",
                                     "silu_done", "hid_done", "down_done"))
    with ExitStack() as s:
        sb = lambda n, shape, dt=F32: s.enter_context(nc.sbuf_tensor(f"sl_{n}", shape, dt))
        late = sb("late", [E2, N])
        V = [sb(f"V{i}", [E2, N]) for i in range(2)]
        top = sb("top", [E2, 2, SLOTS])
        numbers = sb("numbers", [P, N])
        wu, wd = sb("wu", [P, 2 * F2]), sb("wd", [F2, D])
        sg, hid = sb("sg", [F2, 2, 512]), sb("hid", [F2, 2, 512])
        psG, psU = (s.enter_context(nc.psum_tensor(f"sl_ps{n}", [P, 2, 512], F32)) for n in "GU")
        block = s.enter_context(nc.Block())

        @block.sync
        def _(sp):
            sp.dma_start(wu[:], a["L2_ffn_up"][E2]).then_inc(w_in.sem, 16)
            sp.dma_start(wd[:], a["L2_ffn_down"][E2]).then_inc(w_in.sem, 16)
            rows = k.token_rows.rearrange("(t p) r -> p t r", p=P)
            sp.dma_start(rows[:, :, 0:D], k.X[:]).then_inc(saved.sem, 16)
            sp.dma_start(rows[:, :, D:ROW], comb[:]).then_inc(saved.sem, 16)
            sp.wait_ge(*saved.at(32))

        @block.gpsimd
        def _(pool):
            nc.gpsimd.iota(late[:], [[-1, N]], base=int(LATER), channel_multiplier=0,
                           allow_small_or_imprecise_dtypes=True).then_inc(made.sem, 1)
            nc.gpsimd.iota(numbers[:], [[1, N]], base=0, channel_multiplier=0,
                           allow_small_or_imprecise_dtypes=True).then_inc(made.sem, 1)

        @block.tensor
        def _(pe):
            for g in range(NBLK):
                for j in range(4):
                    m = nc.tensor.transpose(acc[0:E2, g, j * P:(j + 1) * P], chosen[:, 4 * g + j, :], k.ident[:])
                m.then_inc(turned.sem, 1)
            pe.wait_ge(*w_in.at(32))

            def up(b):
                if b >= 2:
                    pe.wait_ge(*hid_done.at(b - 1))
                x = k.XT[:, b * 512:(b + 1) * 512]
                nc.tensor.matmul(psG[0:F2, b % 2, :], wu[:, 0:F2], x, start=True, stop=True)
                nc.tensor.matmul(psU[0:F2, b % 2, :], wu[:, F2:2 * F2], x, start=True, stop=True)\
                    .then_inc(up_done.sem, 1)

            up(0)
            pe.wait_ge(*valued.at(NBLK))
            for b in range(NBLK):
                if b + 1 < NBLK:
                    up(b + 1)
                pe.wait_ge(*hid_done.at(b + 1))
                nc.tensor.matmul(acc[:, b, :], wd[:], hid[:, b % 2, :], start=True, stop=True)\
                    .then_inc(down_done.sem, 1)
            pe.wait_ge(*listed.at(1))
            nc.tensor.matmul(psG[:, 0, 0:E2], top[:].rearrange("e h c -> e (h c)"), k.ident[0:E2, 0:E2],
                             start=True, stop=True).then_inc(spread.sem, 1)

        @block.scalar
        def _(act):
            for b in range(NBLK):
                act.wait_ge(*up_done.at(b + 1))
                nc.scalar.activation(sg[:, b % 2, :], psG[0:F2, b % 2, :], ACT.Silu).then_inc(silu_done.sem, 1)

        @block.vector
        def _(dve):
            dve.wait_ge(*made.at(1))
            for g in range(NBLK):
                dve.wait_ge(*turned.at(g + 1))
                c = slice(g * 512, (g + 1) * 512)
                nc.vector.tensor_tensor(V[0][:, c], acc[0:E2, g, :], late[:, c], ALU.mult).then_inc(valued.sem, 1)
            for b in range(NBLK):
                dve.wait_ge(*silu_done.at(b + 1))
                if b >= 2:
                    dve.wait_ge(*down_done.at(b - 1))
                nc.vector.tensor_tensor(hid[:, b % 2, :], psU[0:F2, b % 2, :], sg[:, b % 2, :], ALU.mult)\
                    .then_inc(hid_done.sem, 1)
            dve.drain()
            for r in range(SLOTS // 8):
                nc.vector.max(top[:, 0, 8 * r:8 * r + 8], V[r % 2][:])
                dve.drain()
                if r < SLOTS // 8 - 1:
                    nc.vector.match_replace(V[(r + 1) % 2][:], top[:, 0, 8 * r:8 * r + 8], V[r % 2][:], 0.0)
                    dve.drain()
            nc.vector.tensor_copy(top[:, 1, :], top[:, 0, :]).then_inc(listed.sem, 1)
            dve.wait_ge(*made.at(2))
            nc.vector.tensor_copy(count[:], numbers[:])
            dve.wait_ge(*spread.at(1))
            for h in range(2):
                half = slice(SLOTS * h, SLOTS * (h + 1))
                nc.vector.tensor_scalar(token[half, :], psG[half, 0, h:E2:2], -1.0, LATER, ALU.mult, ALU.add)
            dve.drain()
            nc.vector.tensor_scalar(row[:], token[:], float(N - 1), None, ALU.min)
    saved.close(32)
    w_in.close(32)
    made.close(2)
    for t in (turned, valued, up_done, silu_done, hid_done, down_done):
        t.close(NBLK)
    listed.close(1)
    spread.close(1)


def slot_experts_stage(k, a, acc, token, row, count):
    nc = k.nc
    gathered = [k.tally(f"gathered{m}") for m in range(UNROLL)]
    w_in = [k.tally(f"w_in{m}") for m in range(UNROLL)]
    turned, x_out, up_done, silu_done, hid_done, down_done, high_done, parts_done, placed, used = (
        k.tally(n) for n in ("turned", "x_out", "up_done", "silu_done", "hid_done", "down_done",
                                     "high_done", "parts_done", "placed", "used"))
    with ExitStack() as s:
        sb = lambda n, shape, dt=F32: s.enter_context(nc.sbuf_tensor(f"se_{n}", shape, dt))
        xs = [sb(f"xs{m}", [P, ROW]) for m in range(UNROLL)]
        wu = [sb(f"wu{m}", [P, 2, 2 * F2]) for m in range(UNROLL)]
        wd = [sb(f"wd{m}", [F2, 2, D]) for m in range(UNROLL)]
        weight = [sb(f"weight{m}", [P, 1]) for m in range(UNROLL)]
        xT = [sb(f"xT{b}", [P, P]) for b in range(2)]
        sg, hid = ([sb(f"{n}{b}", [F2, P]) for b in range(2)] for n in ("sg", "hid"))
        rest = sb("rest", [P, D])
        parts = [sb(f"parts{b}", [P, 3, D], BF16) for b in range(2)]
        place = [sb(f"place{b}", [P, N], BF16) for b in range(2)]
        psX, psY = (s.enter_context(nc.psum_tensor(f"se_ps{n}", [P, 512], F32)) for n in "XY")
        psH = [s.enter_context(nc.psum_tensor(f"se_psH{b}", [P, 2, 256], F32)) for b in range(2)]
        block = s.enter_context(nc.Block())

        @block.gpsimd
        def _(pool):
            for j in range(SLOT_TILES):
                m = j % UNROLL
                if j >= UNROLL:
                    pool.wait_ge(*x_out.at(j - UNROLL + 1))
                pool.indirect_dma_start(xs[m][:], None, k.token_rows, bass.IndirectOffsetOnAxis(row[:, j:j + 1], 0))\
                    .then_inc(gathered[m].sem, 16)

        @block.sync
        def _(sp):
            def step(v, m):
                if inside(v):
                    if some(v - 3):
                        sp.wait_ge(*down_done.at(v - 3))
                    sp.dma_start(wu[m][:], a["L2_ffn_up"][bass.ds(v * 2, 2), :, :].rearrange("e p f -> p e f"))\
                        .then_inc(w_in[m].sem, 16)
                    sp.dma_start(wd[m][:], a["L2_ffn_down"][bass.ds(v * 2, 2), :, :].rearrange("e p f -> p e f"))\
                        .then_inc(w_in[m].sem, 16)

            steps(sp, step, SLOT_TILES)

        @block.tensor
        def _(pe):
            def step(v, m):
                j, b = v, m % 2
                if inside(j):
                    pe.wait_ge(*gathered[m].at(rounds(v, m)))
                    if some(j):
                        pe.wait_ge(*x_out.at(j))
                    nc.tensor.transpose(psX[:, 0:P], xs[m][:, 0:D], k.ident[:]).then_inc(turned.sem, 1)
                j, m1, b = v - 1, (m - 1) % UNROLL, (m - 1) % 2
                if inside(j):
                    pe.wait_ge(*w_in[m1].at(rounds(j, m1, each=32)))
                    pe.wait_ge(*x_out.at(j + 1))
                    if some(j - 1):
                        pe.wait_ge(*hid_done.at(j - 1))
                    for e in range(2):
                        half = slice(e * SLOTS, (e + 1) * SLOTS)
                        nc.tensor.matmul(psH[b][0:F2, 0, half], wu[m1][:, e, 0:F2], xT[b][:, half], start=True, stop=True)
                        i = nc.tensor.matmul(psH[b][0:F2, 1, half], wu[m1][:, e, F2:2 * F2], xT[b][:, half],
                                             start=True, stop=True)
                    i.then_inc(up_done.sem, 1)
                j, m2, b = v - 2, (m - 2) % UNROLL, (m - 2) % 2
                if inside(j):
                    pe.wait_ge(*hid_done.at(j + 1))
                    if some(j):
                        pe.wait_ge(*parts_done.at(j))
                    for e in range(2):
                        half = slice(e * SLOTS, (e + 1) * SLOTS)
                        i = nc.tensor.matmul(psY[half, 0:D], hid[b][:, half], wd[m2][:, e, :], start=True, stop=True)
                    i.then_inc(down_done.sem, 1)
                j, b = v - 3, (m - 3) % 2
                if inside(j):
                    pe.wait_ge(*parts_done.at(j + 1))
                    pe.wait_ge(*placed.at(j + 1))
                    for part in range(3):
                        for g in range(NBLK):
                            i = nc.tensor.matmul(acc[:, g, :], parts[b][:, part, :], place[b][:, g * 512:(g + 1) * 512],
                                                 start=False, stop=True, skip_group_check=True)
                    i.then_inc(used.sem, 1)

            steps(pe, step, SLOT_TILES + 3)

        @block.scalar
        def _(act):
            def step(v, m):
                j, b = v, m % 2
                if inside(j):
                    act.wait_ge(*turned.at(j + 1))
                    if some(j - 3):
                        act.wait_ge(*parts_done.at(j - 3))
                    for e in range(2):
                        half = slice(e * SLOTS, (e + 1) * SLOTS)
                        nc.scalar.activation(weight[m][half, :], xs[m][half, bass.ds(j * 2 + (D + e), 1)], ACT.Copy)
                    if some(j - 1):
                        act.wait_ge(*up_done.at(j - 1))
                    nc.scalar.activation(xT[b][:], psX[:, 0:P], ACT.Copy).then_inc(x_out.sem, 1)
                j, b = v - 1, (m - 1) % 2
                if inside(j):
                    act.wait_ge(*up_done.at(j + 1))
                    if some(j - 1):
                        act.wait_ge(*hid_done.at(j - 1))
                    nc.scalar.activation(sg[b][:], psH[b][0:F2, 0, 0:P], ACT.Silu).then_inc(silu_done.sem, 1)
                j, m2, b = v - 2, (m - 2) % UNROLL, (m - 2) % 2
                if inside(j):
                    act.wait_ge(*down_done.at(j + 1))
                    if some(j - 1):
                        act.wait_ge(*used.at(j - 1))
                    nc.scalar.activation(parts[b][:, 0, :], psY[:, 0:D], ACT.Copy, scale=weight[m2][:, 0:1])\
                        .then_inc(high_done.sem, 1)

            steps(act, step, SLOT_TILES + 2)

        @block.vector
        def _(dve):
            def step(v, m):
                j, b = v - 1, (m - 1) % 2
                if inside(j):
                    dve.wait_ge(*silu_done.at(j + 1))
                    if some(j - 1):
                        dve.wait_ge(*down_done.at(j - 1))
                    nc.vector.tensor_tensor(hid[b][:], psH[b][0:F2, 1, 0:P], sg[b][:], ALU.mult).then_inc(hid_done.sem, 1)
                j, m2, b = v - 2, (m - 2) % UNROLL, (m - 2) % 2
                if inside(j):
                    dve.wait_ge(*high_done.at(j + 1))
                    nc.vector.scalar_tensor_tensor(out=rest[:], in0=psY[:, 0:D], scalar=weight[m2][:, 0:1],
                                                   in1=parts[b][:, 0, :], op0=ALU.mult, op1=ALU.subtract)
                    dve.drain()
                    nc.vector.tensor_copy(parts[b][:, 1, :], rest[:])
                    dve.drain()
                    nc.vector.tensor_tensor(parts[b][:, 2, :], rest[:], parts[b][:, 1, :], ALU.subtract)\
                        .then_inc(parts_done.sem, 1)
                    if some(j - 1):
                        dve.wait_ge(*used.at(j - 1))
                    nc.vector.tensor_scalar(place[b][:], count[:], token[:, bass.ds(j, 1)], None, ALU.is_equal)\
                        .then_inc(placed.sem, 1)

            steps(dve, step, SLOT_TILES + 2)
    for t in gathered:
        t.close(16 * SLOT_TILES // UNROLL)
    for t in w_in:
        t.close(32 * SLOT_TILES // UNROLL)
    for t in (turned, x_out, up_done, silu_done, hid_done, down_done, high_done, parts_done, placed, used):
        t.close(SLOT_TILES)


def add_turned_stage(k, acc, ps):
    nc = k.nc
    copied, turned, added = (k.tally(n) for n in ("copied", "turned", "added"))
    with nc.Block() as block:
        @block.scalar
        def _(act):
            for g in range(NBLK):
                nc.scalar.activation(k.XT[:, g * 512:(g + 1) * 512], acc[:, g, :], ACT.Copy).then_inc(copied.sem, 1)

        @block.tensor
        def _(pe):
            for g in range(NBLK):
                pe.wait_ge(*copied.at(g + 1))
                for j in range(4):
                    t = 4 * g + j
                    m = nc.tensor.transpose(ps[:, g, j * P:(j + 1) * P], k.XT[:, t * P:(t + 1) * P], k.ident[:])
                m.then_inc(turned.sem, 1)

        @block.vector
        def _(dve):
            for g in range(NBLK):
                dve.wait_ge(*turned.at(g + 1))
                x = k.X[:, 4 * g:4 * g + 4, :].rearrange("p t d -> p (t d)")
                nc.vector.tensor_tensor(x, ps[:, g, :], x, ALU.add).then_inc(added.sem, 1)
    for t in (copied, turned, added):
        t.close(NBLK)


E3, F3, LAYERS = 16, 512, 4


def load_l3_weights(k, a):
    nc = k.nc
    k.W1, k.W2 = k.keep("W1", [P, E3, F3]), k.keep("W2", [P, E3, F3])
    k.sorted_x = nc.dram_tensor("sorted_x", (SLOT_TILES * P, D), F32).ap()
    k.sorted_y = nc.dram_tensor("sorted_y", (SLOT_TILES * P, D), F32).ap()
    loaded, zeroed, cleared = k.tally("l3_loaded"), k.tally("l3_zeroed"), k.tally("l3_cleared")
    zero = k.keep("zero", [P, D])
    with nc.Block() as block:
        @block.vector
        def _(dve):
            nc.vector.memset(zero[:], 0.0).then_inc(cleared.sem, 1)

        @block.sync
        def _(sp):
            for g in range(4):
                e = slice(4 * g, 4 * g + 4)
                sp.dma_start(k.W1[:, e, :], a["L3_ffn_up"][e].rearrange("e p f -> p e f")).then_inc(loaded.sem, 16)
                sp.dma_start(k.W2[:, e, :], a["L3_ffn_down"][e].rearrange("e p f -> p e f")).then_inc(loaded.sem, 16)
            sp.wait_ge(*cleared.at(1))
            sp.dma_start(k.sorted_x.rearrange("(j p) d -> p j d", p=P),
                         zero[:].unsqueeze(1).to_broadcast([P, SLOT_TILES, D])).then_inc(zeroed.sem, 16)


def sorted_experts_stage(k, name, Y, slot, tile_expert, first):
    nc = k.nc
    C = F3 // P
    scattered, loaded_w, zeroed = k.tally("scattered"), k.tally("l3_loaded"), k.tally("l3_zeroed")
    x_in = [k.tally(f"x_in{i}") for i in range(4)]
    stored = [k.tally(f"stored{i}") for i in range(4)]
    turned_x, x_out, up_done, silu_done, turned_h, h_out, down_done, y_out = (
        k.tally(n) for n in
        ("turned_x", "x_out", "up_done", "silu_done", "turned_h", "h_out", "down_done", "y_out"))
    with ExitStack() as s:
        sb = lambda n, shape: s.enter_context(nc.sbuf_tensor(f"{name}_{n}", shape, F32))
        xs = [sb(f"xs{i}", [P, D]) for i in range(4)]
        ys = [sb(f"ys{i}", [P, D]) for i in range(4)]
        xT = [sb(f"xT{i}", [P, P]) for i in range(2)]
        h = [sb(f"h{i}", [P, F3]) for i in range(2)]
        hT = [sb(f"hT{i}", [P, F3]) for i in range(2)]
        pb = lambda n: s.enter_context(nc.psum_tensor(f"{name}_{n}", [P, 512], F32))
        psX, psH, psT, psY = ([pb(f"ps{n}{i}") for i in range(2)] for n in "XHTY")
        block = s.enter_context(nc.Block())
        tile_rows = lambda t, j: t.rearrange("(j p) d -> j p d", p=P)[bass.ds(j, 1), :, :]\
            .rearrange("a p d -> (a p) d")

        @block.gpsimd
        def _(pool):
            if first:
                pool.wait_ge(*zeroed.at(16))
            for t in range(T):
                pool.indirect_dma_start(k.sorted_x, bass.IndirectOffsetOnAxis(slot[:, t:t + 1], 0), Y[:, t, :], None)\
                    .then_inc(scattered.sem, 16)

        @block.sync
        def _(sp):
            sp.wait_ge(*scattered.at(16 * T))

            def step(v, m):
                if inside(v):
                    if some(v - 3):
                        sp.wait_ge(*turned_x.at(v - 3))
                    sp.dma_start(xs[m][:], tile_rows(k.sorted_x, v)).then_inc(x_in[m].sem, 16)
                j = v - 6
                if inside(j):
                    sp.wait_ge(*y_out.at(j + 1))
                    sp.dma_start(tile_rows(k.sorted_y, j), ys[(m - 6) % 4][:]).then_inc(stored[(m - 6) % 4].sem, 16)

            steps(sp, step, SLOT_TILES + 6)
            for t in stored:
                sp.wait_ge(*t.at(16 * SLOT_TILES // 4))

        @block.tensor
        def _(pe):
            if first:
                pe.wait_ge(*loaded_w.at(128))

            def expert(j):
                return pe.value_load(tile_expert[0:1, bass.ds(j, 1)], min_val=0, max_val=E3 - 1)

            def step(v, m):
                j = v
                if inside(j):
                    pe.wait_ge(*x_in[m].at(rounds(v, m)))
                    if some(j - 1):
                        pe.wait_ge(*x_out.at(j - 1))
                    nc.tensor.transpose(psX[m % 2][:, 0:P], xs[m][:], k.ident[:]).then_inc(turned_x.sem, 1)
                j, b = v - 1, (m - 1) % 2
                if inside(j):
                    e = expert(j)
                    pe.wait_ge(*x_out.at(j + 1))
                    if some(j - 1):
                        pe.wait_ge(*silu_done.at(j - 1))
                    nc.tensor.matmul(psH[b][:], xT[b][:], k.W1[:, bass.ds(e, 1), :].rearrange("p a f -> p (a f)"),
                                     start=True, stop=True).then_inc(up_done.sem, 1)
                j, b = v - 2, (m - 2) % 2
                if inside(j):
                    pe.wait_ge(*silu_done.at(j + 1))
                    if some(j - 1):
                        pe.wait_ge(*h_out.at(j - 1))
                    for c in range(C):
                        i = nc.tensor.transpose(psT[b][:, c * P:(c + 1) * P], h[b][:, c * P:(c + 1) * P], k.ident[:])
                    i.then_inc(turned_h.sem, 1)
                j, b = v - 3, (m - 3) % 2
                if inside(j):
                    e = expert(j)
                    pe.wait_ge(*h_out.at(j + 1))
                    if some(j - 1):
                        pe.wait_ge(*y_out.at(j - 1))
                    for c in range(C):
                        i = nc.tensor.matmul(psY[b][:, 0:D], hT[b][:, c * P:(c + 1) * P],
                                             k.W2[:, bass.ds(e, 1), c * D:(c + 1) * D].rearrange("p a f -> p (a f)"),
                                             start=(c == 0), stop=(c == C - 1))
                    i.then_inc(down_done.sem, 1)

            steps(pe, step, SLOT_TILES + 3)

        @block.scalar
        def _(act):
            def step(v, m):
                j, b = v - 1, (m - 1) % 2
                if inside(j):
                    act.wait_ge(*up_done.at(j + 1))
                    nc.scalar.activation(h[b][:], psH[b][:], ACT.Silu).then_inc(silu_done.sem, 1)
                j, b = v - 3, (m - 3) % 2
                if inside(j):
                    act.wait_ge(*down_done.at(j + 1))
                    q = (m - 3) % 4
                    if some(rounds(j, q, off=1)):
                        act.wait_ge(*stored[q].at(rounds(j, q, off=1)))
                    nc.scalar.activation(ys[q][:], psY[b][:, 0:D], ACT.Copy).then_inc(y_out.sem, 1)

            steps(act, step, SLOT_TILES + 3)

        @block.vector
        def _(dve):
            def step(v, m):
                j = v
                if inside(j):
                    dve.wait_ge(*turned_x.at(j + 1))
                    nc.vector.tensor_copy(xT[m % 2][:], psX[m % 2][:, 0:P]).then_inc(x_out.sem, 1)
                j, b = v - 2, (m - 2) % 2
                if inside(j):
                    dve.wait_ge(*turned_h.at(j + 1))
                    nc.vector.tensor_copy(hT[b][:], psT[b][:]).then_inc(h_out.sem, 1)

            steps(dve, step, SLOT_TILES + 2)
    scattered.close(16 * T)
    for t in x_in + stored:
        t.close(16 * SLOT_TILES // 4)
    for t in (turned_x, x_out, up_done, silu_done, turned_h, h_out, down_done, y_out):
        t.close(SLOT_TILES)
    if first:
        loaded_w.close(128)
        zeroed.close(16)


def gather_stage(k, name, G, Y, weight, slot, last):
    nc = k.nc
    gathered, weighed, turned, copied = (k.tally(n) for n in ("gathered", "weighed", "turned", "copied"))
    gathered = [k.tally(f"gathered{g}") for g in range(4)]
    with nc.psum_tensor(f"{name}_psY", [P, 4, 512], F32) as ps, nc.Block() as block:
        @block.gpsimd
        def _(pool):
            for t in range(T):
                pool.indirect_dma_start(G[:, t, :], None, k.sorted_y, bass.IndirectOffsetOnAxis(slot[:, t:t + 1], 0))\
                    .then_inc(gathered[t // 4].sem, 16)

        @block.vector
        def _(dve):
            for g in range(4):
                dve.wait_ge(*gathered[g].at(64))
                for t in range(4 * g, 4 * g + 4):
                    if last:
                        m = nc.vector.scalar_tensor_tensor(out=k.X[:, t, :], in0=G[:, t, :], scalar=weight[:, t:t + 1],
                                                           in1=k.X[:, t, :], op0=ALU.mult, op1=ALU.add)
                    else:
                        m = nc.vector.tensor_scalar(Y[:, t, :], G[:, t, :], weight[:, t:t + 1], None, ALU.mult)
                m.then_inc(weighed.sem, 1)

        if not last:
            @block.tensor
            def _(pe):
                for g in range(4):
                    pe.wait_ge(*weighed.at(g + 1))
                    for j in range(4):
                        m = nc.tensor.transpose(ps[:, g, j * P:(j + 1) * P], Y[:, 4 * g + j, :], k.ident[:])
                    m.then_inc(turned.sem, 1)

            @block.scalar
            def _(act):
                for g in range(4):
                    act.wait_ge(*turned.at(g + 1))
                    nc.scalar.activation(k.XT[:, g * 512:(g + 1) * 512], ps[:, g, :], ACT.Copy).then_inc(copied.sem, 1)
    for t in gathered:
        t.close(64)
    weighed.close(4)
    if not last:
        turned.close(4)
        copied.close(4)


def moe_l3_stage(k, a):
    nc = k.nc
    with ExitStack() as s:
        sb = lambda n, shape, dt=F32: s.enter_context(nc.sbuf_tensor(f"m3_{n}", shape, dt))
        comb, G, Y, weight = sb("comb", [P, T, E3]), sb("G", [P, T, D]), sb("Y", [P, T, D]), sb("weight", [P, T])
        slot, tile_expert = sb("slot", [P, T], mybir.dt.uint32), sb("tile_expert", [1, SLOT_TILES], mybir.dt.int32)
        for layer in range(LAYERS):
            n = f"m3{layer}"
            route_stage(k, n, comb, a["L3_ffn_routers"][layer], None, E3, top=1, of_probs=True, renormed=False,
                        sort=(weight, slot, tile_expert))
            sorted_experts_stage(k, n, Y if layer else k.X, slot, tile_expert, layer == 0)
            gather_stage(k, n, G, Y, weight, slot, layer == LAYERS - 1)


def inverse_root(nc, dve, out, root, v, scratch):
    nc.vector.reciprocal(out, root)
    dve.drain()
    nc.vector.tensor_tensor(scratch, out, out, ALU.mult)
    dve.drain()
    nc.vector.tensor_tensor(scratch, scratch, v, ALU.mult)
    dve.drain()
    nc.vector.tensor_scalar(scratch, scratch, -0.5, 1.5, ALU.mult, ALU.add)
    dve.drain()
    nc.vector.tensor_tensor(out, out, scratch, ALU.mult)
    dve.drain()


CH = 32
DHEADS = D // CH
UN = N // CH
CPS = SEQ // CH
PE_TAPS = 25
LONG, SHORT, CONV = 64, 5, 4
EPS_L2 = 1e-6
FLOOR = 0.02



def delta_stage(k, a):
    nc = k.nc
    with ExitStack() as s:
        sb = lambda n, shape: s.enter_context(nc.sbuf_tensor(f"de_{n}", shape, F32))
        f = {n: sb(n, [P, N]) for n in (
            "qT", "kT", "short", "long", "qH", "kH", "vH", "sq", "kbH", "vbH", "attn", "delta")}
        pads = [sb(f"pad{i}", [P, BATCH, SEQ + CONV - 1]) for i in range(3)]
        vpad = sb("vpad", [P, BATCH, SEQ + LONG - 1])
        r1, r2, r3 = (t[:].rearrange("p b s -> p (b s)")[:, 0:N] for t in pads)
        w = {n: sb(n, [P, D]) for n in ("Wq", "Wk", "Wv", "Wxg", "Wg1x", "Wg1s", "Wg2", "Wo")}
        w["Wog1x"], w["Wog1s"], w["Wog2"] = sb("Wog1x", [P, D // 2]), sb("Wog1s", [P, D // 2]), sb("Wog2", [D // 2, D])
        taps = sb("taps", [P, 3 * CONV + SHORT + LONG])
        cols = sb("cols", [P, 6])
        rows = sb("rows", [P, 5])
        delta_filters(k, a, f, pads, vpad, w, taps, cols, rows)
        v = vpad[:, :, LONG - 1:]
        small = {n: sb(n, [P, UN]) for n in ("beta", "res", "ssk", "ssq", "rt", "rk", "rq", "t0")}
        delta_heads(k, f, v, w, cols, small, r1, r2, r3)
        delta_scan(k, f, r1, r2, r3)
        delta_gate(k, f, w, cols, rows, small, r1, r2, r3)
        project_and_add_stage(k, "de", None, r1, w["Wo"])


def delta_filters(k, a, f, pads, vpad, w, taps, cols, rows):
    nc = k.nc
    w_in, made, projected, padded, convd, silud, longed, diags = (
        k.tally(f"df_{n}") for n in ("w_in", "made", "projected", "padded", "convd", "silud", "longed", "diags"))
    T0 = 3 * CONV
    T1 = T0 + SHORT
    with nc.sbuf_tensor("df_diag", [P, PE_TAPS, P], F32) as diag, nc.psum_tensor("df_ps", [P, 2, 4, 512], F32) as ps, \
            nc.Block() as block:
        ahead = CONV - 1

        @block.sync
        def _(sp):
            for n in ("Wv", "Wq", "Wk"):
                sp.dma_start(w[n][:], a[f"L1_attn_{n}"]).then_inc(w_in.sem, 16)
            sp.dma_start(taps[:], a["L1_attn_taps"]).then_inc(w_in.sem, 16)
            rest = [(w[n], a[f"L1_attn_{n}"]) for n in
                    ("Wxg", "Wg1x", "Wg1s", "Wg2", "Wo", "Wog1x", "Wog1s", "Wog2", "cols")
                    if n != "cols"] + [(cols, a["L1_attn_cols"]), (rows, a["L1_attn_rows"].partition_broadcast(P))]
            for t, d in rest:
                sp.dma_start(t[:], d).then_inc(w_in.sem, 16)
            sp.wait_ge(*w_in.at(16 * (4 + len(rest))))

        @block.gpsimd
        def _(pool):
            for t in pads:
                nc.gpsimd.memset(t[:, :, 0:ahead], 0.0)
            nc.gpsimd.memset(vpad[:, :, 0:LONG - 1], 0.0).then_inc(made.sem, 1)
            pool.wait_ge(*w_in.at(16 * 14))
            for j in range(PE_TAPS):
                nc.gpsimd.tensor_scalar(diag[:, j, :], k.ident[:], taps[:, T1 + j:T1 + j + 1], None, ALU.mult)\
                    .then_inc(diags.sem, 1)

        @block.tensor
        def _(pe):
            pe.wait_ge(*w_in.at(16 * 14))
            for i, n in enumerate(("Wv", "Wq", "Wk")):
                if i == 2:
                    pe.wait_ge(*padded.at(1))
                for g in range(4):
                    m = nc.tensor.matmul(ps[:, i % 2, g, :], w[n][:], k.XT[:, g * 512:(g + 1) * 512],
                                         start=True, stop=True)
                m.then_inc(projected.sem, 1)
            pe.wait_ge(*padded.at(2))
            pe.wait_ge(*silud.at(1))
            pe.wait_ge(*diags.at(PE_TAPS))
            for g in range(4):
                for j in range(PE_TAPS):
                    m = nc.tensor.matmul(ps[:, 1, g, :], diag[:, j, :], vpad[:, 2 * g:2 * g + 2, j:j + SEQ],
                                         start=(j == 0), stop=(j == PE_TAPS - 1))
            m.then_inc(longed.sem, 1)

        @block.scalar
        def _(act):
            for i in range(3):
                act.wait_ge(*projected.at(i + 1))
                nc.scalar.activation(pads[(i + 2) % 3][:, :, ahead:], ps[:, i % 2, :, :].rearrange(
                    "p g (b s) -> p (g b) s", s=SEQ), ACT.Copy).then_inc(padded.sem, 1)
            outs = (vpad[:, :, LONG - 1:], f["qT"][:].rearrange("p (b s) -> p b s", b=BATCH),
                    f["kT"][:].rearrange("p (b s) -> p b s", b=BATCH))
            srcs = (f["sq"], f["qH"], f["kH"])
            act.wait_ge(*made.at(1))
            for i in range(3):
                act.wait_ge(*convd.at(i + 1))
                nc.scalar.activation(outs[i], srcs[i][:].rearrange("p (b s) -> p b s", b=BATCH), ACT.Silu)\
                    .then_inc(silud.sem, 1)

        @block.vector
        def _(dve):
            def fir(out, src, first, n, start, only_add=False):
                o = out[:].rearrange("p (b s) -> p b s", b=BATCH)
                for j in range(n):
                    x, t = src[:, :, start + j:start + j + SEQ], taps[:, first + j:first + j + 1]
                    if j == 0:
                        m = nc.vector.tensor_scalar(o, x, t, None, ALU.mult)
                    else:
                        dve.drain()
                        m = nc.vector.scalar_tensor_tensor(out=o, in0=x, scalar=t, in1=o, op0=ALU.mult, op1=ALU.add)
                return m

            dve.wait_ge(*w_in.at(16 * 14))
            dve.wait_ge(*made.at(1))
            for i, (tile, pad) in enumerate(((f["sq"], pads[2]), (f["qH"], pads[0]), (f["kH"], pads[1]))):
                dve.wait_ge(*padded.at(i + 1))
                fir(tile, pad, CONV * ((i + 2) % 3), CONV, 0).then_inc(convd.sem, 1)
            dve.wait_ge(*silud.at(1))
            fir(f["short"], vpad, T0, SHORT, LONG - SHORT)
            fir(f["long"], vpad, T1 + PE_TAPS, LONG - PE_TAPS, PE_TAPS)
            dve.wait_ge(*longed.at(1))
            dve.drain()
            l = f["long"][:]
            nc.vector.tensor_tensor(l, l, ps[:, 1, :, :].rearrange("p g c -> p (g c)"), ALU.add)


def delta_heads(k, f, v, w, cols, small, r1, r2, r3):
    nc = k.nc
    gates, gout, turned, squared, summed, rooted, asked, sig = (
        k.tally(f"dh_{n}") for n in ("gates", "gout", "turned", "squared", "summed", "rooted", "asked", "sig"))
    H = lambda ap: ap.rearrange("p (u d) -> p u d", d=CH)
    bc = lambda t: t[:].unsqueeze(2).to_broadcast([P, UN, CH])
    with nc.psum_tensor("dh_ps", [P, 4, 512], F32) as ps, nc.Block() as block:
        @block.tensor
        def _(pe):
            for g in range(4):
                m = nc.tensor.matmul(ps[:, g, :], w["Wxg"][:], k.XT[:, g * 512:(g + 1) * 512], start=True, stop=True)
            m.then_inc(gates.sem, 1)

        @block.scalar
        def _(act):
            act.wait_ge(*gates.at(1))
            nc.scalar.activation(r3, ps[:].rearrange("p g c -> p (g c)"), ACT.Copy).then_inc(gout.sem, 1)
            for i, n in enumerate(("qH", "kH")):
                act.wait_ge(*turned.at(i + 1))
                if i == 1:
                    act.wait_ge(*summed.at(1))
                nc.scalar.activation(f["sq"][:], f[n][:], ACT.Square).then_inc(squared.sem, 1)
            for i, (t, o) in enumerate((("ssq", "rt"), ("ssk", "t0"))):
                act.wait_ge(*asked.at(1))
                m = nc.scalar.activation(small[o][:], small[t][:], ACT.Sqrt)
            m.then_inc(rooted.sem, 1)
            act.wait_ge(*turned.at(3))
            g = r2.rearrange("p (u s) -> p u s", s=CH)
            nc.scalar.activation(small["beta"][:], g[:, :, 0], ACT.Sigmoid)
            nc.scalar.activation(small["res"][:], g[:, :, 1], ACT.Sigmoid, bias=cols[:, 0:1]).then_inc(sig.sem, 1)

        @block.vector
        def _(dve):
            nc.vector.transpose(f["qH"][:], f["qT"][:]).then_inc(turned.sem, 1)
            nc.vector.transpose(f["kH"][:], f["kT"][:]).then_inc(turned.sem, 1)
            for b in range(BATCH):
                nc.vector.transpose(f["vH"][:, b * SEQ:(b + 1) * SEQ], v[:, b, :])
            dve.wait_ge(*gout.at(1))
            nc.vector.transpose(r2, r3).then_inc(turned.sem, 1)
            for i, n in enumerate(("ssq", "ssk")):
                dve.wait_ge(*squared.at(i + 1))
                m = nc.vector.tensor_reduce(small[n][:], H(f["sq"][:]), AX.X, ALU.add)
                m.then_inc(summed.sem, 1)
                dve.drain()
                m = nc.vector.tensor_scalar(small[n][:], small[n][:], EPS_L2, None, ALU.add)
            m.then_inc(asked.sem, 1)
            dve.wait_ge(*rooted.at(1))
            for ss, rt, r in (("ssq", "rt", "rq"), ("ssk", "t0", "rk")):
                inverse_root(nc, dve, small[r][:], small[rt][:], small[ss][:], small[rt][:])
            nc.vector.tensor_tensor(H(f["qH"][:]), H(f["qH"][:]), bc(small["rq"]), ALU.mult)
            nc.vector.tensor_tensor(H(f["kH"][:]), H(f["kH"][:]), bc(small["rk"]), ALU.mult)
            dve.wait_ge(*sig.at(1))
            nc.vector.tensor_tensor(H(f["vbH"][:]), H(f["vH"][:]), bc(small["beta"]), ALU.mult)
            dve.drain()
            nc.vector.tensor_tensor(H(f["kbH"][:]), H(f["kH"][:]), bc(small["beta"]), ALU.mult)
            nc.vector.transpose(f["qT"][:], f["qH"][:])
            nc.vector.transpose(f["kT"][:], f["kH"][:])
            dve.drain()
            nc.vector.transpose(r1, f["kbH"][:])
    gates.close(1); gout.close(1); turned.close(3); squared.close(2); summed.close(2)
    rooted.close(1); asked.close(1); sig.close(1)


def delta_scan(k, f, r1, r2, r3):
    nc = k.nc
    blocked, multiplied, masked, opened, cleared = (
        k.tally(f"ds_{n}") for n in ("blocked", "multiplied", "masked", "opened", "cleared"))
    with ExitStack() as s:
        sb = lambda n, shape: s.enter_context(nc.sbuf_tensor(f"ds_{n}", shape, F32))
        bd = {n: sb(f"bd_{n}", [P, BATCH, D]) for n in ("kbT", "kT", "qT", "kH", "U", "attn")}
        strict, incl = sb("strict", [P, CH]), sb("incl", [P, CH])
        tmp = sb("tmp", [P, 2, CH * CH // 4 + CH])
        state, r, u2 = (sb(n, [P, BATCH, CH]) for n in ("state", "r", "u2"))
        at = lambda t, n: t.rearrange("p (b n i) -> p b n i", b=BATCH, n=CPS)[:, :, bass.ds(n, 1), :]\
            .rearrange("p b a i -> p b (a i)")
        src = {"kbT": r1, "kT": f["kT"][:], "qT": f["qT"][:], "kH": f["kH"][:], "U": r2, "attn": f["attn"][:]}

        def expand(copy, name, n):
            for h in range(DHEADS):
                p = slice(CH * h, CH * (h + 1))
                m = copy(bd[name][p, :, CH * h:CH * (h + 1)], at(src[name], n)[p])
            return m

        with nc.psum_tensor("ds_psA", [P, N], F32) as psA, nc.psum_tensor("ds_psB", [P, N], F32) as psB, \
                nc.Block() as block:
            @block.gpsimd
            def _(pool):
                for n in ("U", "attn", "kH"):
                    m = nc.gpsimd.memset(bd[n][:], 0.0)
                m.then_inc(cleared.sem, 1)
                pool.wait_ge(*cleared.at(1))
                for h in range(DHEADS):
                    p = slice(CH * h, CH * (h + 1))
                    nc.gpsimd.affine_select(out=strict[p, :], in_=k.ones[p, 0:CH], compare_op=ALU.is_ge, fill=0.0,
                                            base=-1, pattern=[[-1, CH]], channel_multiplier=1)
                    m = nc.gpsimd.affine_select(out=incl[p, :], in_=k.ones[p, 0:CH], compare_op=ALU.is_ge, fill=0.0,
                                                base=0, pattern=[[1, CH]], channel_multiplier=-1)
                m.then_inc(masked.sem, 1)

            @block.vector
            def _(dve):
                nc.vector.memset(bd["kbT"][:], 0.0)
                dve.drain()
                with dve.Fori(0, CPS) as n:
                    dve.wait_ge(*multiplied.at(n + 1))
                    expand(nc.vector.tensor_copy, "kbT", n).then_inc(blocked.sem, 1)
                dve.wait_ge(*masked.at(1))
                dve.wait_ge(*multiplied.at(CPS + 1))
                g = lambda t: t.rearrange("p (u j) -> p u j", j=CH)
                m3 = lambda t: t[:].unsqueeze(1).to_broadcast([P, UN, CH])
                nc.vector.tensor_tensor(g(r3), g(psA[:]), m3(strict), ALU.mult)
                nc.vector.tensor_tensor(g(f["attn"][:]), g(psB[:]), m3(incl), ALU.mult)
                dve.drain()
                nc.vector.transpose(r2.rearrange("p (g j i) -> p g j i", g=2, j=CH),
                                    r3.rearrange("p (g u j) -> p g j u", g=2, j=CH))
                Tm = f["sq"][:].rearrange("p (g i c) -> p g i c", g=2, i=CH)
                L = r2.rearrange("p (g j i) -> p g j i", g=2, j=CH)
                nc.vector.memset(f["sq"][:], 0.0)
                dve.drain()
                nc.vector.memset(f["sq"][:].rearrange("p (g x) -> p g x", g=2)[:, :, 0:CH * CH:CH + 1], 1.0)
                dve.drain()
                for j in range(CH - 1):
                    ni, nk = CH - 1 - j, j + 1
                    t = tmp[:, :, 0:ni * nk].rearrange("p g (i c) -> p g i c", c=nk)
                    nc.vector.tensor_tensor(t, L[:, :, j, j + 1:].unsqueeze(3).to_broadcast([P, 2, ni, nk]),
                                            Tm[:, :, j:j + 1, 0:nk].to_broadcast([P, 2, ni, nk]), ALU.mult)
                    dve.drain()
                    rows = Tm[:, :, j + 1:, 0:nk]
                    nc.vector.tensor_tensor(rows, rows, t, ALU.subtract)
                    dve.drain()
                nc.vector.transpose(r2.rearrange("p (g u i) -> p g i u", g=2, i=CH),
                                    f["sq"][:].rearrange("p (g i c) -> p g i c", g=2, i=CH))

            @block.scalar
            def _(act):
                nc.scalar.memzero(bd["kT"][:])
                act.drain()
                with act.Fori(0, CPS) as n:
                    act.wait_ge(*multiplied.at(n + 1))
                    expand(nc.scalar.copy, "kT", n).then_inc(opened.sem, 1)
                nc.scalar.memzero(bd["qT"][:])

            @block.tensor
            def _(pe):
                pe.sem_inc(multiplied.sem, 1)
                with pe.Fori(0, CPS) as n:
                    pe.wait_ge(*blocked.at(n + 1))
                    pe.wait_ge(*opened.at(n + 1))
                    for b in range(BATCH):
                        c = bass.ds(n * CH + b * SEQ, CH)
                        nc.tensor.matmul(psA[:, c], bd["kbT"][:, b, :], f["kT"][:, c], start=True, stop=True)
                        m = nc.tensor.matmul(psB[:, c], bd["kT"][:, b, :], f["qT"][:, c], start=True, stop=True)
                    m.then_inc(multiplied.sem, 1)

        opened_k, read, carried, less, solved, solved_out, out_done, out_copied, added = (
            k.tally(f"dt_{n}") for n in
            ("opened", "read", "carried", "less", "solved", "solved_out", "out_done", "out_copied", "added"))
        opened_d, opened_p = k.tally("dt_opened_d"), k.tally("dt_opened_p")
        with ExitStack() as pc:
            ps1, ps2, ps3, ps4 = (pc.enter_context(nc.psum_tensor(f"dt_ps{i}", [P, 512], F32)) for i in range(1, 5))
            block = pc.enter_context(nc.Block())
            b3 = lambda t: t[:, 0:BATCH * CH].rearrange("p (b c) -> p b c", c=CH)

            @block.gpsimd
            def _(pool):
                with pool.Fori(0, CPS) as n:
                    pool.wait_ge(*added.at(n + 1))
                    expand(nc.gpsimd.tensor_copy, "kH", n)
                    expand(nc.gpsimd.tensor_copy, "attn", n).then_inc(opened_p.sem, 1)

            @block.scalar
            def _(act):
                with act.Fori(0, CPS) as n:
                    act.wait_ge(*added.at(n + 1))
                    expand(nc.scalar.copy, "kbT", n).then_inc(opened_k.sem, 1)
                    expand(nc.scalar.copy, "qT", n).then_inc(opened_k.sem, 1)
                    act.wait_ge(*solved.at(n + 1))
                    nc.scalar.copy(u2[:], b3(ps2)).then_inc(solved_out.sem, 1)
                    act.wait_ge(*out_done.at(n + 1))
                    nc.scalar.copy(at(f["delta"][:], n), b3(ps3)).then_inc(out_copied.sem, 1)

            @block.tensor
            def _(pe):
                with pe.Fori(0, CPS) as n:
                    pe.wait_ge(*added.at(n + 1))
                    pe.wait_ge(*opened_k.at(2 * n + 1))
                    for b in range(BATCH):
                        m = nc.tensor.matmul(ps1[:, b * CH:(b + 1) * CH], bd["kbT"][:, b, :], state[:, b, :],
                                             start=True, stop=True)
                    m.then_inc(carried.sem, 1)
                    pe.wait_ge(*opened_k.at(2 * n + 2))
                    pe.wait_ge(*out_copied.at(n + 1))
                    for b in range(BATCH):
                        nc.tensor.matmul(ps3[:, b * CH:(b + 1) * CH], bd["qT"][:, b, :], state[:, b, :],
                                         start=(b == 0), stop=False, skip_group_check=True)
                    pe.wait_ge(*opened_d.at(n + 1))
                    pe.wait_ge(*less.at(n + 1))
                    for b in range(BATCH):
                        m = nc.tensor.matmul(ps2[:, b * CH:(b + 1) * CH], bd["U"][:, b, :], r[:, b, :],
                                             start=True, stop=True)
                    m.then_inc(solved.sem, 1)
                    pe.wait_ge(*opened_p.at(n + 1))
                    pe.wait_ge(*solved_out.at(n + 1))
                    for b in range(BATCH):
                        m = nc.tensor.matmul(ps4[:, b * CH:(b + 1) * CH], bd["kH"][:, b, :], u2[:, b, :],
                                             start=True, stop=True)
                    m.then_inc(read.sem, 1)
                    for b in range(BATCH):
                        m = nc.tensor.matmul(ps3[:, b * CH:(b + 1) * CH], bd["attn"][:, b, :], u2[:, b, :],
                                             start=False, stop=(b == BATCH - 1), skip_group_check=True)
                    m.then_inc(out_done.sem, 1)

            @block.vector
            def _(dve):
                nc.vector.memset(state[:], 0.0).then_inc(added.sem, 1)
                dve.sem_inc(out_copied.sem, 1)
                with dve.Fori(0, CPS) as n:
                    expand(nc.vector.tensor_copy, "U", n).then_inc(opened_d.sem, 1)
                    dve.wait_ge(*carried.at(n + 1))
                    nc.vector.tensor_tensor(r[:], at(f["vbH"][:], n), b3(ps1), ALU.subtract).then_inc(less.sem, 1)
                    dve.wait_ge(*read.at(n + 1))
                    dve.wait_ge(*out_done.at(n + 1))
                    nc.vector.tensor_tensor(state[:], state[:], b3(ps4), ALU.add).then_inc(added.sem, 1)


def delta_gate(k, f, w, cols, rows, small, r1, r2, r3):
    nc = k.nc
    H = lambda ap: ap.rearrange("p (u d) -> p u d", d=CH)
    with ExitStack() as s:
        sb = lambda n, shape: s.enter_context(nc.sbuf_tensor(f"dg_{n}", shape, F32))
        Z = sb("Z", [P, UN, CH])
        ss = sb("ss", [P, 4, UN])
        l2 = sb("l2", [P, 4, UN])
        su, t1 = sb("su", [P, UN]), sb("t1", [P, UN])
        lg, pr = sb("lg", [P, UN, 4]), sb("pr", [P, UN, 4])
        one = sb("one", [P, 4])
        og, fac = sb("og", [P, UN]), sb("fac", [P, UN])
        sqd, sumd, ask, rt, zt, hid, gel, lgt, lgc, ex, asko, cons = (
            k.tally(f"dg_{n}") for n in ("sqd", "sumd", "ask", "rt", "zt", "hid", "gel", "lgt", "lgc", "ex", "asko", "cons"))
        hpart = {"short": r2, "long": r3, "delta": f["delta"][:], "v": f["vH"][:]}
        ZT = f["qT"][:]
        G = f["kT"]
        o = f["qH"][:]
        tmp = f["kbH"][:]

        def stats(dve, x, n, col, squares):
            nc.vector.tensor_reduce(su[:], H(x), AX.X, ALU.add)
            nc.vector.tensor_reduce(t1[:], H(x), AX.X, ALU.add, apply_absolute_value=True)
            dve.wait_ge(*sqd.at(squares))
            nc.vector.tensor_reduce(ss[:, n, :], H(f["sq"][:]), AX.X, ALU.add).then_inc(sumd.sem, 1)
            dve.drain()
            nc.vector.tensor_scalar(Z[:, :, col], su[:], 1.0 / D, None, ALU.mult)
            nc.vector.tensor_scalar(Z[:, :, col + 2], t1[:], 1.0 / D, None, ALU.mult)
            nc.vector.tensor_tensor(su[:], su[:], su[:], ALU.mult)
            dve.drain()
            nc.vector.tensor_scalar(su[:], su[:], -1.0 / (D * CH), None, ALU.mult)
            dve.drain()
            m = nc.vector.scalar_tensor_tensor(out=Z[:, :, col + 1], in0=ss[:, n, :], scalar=1.0 / D, in1=su[:],
                                               op0=ALU.mult, op1=ALU.add)
            dve.drain()
            return m

        with nc.psum_tensor("dg_ps", [P, 4, 512], F32) as ps, nc.psum_tensor("dg_ps2", [P, 4, 512], F32) as ps2, \
                nc.Block() as block:
            @block.vector
            def _(dve):
                nc.vector.memset(Z[:], 0.0)
                nc.vector.transpose(r2, f["short"][:])
                nc.vector.transpose(r3, f["long"][:])
                dve.drain()
                for i, (n, j) in enumerate((("v", 3), ("delta", 2), ("short", 0), ("long", 1))):
                    m = stats(dve, hpart[n], j, 4 * j, i + 1)
                m.then_inc(ask.sem, 1)
                dve.wait_ge(*rt.at(1))
                for j in range(4):
                    m = nc.vector.tensor_scalar(Z[:, :, 4 * j + 3], l2[:, j, :], 1.0 / DHEADS, None, ALU.mult)
                dve.drain()
                nc.vector.transpose(ZT, Z[:].rearrange("p u s -> p (u s)")).then_inc(zt.sem, 1)
                dve.wait_ge(*lgc.at(1))
                nc.vector.transpose(o, tmp)
                dve.drain()
                dve.wait_ge(*cons.at(1))
                nc.vector.tensor_scalar(one[:, 2:3], rows[:, 4:5], 0.0, None, ALU.max)
                dve.drain()
                nc.vector.tensor_tensor(one[:, 2:3], one[:, 2:3], one[:, 1:2], ALU.add)
                dve.drain()
                nc.vector.reciprocal(one[:, 3:4], one[:, 2:3])
                nc.vector.tensor_tensor(lg[:], H(o)[:, :, 0:4], rows[:, 0:4].unsqueeze(1).to_broadcast([P, UN, 4]),
                                        ALU.add)
                dve.drain()
                nc.vector.tensor_scalar(lg[:], lg[:], one[:, 3:4], None, ALU.mult)
                dve.drain()
                nc.vector.tensor_reduce(su[:], lg[:], AX.X, ALU.max)
                dve.drain()
                b4 = lambda t: t[:].unsqueeze(2).to_broadcast([P, UN, 4])
                nc.vector.tensor_tensor(lg[:], lg[:], b4(su), ALU.subtract).then_inc(ask.sem, 1)
                dve.wait_ge(*rt.at(2))
                for i in range(2):
                    nc.vector.tensor_reduce(su[:], pr[:], AX.X, ALU.add)
                    dve.drain()
                    nc.vector.reciprocal(t1[:], su[:])
                    dve.drain()
                    nc.vector.tensor_tensor(pr[:], pr[:], b4(t1), ALU.mult)
                    dve.drain()
                    if i == 0:
                        nc.vector.tensor_scalar(pr[:], pr[:], FLOOR, None, ALU.max)
                        dve.drain()
                nc.vector.scalar_tensor_tensor(out=pr[:, :, 0], in0=small["res"][:], scalar=one[:, 0:1],
                                               in1=pr[:, :, 0], op0=ALU.mult, op1=ALU.add)
                dve.drain()
                b32 = lambda t: t.unsqueeze(2).to_broadcast([P, UN, CH])
                for j, n in enumerate(("short", "long", "delta", "v")):
                    dst = o if j == 0 else tmp
                    nc.vector.tensor_tensor(H(dst), H(hpart[n]), b32(pr[:, :, j]), ALU.mult)
                    dve.drain()
                    if j:
                        m = nc.vector.tensor_tensor(o, o, tmp, ALU.add)
                        dve.drain()
                m.then_inc(ask.sem, 1)
                stats(dve, o, 0, 0, 5).then_inc(ask.sem, 1)
                dve.wait_ge(*rt.at(3))
                nc.vector.tensor_scalar(Z[:, :, 3], l2[:, 0, :], 1.0 / DHEADS, None, ALU.mult)
                dve.drain()
                nc.vector.transpose(ZT, Z[:].rearrange("p u s -> p (u s)")).then_inc(zt.sem, 1)
                dve.wait_ge(*lgc.at(2))
                nc.vector.transpose(r2, tmp).then_inc(asko.sem, 1)
                dve.wait_ge(*rt.at(4))
                nc.vector.tensor_tensor(t1[:], og[:], og[:], ALU.mult)
                dve.drain()
                nc.vector.tensor_tensor(t1[:], t1[:], ss[:, 0, :], ALU.mult)
                dve.drain()
                nc.vector.tensor_scalar(t1[:], t1[:], 1.0 / CH, LN_EPS, ALU.mult, ALU.add).then_inc(asko.sem, 1)
                dve.wait_ge(*rt.at(5))
                inverse_root(nc, dve, fac[:], su[:], t1[:], l2[:, 1, :])
                nc.vector.tensor_tensor(fac[:], fac[:], og[:], ALU.mult)
                dve.drain()
                nc.vector.tensor_tensor(H(o), H(o), b32(fac[:]), ALU.mult)
                dve.drain()
                nc.vector.transpose(r1, o)
                nc.vector.tensor_scalar(w["Wo"][:], w["Wo"][:], cols[:, 2:3], None, ALU.mult)

            @block.scalar
            def _(act):
                nc.scalar.activation(one[:, 0:1], cols[:, 1:2], ACT.Sigmoid)
                nc.scalar.activation(one[:, 1:2], rows[:, 4:5], ACT.Abs)
                act.drain()
                nc.scalar.activation(one[:, 1:2], one[:, 1:2], ACT.Exp, scale=-1.0)
                act.drain()
                nc.scalar.activation(one[:, 1:2], one[:, 1:2], ACT.Ln, bias=k.ones[:, 0:1]).then_inc(cons.sem, 1)
                for i, n in enumerate(("v", "delta", "short", "long")):
                    if i:
                        act.wait_ge(*sumd.at(i))
                    nc.scalar.activation(f["sq"][:], hpart[n], ACT.Square).then_inc(sqd.sem, 1)
                act.wait_ge(*ask.at(1))
                nc.scalar.activation(l2[:], ss[:], ACT.Sqrt).then_inc(rt.sem, 1)
                for g in range(4):
                    act.wait_ge(*hid.at(g + 1))
                    nc.scalar.activation(G[:, g * 512:(g + 1) * 512], ps[:, g, :], ACT.Gelu, bias=cols[:, 3:4])\
                        .then_inc(gel.sem, 1)
                for g in range(4):
                    act.wait_ge(*lgt.at(g + 1))
                    m = nc.scalar.activation(tmp[:, g * 512:(g + 1) * 512], ps2[:, g, :], ACT.Copy)
                m.then_inc(lgc.sem, 1)
                act.wait_ge(*ask.at(2))
                nc.scalar.activation(pr[:], lg[:], ACT.Exp).then_inc(rt.sem, 1)
                act.wait_ge(*ask.at(3))
                nc.scalar.activation(f["sq"][:], o, ACT.Square).then_inc(sqd.sem, 1)
                act.wait_ge(*ask.at(4))
                nc.scalar.activation(l2[:, 0, :], ss[:, 0, :], ACT.Sqrt).then_inc(rt.sem, 1)
                for g in range(4):
                    act.wait_ge(*hid.at(4 + g + 1))
                    nc.scalar.activation(G[0:D // 2, g * 512:(g + 1) * 512], ps[0:D // 2, g, :], ACT.Gelu,
                                         bias=cols[0:D // 2, 4:5]).then_inc(gel.sem, 1)
                for g in range(4):
                    act.wait_ge(*lgt.at(4 + g + 1))
                    m = nc.scalar.activation(tmp[:, g * 512:(g + 1) * 512], ps2[:, g, :], ACT.Copy)
                m.then_inc(lgc.sem, 1)
                act.wait_ge(*asko.at(1))
                nc.scalar.activation(og[:], H(r2)[:, :, 0], ACT.Sigmoid, bias=cols[:, 5:6]).then_inc(rt.sem, 1)
                act.wait_ge(*asko.at(2))
                nc.scalar.activation(su[:], t1[:], ACT.Sqrt).then_inc(rt.sem, 1)

            @block.tensor
            def _(pe):
                for i, (wx, ws, w2, M) in enumerate((("Wg1x", "Wg1s", "Wg2", P), ("Wog1x", "Wog1s", "Wog2", D // 2))):
                    if i == 1:
                        pe.wait_ge(*lgc.at(1))
                    pe.wait_ge(*zt.at(i + 1))
                    for g in range(4):
                        c = slice(g * 512, (g + 1) * 512)
                        nc.tensor.matmul(ps[0:M, g, :], w[wx][:], k.XT[:, c], start=True, stop=False)
                        nc.tensor.matmul(ps[0:M, g, :], w[ws][:], ZT[:, c], start=False, stop=True)\
                            .then_inc(hid.sem, 1)
                    for g in range(4):
                        pe.wait_ge(*gel.at(4 * i + g + 1))
                        nc.tensor.matmul(ps2[:, g, :], w[w2][:], G[0:M, g * 512:(g + 1) * 512], start=True, stop=True)\
                            .then_inc(lgt.sem, 1)


def retention_stage(k, a):
    nc = k.nc
    w_in, consts, made, projected, scanned, turned, gated, asked, rooted, scaled, tail = (
        k.tally(f"re_{n}") for n in
        ("w_in", "consts", "made", "projected", "scanned", "turned", "gated", "asked", "rooted", "scaled", "tail"))
    with ExitStack() as s:
        sb = lambda n, shape: s.enter_context(nc.sbuf_tensor(f"re_{n}", shape, F32))
        w = {n: sb(n, [P, D]) for n in ("wq", "wv", "wg", "wo")}
        col = sb("col", [P, 3])
        lam = sb("lam", [P, 1])
        decay = sb("decay", [P, BATCH, SEQ])
        state, yT, gate, y2T = (sb(n, [P, N]) for n in ("state", "yT", "gate", "y2T"))
        Y = sb("Y", [P, T, D])
        stats, agg = sb("stats", [P, T, 6]), sb("agg", [P, T, 2])
        vare, root, rstd, scratch = (sb(n, [P, T]) for n in ("vare", "root", "rstd", "scratch"))
        with nc.psum_tensor("re_psQ", [P, N], F32) as psQ, nc.psum_tensor("re_psV", [P, N], F32) as psV, \
                nc.Block() as block:
            @block.sync
            def _(sp):
                sp.dma_start(col[:], a["L2_attn_cols"]).then_inc(consts.sem, 16)
                for n in ("wv", "wq", "wg", "wo"):
                    sp.dma_start(w[n][:], a[f"L2_attn_{n}"]).then_inc(w_in.sem, 16)
                sp.wait_ge(*w_in.at(64))

            @block.tensor
            def _(pe):
                pe.wait_ge(*w_in.at(64))
                for n, ps in (("wv", psV), ("wq", psQ)):
                    for g in range(4):
                        m = nc.tensor.matmul(ps[:, g * 512:(g + 1) * 512], w[n][:], k.XT[:, g * 512:(g + 1) * 512],
                                             start=True, stop=True)
                    m.then_inc(projected.sem, 1)

            @block.scalar
            def _(act):
                act.wait_ge(*consts.at(16))
                nc.scalar.activation(lam[:], col[:, 0:1], ACT.Sigmoid).then_inc(made.sem, 1)

            @block.vector
            def _(dve):
                nc.vector.memset(decay[:], 1.0)
                dve.wait_ge(*made.at(1))
                dve.drain()
                nc.vector.tensor_scalar(decay[:], decay[:], lam[:, 0:1], None, ALU.mult)
                dve.drain()
                nc.vector.memset(decay[:, :, 0:1], 0.0)
                dve.drain()
                dve.wait_ge(*projected.at(1))
                nc.vector.tensor_tensor_scan(state[:], decay[:].rearrange("p b s -> p (b s)"), psV[:], 0.0,
                                             ALU.mult, ALU.add)
                dve.drain()
                dve.wait_ge(*projected.at(2))
                nc.vector.tensor_tensor(yT[:], psQ[:], state[:], ALU.mult)

        with nc.psum_tensor("re_psY", [P, T, D], F32) as psY, nc.psum_tensor("re_psG", [P, 4, 512], F32) as psG, \
                nc.Block() as block:
            @block.tensor
            def _(pe):
                for t in range(T):
                    m = nc.tensor.transpose(psY[:, t, :], yT[:, t * P:(t + 1) * P], k.ident[:])
                    if t % 4 == 3:
                        m.then_inc(turned.sem, 1)
                for g in range(4):
                    nc.tensor.matmul(psG[:, g, :], w["wg"][:], k.XT[:, g * 512:(g + 1) * 512], start=True, stop=True)\
                        .then_inc(gated.sem, 1)

            @block.scalar
            def _(act):
                act.wait_ge(*asked.at(1))
                nc.scalar.activation(root[:], vare[:], ACT.Sqrt).then_inc(rooted.sem, 1)
                for g in range(4):
                    act.wait_ge(*gated.at(g + 1))
                    nc.scalar.activation(gate[:, g * 512:(g + 1) * 512], psG[:, g, :], ACT.Silu)

            @block.vector
            def _(dve):
                for t in range(T):
                    if t % 4 == 0:
                        dve.wait_ge(*turned.at(t // 4 + 1))
                    nc.vector.bn_stats(stats[:, t, :], psY[:, t, :])
                dve.drain()
                for t in range(T):
                    nc.vector.bn_aggr(agg[:, t, :], stats[:, t, :])
                dve.drain()
                nc.vector.tensor_scalar(vare[:], agg[:, :, 1], LN_EPS, None, ALU.add).then_inc(asked.sem, 1)
                dve.wait_ge(*rooted.at(1))
                inverse_root(nc, dve, rstd[:], root[:], vare[:], scratch[:])
                for t in range(T):
                    nc.vector.tensor_scalar(Y[:, t, :], psY[:, t, :], agg[:, t, 0:1], rstd[:, t:t + 1],
                                            ALU.subtract, ALU.mult)

        with nc.psum_tensor("re_psN", [P, 4, 512], F32) as psN, nc.Block() as block:
            @block.tensor
            def _(pe):
                for g in range(4):
                    for j in range(4):
                        m = nc.tensor.transpose(psN[:, g, j * P:(j + 1) * P], Y[:, 4 * g + j, :], k.ident[:])
                    m.then_inc(tail.sem, 1)

            @block.scalar
            def _(act):
                for g in range(4):
                    act.wait_ge(*tail.at(g + 1))
                    nc.scalar.activation(y2T[:, g * 512:(g + 1) * 512], psN[:, g, :], ACT.Identity,
                                         scale=col[:, 1:2], bias=col[:, 2:3]).then_inc(scaled.sem, 1)

            @block.vector
            def _(dve):
                for g in range(4):
                    dve.wait_ge(*scaled.at(g + 1))
                    c = slice(g * 512, (g + 1) * 512)
                    nc.vector.tensor_tensor(y2T[:, c], y2T[:, c], gate[:, c], ALU.mult)
        project_and_add_stage(k, "re", None, y2T, w["wo"])


def lru_stage(k, a):
    nc = k.nc
    w_in, iotad, exped, prepared, sined, halved, projected, scaled, rotated, out_done = (
        k.tally(f"lr_{n}") for n in
        ("w_in", "iotad", "exped", "prepared", "sined", "halved", "projected", "scaled", "rotated", "out_done"))
    TURN_HI, TURN_LO = 6.28125, float(2 * np.pi - 6.28125)
    with ExitStack() as s:
        sb = lambda n, shape: s.enter_context(nc.sbuf_tensor(f"lr_{n}", shape, F32))
        w = {n: sb(n, [P, D]) for n in ("Br", "Bi", "Cr", "Ci")}
        col = sb("col", [P, 3])
        nu, th, mag, mag2, gamma, g1 = (sb(n, [P, 1]) for n in ("nu", "th", "mag", "mag2", "gamma", "g1"))
        time, angle, turns, sin, half, cos = (sb(n, [P, SEQ]) for n in ("time", "angle", "turns", "sin", "half", "cos"))
        diag = sb("diag", [P, D])
        decay, br, bi, m1, m2, hr, hi = (sb(n, [P, BATCH, SEQ]) for n in ("decay", "br", "bi", "m1", "m2", "hr", "hi"))
        gr, gi = sb("gr", [P, BATCH, SEQ]), sb("gi", [P, BATCH, SEQ])
        all_seqs = lambda t: t[:].unsqueeze(1).to_broadcast([P, BATCH, SEQ])
        flat = lambda t: t[:].rearrange("p b s -> p (b s)")
        with nc.psum_tensor("lr_psR", [P, N], F32) as psR, nc.psum_tensor("lr_psI", [P, N], F32) as psI, \
                nc.Block() as block:
            @block.sync
            def _(sp):
                sp.dma_start(col[:], a["L3_attn_cols"]).then_inc(w_in.sem, 16)
                for n in w:
                    sp.dma_start(w[n][:], a[f"L3_attn_{n}"]).then_inc(w_in.sem, 16)

            @block.gpsimd
            def _(pool):
                nc.gpsimd.iota(time[:], [[1, SEQ]], base=0, channel_multiplier=0,
                               allow_small_or_imprecise_dtypes=True).then_inc(iotad.sem, 1)

            @block.tensor
            def _(pe):
                pe.wait_ge(*w_in.at(80))
                for n, ps in (("Br", psR), ("Bi", psI)):
                    for g in range(4):
                        m = nc.tensor.matmul(ps[:, g * 512:(g + 1) * 512], w[n][:], k.XT[:, g * 512:(g + 1) * 512],
                                             start=True, stop=True)
                    m.then_inc(projected.sem, 1)

            @block.scalar
            def _(act):
                act.wait_ge(*w_in.at(80))
                nc.scalar.activation(nu[:], col[:, 0:1], ACT.Exp)
                nc.scalar.activation(th[:], col[:, 1:2], ACT.Exp)
                act.drain()
                nc.scalar.activation(mag[:], nu[:], ACT.Exp, scale=-1.0)
                nc.scalar.activation(mag2[:], nu[:], ACT.Exp, scale=-2.0).then_inc(exped.sem, 1)
                act.wait_ge(*prepared.at(1))
                nc.scalar.activation(gamma[:], g1[:], ACT.Sqrt)
                act.drain()
                act.wait_ge(*projected.at(1))
                nc.scalar.activation(flat(br), psR[:], ACT.Copy, scale=gamma[:, 0:1])
                act.wait_ge(*projected.at(2))
                nc.scalar.activation(flat(bi), psI[:], ACT.Copy, scale=gamma[:, 0:1]).then_inc(scaled.sem, 1)
                act.wait_ge(*prepared.at(2))
                nc.scalar.activation(sin[:], angle[:], ACT.Sin)
                nc.scalar.activation(half[:], angle[:], ACT.Sin, scale=0.5).then_inc(sined.sem, 1)

            @block.vector
            def _(dve):
                dve.wait_ge(*exped.at(1))
                nc.vector.tensor_scalar(g1[:], mag2[:], -1.0, 1.0, ALU.mult, ALU.add)
                dve.drain()
                nc.vector.tensor_scalar(g1[:], g1[:], LN_EPS, None, ALU.add).then_inc(prepared.sem, 1)
                dve.wait_ge(*iotad.at(1))
                nc.vector.tensor_scalar(angle[:], time[:], th[:, 0:1], None, ALU.mult)
                dve.drain()
                nc.vector.tensor_scalar(turns[:], angle[:], float(1 / (2 * np.pi)), ROUND, ALU.mult, ALU.add)
                dve.drain()
                nc.vector.tensor_scalar(turns[:], turns[:], -ROUND, None, ALU.add)
                dve.drain()
                nc.vector.scalar_tensor_tensor(out=angle[:], in0=turns[:], scalar=-TURN_HI, in1=angle[:],
                                               op0=ALU.mult, op1=ALU.add)
                dve.drain()
                nc.vector.scalar_tensor_tensor(out=angle[:], in0=turns[:], scalar=-TURN_LO, in1=angle[:],
                                               op0=ALU.mult, op1=ALU.add)
                dve.drain()
                nc.vector.tensor_scalar(angle[:], angle[:], 3.1415925, -3.1415925, ALU.min, ALU.max)\
                    .then_inc(prepared.sem, 1)
                nc.vector.memset(decay[:], 1.0)
                dve.drain()
                nc.vector.tensor_scalar(decay[:], decay[:], mag[:, 0:1], None, ALU.mult)
                dve.drain()
                nc.vector.memset(decay[:, :, 0:1], 0.0)
                dve.wait_ge(*w_in.at(80))
                nc.vector.tensor_scalar(diag[:], k.ident[:], col[:, 2:3], None, ALU.mult)
                nc.vector.tensor_scalar(w["Ci"][:], w["Ci"][:], -1.0, None, ALU.mult)
                dve.wait_ge(*sined.at(1))
                nc.vector.tensor_tensor(cos[:], half[:], half[:], ALU.mult)
                dve.drain()
                nc.vector.tensor_scalar(cos[:], cos[:], -2.0, 1.0, ALU.mult, ALU.add)
                dve.drain()
                dve.wait_ge(*scaled.at(1))
                C, S = all_seqs(cos), all_seqs(sin)
                nc.vector.tensor_tensor(gr[:], br[:], C, ALU.mult)
                nc.vector.tensor_tensor(m1[:], bi[:], S, ALU.mult)
                nc.vector.tensor_tensor(gi[:], bi[:], C, ALU.mult)
                nc.vector.tensor_tensor(m2[:], br[:], S, ALU.mult)
                dve.drain()
                nc.vector.tensor_tensor(gr[:], gr[:], m1[:], ALU.add)
                nc.vector.tensor_tensor(gi[:], gi[:], m2[:], ALU.subtract)
                dve.drain()
                nc.vector.tensor_tensor_scan(flat(br), flat(decay), flat(gr), 0.0, ALU.mult, ALU.add)
                nc.vector.tensor_tensor_scan(flat(bi), flat(decay), flat(gi), 0.0, ALU.mult, ALU.add)
                dve.drain()
                nc.vector.tensor_tensor(hr[:], br[:], C, ALU.mult)
                nc.vector.tensor_tensor(m1[:], bi[:], S, ALU.mult)
                nc.vector.tensor_tensor(hi[:], br[:], S, ALU.mult)
                nc.vector.tensor_tensor(m2[:], bi[:], C, ALU.mult)
                dve.drain()
                nc.vector.tensor_tensor(hr[:], hr[:], m1[:], ALU.subtract)
                nc.vector.tensor_tensor(hi[:], hi[:], m2[:], ALU.add)

        with nc.psum_tensor("lr_psO", [P, 4, 512], F32) as psO, nc.Block() as block:
            @block.tensor
            def _(pe):
                for g in range(4):
                    for j in range(4):
                        t = 4 * g + j
                        o, c = psO[:, g, j * P:(j + 1) * P], slice(t * P, (t + 1) * P)
                        nc.tensor.matmul(o, flat(hr)[:, c], w["Cr"][:], start=True, stop=False)
                        nc.tensor.matmul(o, flat(hi)[:, c], w["Ci"][:], start=False, stop=False)
                        m = nc.tensor.matmul(o, k.XT[:, c], diag[:], start=False, stop=True)
                    m.then_inc(out_done.sem, 1)

            @block.vector
            def _(dve):
                for g in range(4):
                    dve.wait_ge(*out_done.at(g + 1))
                    x = k.X[:, 4 * g:4 * g + 4, :]
                    nc.vector.tensor_tensor(x, x, psO[:, g, :].rearrange("p (t d) -> p t d", d=D), ALU.add)


def store_stage(k, out):
    nc = k.nc
    stored = k.tally("stored")
    with nc.Block() as block:
        @block.sync
        def _(sp):
            sp.dma_start(out.rearrange("b (t p) d -> p (b t) d", p=P), k.X[:]).then_inc(stored.sem, 16)
            sp.wait_ge(*stored.at(16))


def program(nc, a, out, upto=8, start=0):
    with ExitStack() as ctx:
        k = Core(nc, ctx)
        setup_stage(k, a["L0_attn_x"])
        stages = [
            lambda: attention_stage(k, a["L0_attn_W_Q"], a["L0_attn_W_K"], a["L0_attn_W_V"], a["L0_attn_W_O"]),
            lambda: moe_l0_stage(k, a),
            lambda: delta_stage(k, a),
            lambda: moe_l1_stage(k, a),
            lambda: retention_stage(k, a),
            lambda: moe_l2_stage(k, a),
            lambda: lru_stage(k, a),
            lambda: moe_l3_stage(k, a),
        ]
        for n in range(start, upto):
            if n == max(start, 6) and upto == 8:
                load_l3_weights(k, a)
            stages[n]()
            layernorm_stage(k, f"ln{n}", turn=n < 7)
        store_stage(k, out)


def lay_out(v):
    r = {}
    r["L0_attn_x"] = v["L0_attn_x"]
    for n in "QKVO":
        r[f"L0_attn_W_{n}"] = v[f"L0_attn_W_{n}"].T
    cat = lambda *x: np.concatenate(x, axis=2)
    E, F = v["L0_ffn_b1"].shape
    cols = lambda b: b.reshape(E, F // P, P).transpose(0, 2, 1)
    down = lambda w: w.reshape(w.shape[0], -1, P, D).transpose(0, 2, 1, 3).reshape(w.shape[0], P, -1)
    r["L0_ffn_router"] = v["L0_ffn_Wg"].T
    r["L0_ffn_up"] = cat(v["L0_ffn_W1"].transpose(0, 2, 1), v["L0_ffn_W2"].transpose(0, 2, 1),
                         cols(v["L0_ffn_b1"]), cols(v["L0_ffn_b2"]))
    r["L0_ffn_down"] = down(v["L0_ffn_W3"].transpose(0, 2, 1))
    r["L0_ffn_b3"] = v["L0_ffn_b3"]
    for n in "qkvo":
        r[f"L1_attn_W{n}"] = v[f"L1_attn_W{n}"]
    r["L1_attn_taps"] = np.concatenate(
        [v["L1_attn_wq_conv"], v["L1_attn_wk_conv"], v["L1_attn_wv_conv"], v["L1_attn_fir_short"].reshape(D, -1),
         v["L1_attn_fir_long"].reshape(D, -1)], axis=1)

    def spread(rows, columns):
        out = np.zeros((rows, DHEADS, CH), np.float32)
        for s, c in columns.items():
            out[:, :, s] = c if c.ndim == 2 else c[:, None]
        return out.reshape(rows, D)

    wg1, wg2, wog1, wog2 = (v[f"L1_attn_{n}"] for n in ("Wg1", "Wg2", "Wog1", "Wog2"))
    r["L1_attn_Wxg"] = spread(D, {0: v["L1_attn_Wb"], 1: v["L1_attn_Wres"]})
    r["L1_attn_Wg1x"], r["L1_attn_Wog1x"] = wg1[:D], wog1[:D]
    r["L1_attn_Wg1s"] = spread(D, {i: wg1[D + i] for i in range(16)}).T
    r["L1_attn_Wog1s"] = spread(D // 2, {(i if i < 4 else 8 + i): wog1[D + i] for i in range(8)}).T
    r["L1_attn_Wg2"] = spread(D, {i: wg2[:, i] for i in range(4)})
    r["L1_attn_Wog2"] = spread(D // 2, {0: wog2[:, 0]})
    r["L1_attn_cols"] = np.stack(
        [np.repeat(v["L1_attn_bres"], CH), np.repeat(v["L1_attn_conv_res_logit"], CH),
         np.tile(v["L1_attn_norm_w"], DHEADS), v["L1_attn_bg1"],
         np.concatenate([v["L1_attn_bog1"], np.zeros(D // 2, np.float32)]), np.repeat(v["L1_attn_bog2"], D)], axis=1)
    r["L1_attn_rows"] = np.concatenate([v["L1_attn_bg2"], v["L1_attn_logit_temp"]])
    r["L1_ffn_router"] = v["L1_ffn_router_w"].T
    r["L1_ffn_router_bias"] = v["L1_ffn_router_bias"]
    halves = lambda w: w.T.reshape(D, 2, -1).transpose(1, 0, 2)
    r["L1_ffn_up"] = np.concatenate([cat(v["L1_ffn_gate_proj"], v["L1_ffn_up_proj"]),
                                     cat(halves(v["L1_ffn_sh_gate"]), halves(v["L1_ffn_sh_up"]))])
    r["L1_ffn_down"] = np.concatenate([v["L1_ffn_down_proj"], v["L1_ffn_sh_down"].T.reshape(2, -1, D)])
    r["L2_ffn_router"] = v["L2_ffn_router_w"].T
    r["L2_ffn_up"] = np.concatenate([cat(v["L2_ffn_w_gate"], v["L2_ffn_w_up"]), v["L2_ffn_ws_gate_up"][None]])
    r["L2_ffn_down"] = np.concatenate([v["L2_ffn_w_down"], v["L2_ffn_ws_down"][None]])
    c = lambda *x: np.stack(x, axis=1)
    r["L2_attn_cols"] = c(np.repeat(v["L2_attn_beta"], HD), v["L2_attn_ln_gamma"], v["L2_attn_ln_beta"])
    for n in "qvgo":
        r[f"L2_attn_w{n}"] = v[f"L2_attn_W{n}"].T
    r["L3_attn_cols"] = c(v["L3_attn_nu_log"], v["L3_attn_theta_log"], v["L3_attn_D_skip"])
    for n, m in (("Br", "B_re"), ("Bi", "B_im"), ("Cr", "C_re"), ("Ci", "C_im")):
        r[f"L3_attn_{n}"] = v[f"L3_attn_{m}"].T
    r["L3_ffn_routers"] = v["L3_ffn_routers"]
    r["L3_ffn_up"] = v["L3_ffn_W1"]
    r["L3_ffn_down"] = down(v["L3_ffn_W2"])
    return r


def kernel(**inputs):
    import concourse.bacc as bacc
    from concourse.bass_utils import run_bass_kernel_spmd

    laid = {n: np.ascontiguousarray(x) for n, x in lay_out({n: np.asarray(x) for n, x in inputs.items()}).items()}
    nc = bacc.Bacc("TRN2", target_bir_lowering=False, num_devices=1)
    aps = {n: nc.dram_tensor(f"in_{n}", x.shape, mybir.dt.from_np(x.dtype), kind="ExternalInput").ap()
           for n, x in laid.items()}
    out = nc.dram_tensor("out", (BATCH, SEQ, D), F32, kind="ExternalOutput").ap()
    program(nc, aps, out)
    r = run_bass_kernel_spmd(nc, [{f"in_{n}": x for n, x in laid.items()}], core_ids=[0])
    return r.results[0]["out"]
```

```python
from contextlib import ExitStack

import numpy as np
import concourse.bass as bass
from concourse import mybir

F32, F16, BF16 = mybir.dt.float32, mybir.dt.float16, mybir.dt.bfloat16
ALU = mybir.AluOpType
ACT = mybir.ActivationFunctionType
AX = mybir.AxisListType

P = 128
D = 128
BATCH = 8
SEQ = 256
N = BATCH * SEQ
T = N // P
NBLK = N // 512
LN_EPS = 1e-5
MASKED = -1e30


class Tally:

    def __init__(self, sem):
        self.sem, self.before = sem, 0

    def at(self, n):
        return self.sem, n + self.before

    def close(self, total):
        self.before += total


class Core:

    def __init__(self, nc, ctx):
        self.nc, self.ctx, self.tallies = nc, ctx, {}
        self.X = self.keep("X", [P, T, D])
        self.XT = self.keep("XT", [P, N])
        self.ident = self.keep("ident", [P, P])
        self.ones = self.keep("ones", [P, P])

    def keep(self, name, shape, dt=F32):
        return self.ctx.enter_context(self.nc.sbuf_tensor(name, shape, dt))

    def open_logits(self, name, experts):
        self.logits_room = ExitStack()
        self.logits = self.logits_room.enter_context(self.nc.psum_tensor(name, [P, T, experts], F32))

    def close_logits(self):
        self.logits_room.close()

    def tally(self, name):
        if name not in self.tallies:
            self.tallies[name] = Tally(self.ctx.enter_context(self.nc.semaphore(name)))
        return self.tallies[name]


def setup_stage(k, x_in):
    nc = k.nc
    loaded, made, turned, copied = (k.tally(n) for n in ("loaded", "made", "ln_turned", "ln_copied"))
    with nc.psum_tensor("ps_setup", [P, 4, 512], F32) as ps, nc.Block() as block:
        @block.sync
        def _(sp):
            sp.dma_start(k.X[:], x_in.rearrange("b (t p) d -> p (b t) d", p=P)).then_inc(loaded.sem, 16)

        @block.gpsimd
        def _(pool):
            nc.gpsimd.memset(k.ident[:], 0.0).then_inc(made.sem, 1)
            pool.wait_ge(*made.at(1))
            nc.gpsimd.affine_select(out=k.ident[:], in_=k.ident[:], compare_op=ALU.not_equal, fill=1.0,
                                    base=0, pattern=[[-1, P]], channel_multiplier=1).then_inc(made.sem, 1)
            nc.gpsimd.memset(k.ones[:], 1.0).then_inc(made.sem, 1)
            pool.wait_ge(*made.at(3))

        @block.tensor
        def _(pe):
            pe.wait_ge(*loaded.at(16))
            pe.wait_ge(*made.at(2))
            for g in range(4):
                for j in range(4):
                    t = nc.tensor.transpose(ps[:, g, j * P:(j + 1) * P], k.X[:, 4 * g + j, :], k.ident[:])
                t.then_inc(turned.sem, 1)

        @block.scalar
        def _(act):
            for g in range(4):
                act.wait_ge(*turned.at(g + 1))
                nc.scalar.activation(k.XT[:, g * 512:(g + 1) * 512], ps[:, g, :], ACT.Copy).then_inc(copied.sem, 1)
    loaded.close(16)
    made.close(3)
    turned.close(4)
    copied.close(4)


def layernorm_stage(k, name, turn=True, router=None):
    nc = k.nc
    w_in = k.tally("ln_w_in")
    asked, rooted, scaled, turned, copied = (
        k.tally(n) for n in ("ln_asked", "ln_rooted", "ln_scaled", "ln_turned", "ln_copied"))
    with ExitStack() as s:
        stats = s.enter_context(nc.sbuf_tensor(f"{name}_stats", [P, T, 6], F32))
        agg = s.enter_context(nc.sbuf_tensor(f"{name}_agg", [P, T, 2], F32))
        vare = s.enter_context(nc.sbuf_tensor(f"{name}_vare", [P, T], F32))
        root = s.enter_context(nc.sbuf_tensor(f"{name}_root", [P, T], F32))
        rstd = s.enter_context(nc.sbuf_tensor(f"{name}_rstd", [P, T], F32))
        t0 = s.enter_context(nc.sbuf_tensor(f"{name}_t0", [P, T], F32))
        ps = s.enter_context(nc.psum_tensor(f"{name}_ps", [P, 4, 512], F32))
        if router is not None:
            wr = s.enter_context(nc.sbuf_tensor(f"{name}_wr", list(router.shape), F32))
        block = s.enter_context(nc.Block())

        @block.sync
        def _(sp):
            if router is not None:
                sp.dma_start(wr[:], router).then_inc(w_in.sem, 16)

        @block.vector
        def _(dve):
            for t in range(T):
                nc.vector.bn_stats(stats[:, t, :], k.X[:, t, :])
            dve.drain()
            for t in range(T):
                nc.vector.bn_aggr(agg[:, t, :], stats[:, t, :])
            dve.drain()
            nc.vector.tensor_scalar(vare[:], agg[:, :, 1], LN_EPS, None, ALU.add).then_inc(asked.sem, 1)
            dve.wait_ge(*rooted.at(1))
            inverse_root(nc, dve, rstd[:], root[:], vare[:], t0[:])
            for t in range(T):
                ins = nc.vector.tensor_scalar(k.X[:, t, :], k.X[:, t, :], agg[:, t, 0:1], rstd[:, t:t + 1],
                                              ALU.subtract, ALU.mult)
                if t % 4 == 3:
                    ins.then_inc(scaled.sem, 1)

        @block.scalar
        def _(act):
            act.wait_ge(*asked.at(1))
            nc.scalar.activation(root[:], vare[:], ACT.Sqrt).then_inc(rooted.sem, 1)
            if turn:
                for g in range(4):
                    act.wait_ge(*turned.at(g + 1))
                    nc.scalar.activation(k.XT[:, g * 512:(g + 1) * 512], ps[:, g, :], ACT.Copy)\
                        .then_inc(copied.sem, 1)

        if turn:
            @block.tensor
            def _(pe):
                def route(g):
                    pe.wait_ge(*copied.at(g + 1))
                    for t in range(4 * g, 4 * g + 4):
                        nc.tensor.matmul(k.logits[:, t, :], k.XT[:, t * P:(t + 1) * P], wr[:], start=True, stop=True)

                for g in range(4):
                    pe.wait_ge(*scaled.at(g + 1))
                    for j in range(4):
                        t = nc.tensor.transpose(ps[:, g, j * P:(j + 1) * P], k.X[:, 4 * g + j, :], k.ident[:])
                    t.then_inc(turned.sem, 1)
                    if router is not None:
                        if g == 0:
                            pe.wait_ge(*w_in.at(16))
                        else:
                            route(g - 1)
                if router is not None:
                    route(3)
    asked.close(1)
    rooted.close(1)
    scaled.close(4)
    if turn:
        turned.close(4)
        copied.close(4)
    if router is not None:
        w_in.close(16)


HEADS = 16
HD = D // HEADS


def attention_stage(k, w_q, w_k, w_v, w_o):
    nc = k.nc
    KC = SEQ // P
    RING = 4
    SC = P + SEQ
    slopes = (np.float32(1.0) / np.power(np.float32(256.0), (np.arange(HEADS, dtype=np.float32) + 1) / HEADS)).astype(np.float32)
    with ExitStack() as s:
        sb = lambda n, shape: s.enter_context(nc.sbuf_tensor(f"at_{n}", shape, F32))
        wq, wk, wv, wo = (sb(n, [P, D]) for n in ("wq", "wk", "wv", "wo"))
        QT, KT = sb("QT", [P, N]), sb("KT", [P, N])
        V = sb("V", [P, T, D])
        rel = sb("rel", [P, SEQ])
        bias = sb("bias", [P, HEADS, SEQ])
        hmask = sb("hmask", [P, HEADS])
        qm = sb("qm", [P, HEADS, SEQ])
        S = sb("S", [P, RING, SC])
        nmax = sb("nmax", [P, 2, HEADS, KC])
        rsum = sb("rsum", [P, 2, HEADS, KC])
        rinv = sb("rinv", [P, 2, HEADS, KC])
        Pr = sb("Pr", [P, RING, SC])
        PT = sb("PT", [P, 2, SC])
        O = sb("O", [P, T, D])
        OT = sb("OT", [P, N])
        sem = lambda n: k.tally(f"at_{n}")
        w_in, biased, masked, projected, proj_out, v_out = map(sem, ("w_in", "biased", "masked", "projected", "proj_out", "v_out"))
        psA_cm = nc.psum_tensor("at_psA", [P, 8, 512], F32)
        with psA_cm as psA, nc.Block() as block:
            @block.sync
            def _(sp):
                for t, w in ((wq, w_q), (wk, w_k), (wv, w_v), (wo, w_o)):
                    sp.dma_start(t[:], w).then_inc(w_in.sem, 16)

            @block.gpsimd
            def _(pool):
                nc.gpsimd.iota(rel[:], [[1, SEQ]], base=-P, channel_multiplier=-1,
                               allow_small_or_imprecise_dtypes=True).then_inc(biased.sem, 1)
                nc.gpsimd.memset(hmask[:], 1.0).then_inc(masked.sem, 1)
                pool.wait_ge(*masked.at(1))
                nc.gpsimd.affine_select(out=hmask[:], in_=hmask[:], compare_op=ALU.is_ge, fill=0.0, base=0,
                                        pattern=[[-HD, HEADS]], channel_multiplier=1).then_inc(masked.sem, 1)
                pool.wait_ge(*masked.at(2))
                nc.gpsimd.affine_select(out=hmask[:], in_=hmask[:], compare_op=ALU.is_ge, fill=0.0, base=HD - 1,
                                        pattern=[[HD, HEADS]], channel_multiplier=-1).then_inc(masked.sem, 1)
                pool.wait_ge(*biased.at(2))
                nc.gpsimd.affine_select(out=bias[:], in_=bias[:], compare_op=ALU.is_ge, fill=MASKED, base=P,
                                        pattern=[[0, HEADS], [-1, SEQ]], channel_multiplier=1)\
                    .then_inc(biased.sem, 1)

            @block.tensor
            def _(pe):
                pe.wait_ge(*w_in.at(64))
                for g in range(4):
                    nc.tensor.matmul(psA[:, g, :], wq[:], k.XT[:, g * 512:(g + 1) * 512], start=True, stop=True)\
                        .then_inc(projected.sem, 1)
                    nc.tensor.matmul(psA[:, 4 + g, :], wk[:], k.XT[:, g * 512:(g + 1) * 512], start=True, stop=True)\
                        .then_inc(projected.sem, 1)
                for g in range(4):
                    pe.wait_ge(*proj_out.at(g + 1))
                    for j in range(4):
                        t = 4 * g + j
                        m = nc.tensor.matmul(psA[:, g, j * P:(j + 1) * P], k.XT[:, t * P:(t + 1) * P], wv[:],
                                             start=True, stop=True)
                    m.then_inc(projected.sem, 1)

            @block.scalar
            def _(act):
                for g in range(4):
                    act.wait_ge(*projected.at(2 * g + 1))
                    nc.scalar.activation(QT[:, g * 512:(g + 1) * 512], psA[:, g, :], ACT.Copy,
                                         scale=float(1.0 / np.sqrt(np.float32(HD)))).then_inc(proj_out.sem, 1)
                for g in range(4):
                    act.wait_ge(*projected.at(8 + g + 1))
                    nc.scalar.activation(V[:, 4 * g:4 * g + 4, :], psA[:, g, :].rearrange("p (t d) -> p t d", d=D),
                                         ACT.Copy).then_inc(v_out.sem, 1)

            @block.vector
            def _(dve):
                dve.wait_ge(*biased.at(1))
                for h in range(HEADS):
                    m = nc.vector.tensor_scalar(bias[:, h, :], rel[:], float(slopes[h]), None, ALU.mult)
                m.then_inc(biased.sem, 1)
                for g in range(4):
                    dve.wait_ge(*projected.at(2 * g + 2))
                    nc.vector.tensor_copy(KT[:, g * 512:(g + 1) * 512], psA[:, 4 + g, :])

        scored, biasd, expd, turned, tcopied, weighted, normed, qmasked, begun, groups_begun = map(
            sem, ("scored", "biasd", "expd", "turned", "tcopied", "weighted", "normed", "qmasked", "begun",
                  "groups_begun"))
        QG = 4
        PAIR = 2 * HEADS
        NG = HEADS // QG
        with ExitStack() as ps_ctx:
            psS = [ps_ctx.enter_context(nc.psum_tensor(f"at_psS{i}", [P, 512], F32)) for i in range(RING)]
            psT = [ps_ctx.enter_context(nc.psum_tensor(f"at_psT{i}", [P, 512], F32)) for i in range(2)]
            psO = [ps_ctx.enter_context(nc.psum_tensor(f"at_psO{i}", [P, 512], F32)) for i in range(2)]
            block = ps_ctx.enter_context(nc.Block())

            @block.gpsimd
            def _(pool):
                with pool.Fori(0, BATCH) as b:
                    for g in range(NG):
                        pool.wait_ge(scored.sem, HEADS * b + (g + 1) * QG)
                        pool.sem_inc(groups_begun.sem, 1)
                        nc.gpsimd.tensor_tensor(
                            qm[:, g * QG:(g + 1) * QG, :],
                            QT[:, bass.ds(b * SEQ, SEQ)].unsqueeze(1).to_broadcast([P, QG, SEQ]),
                            hmask[:, g * QG:(g + 1) * QG].unsqueeze(2).to_broadcast([P, QG, SEQ]),
                            ALU.mult).then_inc(qmasked.sem, 1)

            @block.tensor
            def _(pe):
                pe.sem_inc(scored.sem, HEADS)
                with pe.Fori(0, BATCH // 2) as pair:
                    def scores(h):
                        if h % QG == 0:
                            pe.wait_ge(qmasked.sem, 2 * NG * pair + (h // QG + 1))
                        if h >= RING:
                            pe.wait_ge(biasd.sem, PAIR * pair + (h - RING + 1))
                        nc.tensor.matmul(psS[h % RING][:, 0:P], qm[:, h % HEADS, 0:P], KT[:, bass.ds(pair * (2 * SEQ) + h // HEADS * SEQ, P)],
                                         start=True, stop=True)
                        nc.tensor.matmul(psS[h % RING][:, P:SC], qm[:, h % HEADS, P:SEQ], KT[:, bass.ds(pair * (2 * SEQ) + h // HEADS * SEQ, SEQ)],
                                         start=True, stop=True).then_inc(scored.sem, 1)

                    def turn(h):
                        pe.wait_ge(expd.sem, PAIR * pair + (h + 1))
                        if h >= 2:
                            pe.wait_ge(tcopied.sem, PAIR * pair + (h - 1))
                        for j in range(3):
                            m = nc.tensor.transpose(psT[h % 2][:, j * P:(j + 1) * P], Pr[:, h % RING, j * P:(j + 1) * P],
                                                    k.ident[:])
                        m.then_inc(turned.sem, 1)

                    def weigh(h):
                        pe.wait_ge(tcopied.sem, PAIR * pair + (h + 1))
                        seq = h // HEADS
                        if h % HEADS == 0:
                            pe.wait_ge(normed.sem, 2 * pair + (seq + 1))
                        c = h % HEADS * HD
                        o0 = psO[seq][:, c:c + HD]
                        o1 = psO[seq][:, D + c:D + c + HD]
                        v0 = V[:, bass.ds(pair * (2 * KC) + seq * KC, 1), c:c + HD].rearrange("p a d -> p (a d)")
                        v1 = V[:, bass.ds(pair * (2 * KC) + (seq * KC + 1), 1), c:c + HD].rearrange("p a d -> p (a d)")
                        nc.tensor.matmul(o0, PT[:, h % 2, 0:P], v0, start=True, stop=True)
                        nc.tensor.matmul(o1, PT[:, h % 2, P:2 * P], v0, start=True, stop=False)
                        nc.tensor.matmul(o1, PT[:, h % 2, 2 * P:SC], v1, start=False, stop=True)\
                            .then_inc(weighted.sem, 1)

                    for h in range(PAIR + 3):
                        if h < PAIR:
                            scores(h)
                        if 2 <= h < PAIR + 2:
                            turn(h - 2)
                        if h >= 3:
                            weigh(h - 3)

            @block.vector
            def _(dve):
                dve.sem_inc(normed.sem, 2)
                with dve.Fori(0, BATCH // 2) as pair:
                    def add_bias(h):
                        dve.wait_ge(scored.sem, PAIR * pair + (HEADS + h + 1))
                        if h >= RING:
                            dve.wait_ge(expd.sem, PAIR * pair + (h - RING + 1))
                        dve.sem_inc(begun.sem, 1)
                        nc.vector.tensor_tensor_reduce(S[:, h % RING, 0:P], psS[h % RING][:, 0:P], bias[:, h % HEADS, P:SEQ], -1.0,
                                                       -MASKED, ALU.add, ALU.min, nmax[:, h // HEADS, h % HEADS, 0:1])
                        nc.vector.tensor_tensor_reduce(S[:, h % RING, P:SC], psS[h % RING][:, P:SC], bias[:, h % HEADS, :], -1.0,
                                                       -MASKED, ALU.add, ALU.min, nmax[:, h // HEADS, h % HEADS, 1:2])\
                            .then_inc(biasd.sem, 1)

                    def copy_turned(h):
                        dve.wait_ge(turned.sem, PAIR * pair + (h + 1))
                        if h >= 2:
                            dve.wait_ge(weighted.sem, PAIR * pair + (h - 1))
                        nc.vector.tensor_copy(PT[:, h % 2, :], psT[h % 2][:, 0:SC]).then_inc(tcopied.sem, 1)

                    def norm(seq):
                        dve.wait_ge(weighted.sem, PAIR * pair + HEADS * (seq + 1))
                        nc.vector.reciprocal(rinv[:, seq], rsum[:, seq])
                        dve.drain()
                        for qt in range(KC):
                            m = nc.vector.tensor_tensor(
                                O[:, bass.ds(pair * (2 * KC) + (seq * KC + qt), 1), :]
                                .rearrange("p a (h e) -> p (a h) e", e=HD),
                                psO[seq][:, qt * D:(qt + 1) * D].rearrange("p (h e) -> p h e", e=HD),
                                rinv[:, seq, :, qt:qt + 1].to_broadcast([P, HEADS, HD]), ALU.mult)
                        m.then_inc(normed.sem, 1)

                    for h in range(PAIR + 2):
                        if h < PAIR:
                            add_bias(h)
                        if h >= 2:
                            copy_turned(h - 2)
                        if h == HEADS + RING:
                            norm(0)
                    norm(1)

            @block.scalar
            def _(act):
                with act.Fori(0, BATCH // 2) as pair:
                    for h in range(PAIR):
                        act.wait_ge(biasd.sem, PAIR * pair + (h + 1))
                        if h >= RING:
                            act.wait_ge(turned.sem, PAIR * pair + (h - RING + 1))
                        if h % HEADS == 0:
                            act.wait_ge(normed.sem, 2 * pair + (h // HEADS + 1))
                        nc.scalar.activation(Pr[:, h % RING, 0:P], S[:, h % RING, 0:P], ACT.Exp, scale=-1.0,
                                             bias=nmax[:, h // HEADS, h % HEADS, 0:1], accum_out=rsum[:, h // HEADS, h % HEADS, 0:1])
                        nc.scalar.activation(Pr[:, h % RING, P:SC], S[:, h % RING, P:SC], ACT.Exp, scale=-1.0,
                                             bias=nmax[:, h // HEADS, h % HEADS, 1:2], accum_out=rsum[:, h // HEADS, h % HEADS, 1:2]).then_inc(expd.sem, 1)

        project_and_add_stage(k, "at", O, OT, wo)
        w_in.close(64)
        biased.close(3)
        masked.close(3)
        projected.close(12)
        proj_out.close(4)
        v_out.close(4)


def project_and_add_stage(k, name, O, OT, w, w_in_dram=None):
    nc = k.nc
    rows = OT.shape[0]
    loaded = k.tally("pr_loaded")
    turned, copied, projected = (k.tally(f"pr_{n}") for n in ("turned", "copied", "projected"))
    with nc.psum_tensor(f"{name}_pr_psT", [P, 4, 512], F32) as psT, \
            nc.psum_tensor(f"{name}_pr_psR", [P, 4, 512], F32) as psR, nc.Block() as block:
        @block.sync
        def _(sp):
            if w_in_dram is not None:
                sp.dma_start(w[:], w_in_dram).then_inc(loaded.sem, 16)

        @block.tensor
        def _(pe):
            if O is not None:
                for g in range(4):
                    for j in range(4):
                        m = nc.tensor.transpose(psT[0:rows, g, j * P:(j + 1) * P], O[:, 4 * g + j, :], k.ident[:])
                    m.then_inc(turned.sem, 1)
            if w_in_dram is not None:
                pe.wait_ge(*loaded.at(16))
            for g in range(4):
                if O is not None:
                    pe.wait_ge(*copied.at(g + 1))
                for j in range(4):
                    t = 4 * g + j
                    m = nc.tensor.matmul(psR[:, g, j * P:(j + 1) * P], OT[:, t * P:(t + 1) * P], w[:],
                                         start=True, stop=True)
                m.then_inc(projected.sem, 1)

        if O is not None:
            @block.scalar
            def _(act):
                for g in range(4):
                    act.wait_ge(*turned.at(g + 1))
                    nc.scalar.activation(OT[:, g * 512:(g + 1) * 512], psT[0:rows, g, :], ACT.Copy)\
                        .then_inc(copied.sem, 1)

        @block.vector
        def _(dve):
            for g in range(4):
                dve.wait_ge(*projected.at(g + 1))
                x = k.X[:, 4 * g:4 * g + 4, :]
                nc.vector.tensor_tensor(x, x, psR[:, g, :].rearrange("p (t d) -> p t d", d=D), ALU.add)
    projected.close(4)
    if w_in_dram is not None:
        loaded.close(16)
    if O is not None:
        turned.close(4)
        copied.close(4)


PAD = -3e38
TAKEN = -1e38
ROUND = float(1.5 * 2 ** 23)


def route_stage(k, name, comb, r_bias, experts, top, of_probs, renormed, always=0, chosen=None,
                sort=None, psL=None):
    nc = k.nc
    E = experts
    w_in, made, asked, exped, counted, counts = (
        k.tally(n) for n in ("w_in", "made", "asked", "exped", "counted", "counts"))
    with ExitStack() as s:
        sb = lambda n, shape: s.enter_context(nc.sbuf_tensor(f"{name}_rt_{n}", shape, F32))
        rb = sb("rb", [P, E])
        L = sb("L", [P, T, E + 8])
        R = sb("R", [P, T, E + 8])
        m8, rep8 = sb("m8", [P, T, 8]), sb("rep8", [P, T, 8])
        ex, sel = sb("ex", [P, T, E]), sb("sel", [P, E, T] if sort else [P, T, E])
        total, inv, peak = sb("total", [P, T]), sb("inv", [P, T]), sb("peak", [P, T])
        psL = psL or k.logits
        if sort:
            weight, slot, tile_expert = sort
            tiles = tile_expert.shape[1]
            count, first, last = (sb(n, [P, E]) for n in ("count", "first", "last"))
            place = sb("place", [P, T])
            tile_no = sb("tile_no", [1, tiles])
            past = sb("past", [1, tiles, E])
            psN = s.enter_context(nc.psum_tensor(f"{name}_psN", [P, E], F32))
            upto, before, again = sb("upto", [P, E, T]), sb("before", [P, E, T]), sb("again", [P, E, T])
            tri = sb("tri", [P, P])
            psC = s.enter_context(nc.psum_tensor(f"{name}_psC", [P, E, T], F32))
        block = s.enter_context(nc.Block())
        bc = lambda ap, n: ap.unsqueeze(2).to_broadcast([P, T, n])

        @block.sync
        def _(sp):
            if r_bias is not None:
                sp.dma_start(rb[:], r_bias.partition_broadcast(P)).then_inc(w_in.sem, 16)

        @block.gpsimd
        def _(pool):
            if sort:
                nc.gpsimd.iota(tile_no[:], [[1, tiles]], base=0, channel_multiplier=0,
                               allow_small_or_imprecise_dtypes=True)
                nc.gpsimd.affine_select(out=tri[:], in_=k.ones[:], compare_op=ALU.is_ge, fill=0.0, base=-1,
                                        pattern=[[1, P]], channel_multiplier=-1).then_inc(made.sem, 1)

        @block.tensor
        def _(pe):
            if sort:
                pe.wait_ge(*made.at(1))
                pe.wait_ge(*counted.at(1))
                flat = lambda t: t[:].rearrange("p e t -> p (e t)")
                nc.tensor.matmul(flat(psC), tri[:], flat(sel), start=True, stop=False)
                nc.tensor.matmul(flat(psC), k.ones[:], flat(before), start=False, stop=True)
                m = nc.tensor.matmul(psN[:], k.ones[:], upto[:, :, T - 1], start=True, stop=True)
                m.then_inc(counts.sem, 1)

        @block.scalar
        def _(act):
            act.wait_ge(*asked.at(1))
            nc.scalar.activation(ex[:], ex[:], ACT.Exp).then_inc(exped.sem, 1)

        @block.vector
        def _(dve):
            nc.vector.memset(L[:, :, E:E + 8], PAD)
            if always:
                nc.vector.memset(comb[:, :, E:E + always], 1.0)
            if sort:
                nc.vector.memset(again[:], 1.0)
                dve.drain()
                nc.vector.memset(again[:, :, 0:1], 0.0)
            if r_bias is not None:
                dve.wait_ge(*w_in.at(16))
                nc.vector.tensor_tensor(L[:, :, 0:E], psL[:], rb[:].unsqueeze(1).to_broadcast([P, T, E]), ALU.add)
            else:
                nc.vector.tensor_copy(L[:, :, 0:E], psL[:])
            dve.drain()
            nc.vector.tensor_reduce(peak[:], L[:, :, 0:E], AX.X, ALU.max)
            dve.drain()
            nc.vector.tensor_tensor(ex[:], L[:, :, 0:E], bc(peak[:], E), ALU.subtract).then_inc(asked.sem, 1)
            if top > 1 and not of_probs:
                for t in range(T):
                    nc.vector.max(m8[:, t, :], L[:, t, 0:E])
            dve.wait_ge(*exped.at(1))
            if of_probs:
                nc.vector.tensor_reduce(total[:], ex[:], AX.X, ALU.add)
                dve.drain()
                nc.vector.reciprocal(inv[:], total[:])
                dve.drain()
                nc.vector.tensor_tensor(ex[:], ex[:], bc(inv[:], E), ALU.mult)
                dve.drain()
                nc.vector.tensor_copy(L[:, :, 0:E], ex[:])
                dve.drain()
                if top > 1:
                    for t in range(T):
                        nc.vector.max(m8[:, t, :], L[:, t, 0:E])
            dve.drain()
            if top == 1:
                nc.vector.tensor_copy(rep8[:, :, 0], inv[:])
            else:
                nc.vector.tensor_copy(rep8[:], m8[:])
                dve.drain()
            if top < 8:
                nc.vector.memset(rep8[:, :, top:8], PAD)
            dve.drain()
            for t in range(T):
                nc.vector.match_replace(R[:, t, :], rep8[:, t, :], L[:, t, :], TAKEN)
            dve.drain()
            nc.vector.tensor_tensor(sel[:].rearrange("p e t -> p t e") if sort else sel[:], R[:, :, 0:E], L[:, :, 0:E],
                                    ALU.not_equal)
            dve.drain()
            if chosen:
                nc.vector.tensor_copy(chosen[:].rearrange("p t (h e) -> p h t e", h=2),
                                      sel[:].rearrange("p (h t) e -> p h t e", h=2))
            if not sort:
                c = comb[:, :, 0:E]
                nc.vector.tensor_tensor(c, ex[:], sel[:], ALU.mult)
                dve.drain()
            if renormed:
                nc.vector.tensor_reduce(total[:], c, AX.X, ALU.add)
                dve.drain()
                nc.vector.reciprocal(inv[:], total[:])
                dve.drain()
                nc.vector.tensor_tensor(c, c, bc(inv[:], E), ALU.mult)
                dve.drain()
            if sort:
                flat = lambda t: t[:].rearrange("p e t -> p (e t)")
                nc.vector.tensor_tensor_scan(flat(upto), flat(again), flat(sel), 0.0, ALU.mult, ALU.add)
                dve.drain()
                nc.vector.tensor_tensor(before[:], upto[:], sel[:], ALU.subtract).then_inc(counted.sem, 1)
                dve.wait_ge(*counts.at(1))
                dve.wait_ge(*made.at(1))
                nc.vector.tensor_copy(weight[:], inv[:])
                nc.vector.tensor_scalar(count[:], psN[:], 1.0 / P, 63.5 / P, ALU.mult, ALU.add)
                dve.drain()
                nc.vector.tensor_scalar(count[:], count[:], ROUND, None, ALU.add)
                dve.drain()
                nc.vector.tensor_scalar(count[:], count[:], -ROUND, None, ALU.add)
                dve.drain()
                nc.vector.tensor_tensor_scan(last[:], k.ones[:, 0:E], count[:], 0.0, ALU.mult, ALU.add)
                dve.drain()
                nc.vector.tensor_tensor(first[:], last[:], count[:], ALU.subtract)
                dve.drain()
                nc.vector.tensor_scalar(first[:], first[:], float(P), None, ALU.mult)
                dve.drain()
                nc.vector.tensor_tensor(before[:], psC[:], first[:].unsqueeze(2).to_broadcast([P, E, T]), ALU.add)
                dve.drain()
                nc.vector.tensor_tensor(before[:], before[:], sel[:], ALU.mult)
                dve.drain()
                nc.vector.tensor_reduce(place[:], before[:].rearrange("p e t -> p t e"), AX.X, ALU.add)
                dve.drain()
                nc.vector.tensor_copy(slot[:], place[:])
                nc.vector.tensor_tensor(past[:], tile_no[:].unsqueeze(2).to_broadcast([1, tiles, E]),
                                        last[0:1, :].unsqueeze(1).to_broadcast([1, tiles, E]), ALU.is_ge)
                dve.drain()
                nc.vector.tensor_reduce(tile_no[:], past[:], AX.X, ALU.add)
                dve.drain()
                nc.vector.tensor_scalar(tile_expert[:], tile_no[:], float(E - 1), float(F3), ALU.min, ALU.mult)
    if r_bias is not None:
        w_in.close(16)
    asked.close(1)
    exped.close(1)
    if sort:
        for t in (made, counted, counts):
            t.close(1)


def experts_stage(k, name, comb, w_up, w_down, count, chunk, chunks, biased, acc, packed=1):
    nc = k.nc
    WU = chunks * chunk * 2 + (2 * chunks if biased else 0)
    subs = [(j, slice(chunk // packed * j, chunk // packed * (j + 1))) for j in range(packed)]
    UNITS = NBLK * chunks
    up_done, silu_done, hid_done, down_done, acc_done = (
        k.tally(n) for n in ("up_done", "silu_done", "hid_done", "down_done", "acc_done"))
    w_in = [k.tally(f"w_in{i}") for i in range(2)]
    pairs = count // 2
    odd = count % 2
    looped = pairs if odd else pairs - 1
    with ExitStack() as s:
        wu = [s.enter_context(nc.sbuf_tensor(f"{name}_wu{i}", [P, WU], F32)) for i in range(2)]
        wd = [s.enter_context(nc.sbuf_tensor(f"{name}_wd{i}", [chunk, chunks * D], F32)) for i in range(2)]
        sg = s.enter_context(nc.sbuf_tensor(f"{name}_sg", [chunk, 2, 512], F32))
        hid = s.enter_context(nc.sbuf_tensor(f"{name}_hid", [chunk, 2, 512], F32))
        psG = s.enter_context(nc.psum_tensor(f"{name}_psG", [P, 2, 512], F32))
        psU = s.enter_context(nc.psum_tensor(f"{name}_psU", [P, 2, 512], F32))
        psD = s.enter_context(nc.psum_tensor(f"{name}_psD", [P, packed, 2, 512], F32))
        block = s.enter_context(nc.Block())

        def units(experts, follow):
            u = [(e, b, c) for e in range(experts) for b in range(NBLK) for c in range(chunks)]
            for j, unit in enumerate(u):
                nxt = u[j + 1] if j + 1 < len(u) else ((0, 0, 0) if follow else None)
                yield j, unit, nxt

        def engine(eng, body):
            if looped:
                with eng.Fori(0, looped) as i:
                    body(i, 2, True)
            if odd:
                body(pairs, 1, False)
            else:
                body(pairs - 1, 2, False)

        @block.sync
        def _(sp):
            def load(e, half):
                sp.dma_start(wu[half][:], w_up[bass.ds(e, 1), :, :].rearrange("a p f -> p (a f)"))\
                    .then_inc(w_in[half].sem, 16)
                sp.dma_start(wd[half][:], w_down[bass.ds(e, 1), :, :].rearrange("a p f -> p (a f)"))\
                    .then_inc(w_in[half].sem, 16)

            load(0, 0)
            if count > 1:
                load(1, 1)
            if pairs > 1:
                with sp.Fori(1, pairs) as i:
                    for half in range(2):
                        sp.wait_ge(*down_done.at(2 * NBLK * i + (NBLK * (half - 1))))
                        load(2 * i + half, half)
            if odd:
                sp.wait_ge(*down_done.at(NBLK * (count - 2)))
                load(count - 1, 0)

        @block.tensor
        def _(pe):
            def up(i, j, unit):
                half, b, c = unit
                if b == 0 and c == 0:
                    pe.wait_ge(*w_in[half].at(32 * i + 32))
                pe.wait_ge(*hid_done.at(2 * UNITS * i + (j + 1)))
                x = k.XT[:, b * 512:(b + 1) * 512]
                w = wu[half]
                nc.tensor.matmul(psG[0:chunk, j % 2, :], w[:, c * chunk:(c + 1) * chunk], x, start=True, stop=True)
                o = (chunks + c) * chunk
                nc.tensor.matmul(psU[0:chunk, j % 2, :], w[:, o:o + chunk], x, start=True, stop=True)\
                    .then_inc(up_done.sem, 1)

            def down(i, j, unit):
                half, b, c = unit
                pe.wait_ge(*hid_done.at(2 * UNITS * i + (j + 3)))
                if c == 0:
                    pe.wait_ge(*acc_done.at(2 * NBLK * i + (NBLK * half + b + 1)))
                for sub, p in subs:
                    for t in range(4):
                        m = nc.tensor.matmul(psD[:, sub, b % 2, t * P:(t + 1) * P], hid[p, j % 2, t * P:(t + 1) * P],
                                             wd[half][p, c * D:(c + 1) * D], start=(c == 0 and t == 0),
                                             stop=(c == chunks - 1 and t == 3), skip_group_check=True)
                if c == chunks - 1:
                    m.then_inc(down_done.sem, 1)

            def body(i, experts, follow):
                for j, unit, nxt in units(experts, follow):
                    if nxt is not None:
                        if j + 1 < experts * UNITS:
                            up(i, j + 1, nxt)
                        else:
                            up(i + 1, 0, nxt)
                    down(i, j, unit)

            up(0, 0, (0, 0, 0))
            engine(pe, body)

        @block.scalar
        def _(act):
            def body(i, experts, follow):
                for j, (half, b, c), _ in units(experts, follow):
                    act.wait_ge(*up_done.at(2 * UNITS * i + (j + 1)))
                    w = wu[half]
                    o = chunks * chunk * 2 + c
                    bias = {"bias": w[0:chunk, o:o + 1]} if biased else {}
                    nc.scalar.activation(sg[:, j % 2, :], psG[0:chunk, j % 2, :], ACT.Silu, **bias)\
                        .then_inc(silu_done.sem, 1)

            engine(act, body)

        @block.vector
        def _(dve):
            def hide(i, j, unit):
                half, b, c = unit
                dve.wait_ge(*silu_done.at(2 * UNITS * i + (j + 1)))
                w = wu[half]
                o = chunks * chunk * 2 + chunks + c
                if biased:
                    m = nc.vector.scalar_tensor_tensor(out=hid[:, j % 2, :], in0=psU[0:chunk, j % 2, :],
                                                       scalar=w[0:chunk, o:o + 1], in1=sg[:, j % 2, :],
                                                       op0=ALU.add, op1=ALU.mult)
                else:
                    m = nc.vector.tensor_tensor(hid[:, j % 2, :], psU[0:chunk, j % 2, :], sg[:, j % 2, :], ALU.mult)
                m.then_inc(hid_done.sem, 1)

            def add(i, unit):
                half, b, c = unit
                dve.wait_ge(*down_done.at(2 * NBLK * i + (NBLK * half + b + 1)))
                for sub, _ in subs:
                    if sub:
                        dve.drain()
                    for t in range(4):
                        a = acc[:, 4 * b + t, :]
                        e = bass.ds(i * (2 * packed) + (packed * half + sub), 1)
                        m = nc.vector.scalar_tensor_tensor(out=a, in0=psD[:, sub, b % 2, t * P:(t + 1) * P],
                                                           scalar=comb[:, 4 * b + t, e], in1=a,
                                                           op0=ALU.mult, op1=ALU.add)
                m.then_inc(acc_done.sem, 1)

            def body(i, experts, follow):
                for j, unit, nxt in units(experts, follow):
                    if nxt is not None:
                        if j + 1 < experts * UNITS:
                            hide(i, j + 1, nxt)
                        else:
                            hide(i + 1, 0, nxt)
                    if unit[2] == chunks - 1:
                        add(i, unit)

            dve.sem_inc(acc_done.sem, 2)
            dve.sem_inc(hid_done.sem, 2)
            hide(0, 0, (0, 0, 0))
            engine(dve, body)
    up_done.close(count * UNITS)
    silu_done.close(count * UNITS)
    hid_done.close(count * UNITS + 2)
    down_done.close(count * NBLK)
    acc_done.close(count * NBLK + 2)
    w_in[0].close(32 * (pairs + odd))
    w_in[1].close(32 * pairs)


def moe_l0_stage(k, a):
    E, F = 8, 256
    nc = k.nc
    with nc.sbuf_tensor("m0_comb", [P, T, E], F32) as comb:
        route_stage(k, "m0", comb, None, E, top=2, of_probs=False, renormed=True)
        k.close_logits()
        with nc.sbuf_tensor("m0_combT", [E, N], F32) as combT, nc.sbuf_tensor("m0_b3", [E, D], F32) as b3:
            project_and_add_stage(k, "m0", comb, combT, b3, a["L0_ffn_b3"])
        experts_stage(k, "m0", comb, a["L0_ffn_up"], a["L0_ffn_down"], E, P, F // P, True, k.X)


def moe_l1_stage(k, a):
    E, F, S = 16, 64, 2
    with k.nc.sbuf_tensor("m1_comb", [P, T, E + S], F32) as comb:
        route_stage(k, "m1", comb, a["L1_ffn_router_bias"], E, top=2, of_probs=False,
                    renormed=True, always=S)
        k.close_logits()
        experts_stage(k, "m1", comb, a["L1_ffn_up"], a["L1_ffn_down"], (E + S) // 2, 2 * F, 1, False,
                      k.X, packed=2)


UNROLL, AHEAD = 4, 7


def steps(eng, step, tiles, more=0):
    for v in range(AHEAD):
        step(v, v % UNROLL)
    trips = (tiles - AHEAD) // UNROLL
    with eng.Fori(0, trips) as i:
        for c in range(UNROLL):
            step(i * UNROLL + (AHEAD + c), (AHEAD + c) % UNROLL)
    for v in range(AHEAD + trips * UNROLL, tiles + more):
        step(v, v % UNROLL)


def inside(j, tiles):
    return not isinstance(j, int) or 0 <= j < tiles


def some(n):
    return not isinstance(n, int) or n > 0


def rounds(v, m, off=0, each=16):
    if isinstance(v, int):
        return each * ((v - m) // UNROLL + 1 - off)
    return v * (each // UNROLL) + (each - each // UNROLL * m - each * off)


E2, F2, SLOTS = 64, 96, 64
SLOT_TILES = E2 * SLOTS // P
ROW = D + E2
LATER = 2.0 * N


def moe_l2_stage(k, a):
    nc = k.nc
    with ExitStack() as s:
        sb = lambda n, shape, dt=F32: s.enter_context(nc.sbuf_tensor(f"m2_{n}", shape, dt))
        comb, pairs = sb("comb", [P, T, E2]), sb("pairs", [P, T // 2, 2 * E2])
        token, row = sb("token", [P, SLOT_TILES]), sb("row", [P, SLOT_TILES], mybir.dt.uint32)
        count = sb("count", [P, N], F16)
        k.token_rows = nc.dram_tensor("token_rows", (N, ROW), F32).ap()
        route_stage(k, "m2", comb, None, E2, top=8, of_probs=True, renormed=True,
                    chosen=pairs)
        k.close_logits()
        acc = s.enter_context(nc.psum_tensor("m2_acc", [P, NBLK, 512], F32))
        slots_stage(k, a, comb, pairs, acc, token, row, count)
        slot_experts_stage(k, a, acc, token, row, count)
        with nc.psum_tensor("m2_psA", [P, NBLK, 512], F32) as ps:
            add_turned_stage(k, acc, ps)


def slots_stage(k, a, comb, pairs, acc, token, row, count):
    nc = k.nc
    saved, w_in, made, turned, valued, halved, joined, listed, spread, up_done, silu_done, hid_done, down_done = (
        k.tally(n) for n in ("saved", "w_in", "made", "turned", "valued", "halved", "joined", "listed", "spread", "up_done",
                                     "silu_done", "hid_done", "down_done"))
    with ExitStack() as s:
        sb = lambda n, shape, dt=F32: s.enter_context(nc.sbuf_tensor(f"sl_{n}", shape, dt))
        late = sb("late", [P, N // 2])
        V = [sb(f"V{i}", [P, N // 2]) for i in range(2)]
        half_top = sb("half_top", [P, SLOTS])
        W = [sb(f"W{i}", [E2, 2 * SLOTS]) for i in range(2)]
        top = sb("top", [E2, 2, SLOTS])
        numbers = sb("numbers", [P, N])
        wu, wd = sb("wu", [P, 2 * F2]), sb("wd", [F2, D])
        sg, hid = sb("sg", [F2, 2, 512]), sb("hid", [F2, 2, 512])
        psG, psU = (s.enter_context(nc.psum_tensor(f"sl_ps{n}", [P, 2, 512], F32)) for n in "GU")
        block = s.enter_context(nc.Block())

        @block.sync
        def _(sp):
            sp.dma_start(wu[:], a["L2_ffn_up"][E2]).then_inc(w_in.sem, 16)
            sp.dma_start(wd[:], a["L2_ffn_down"][E2]).then_inc(w_in.sem, 16)
            rows = k.token_rows.rearrange("(t p) r -> p t r", p=P)
            sp.dma_start(rows[:, :, 0:D], k.X[:]).then_inc(saved.sem, 16)
            sp.dma_start(rows[:, :, D:ROW], comb[:]).then_inc(saved.sem, 16)
            sp.wait_ge(*saved.at(32))

        @block.gpsimd
        def _(pool):
            for h in range(2):
                i = nc.gpsimd.iota(late[h * E2:(h + 1) * E2, :], [[-1, N // 2]], base=int(LATER) - h * N // 2,
                                   channel_multiplier=0, allow_small_or_imprecise_dtypes=True)
                i.then_inc(made.sem, 1)
            pool.wait_ge(*made.at(2))
            nc.gpsimd.iota(numbers[:], [[1, N]], base=0, channel_multiplier=0,
                           allow_small_or_imprecise_dtypes=True).then_inc(made.sem, 1)

        @block.tensor
        def _(pe):
            for g in range(2):
                for j in range(4):
                    t = 4 * g + j
                    m = nc.tensor.transpose(acc[:, g, j * P:(j + 1) * P], pairs[:, t, :], k.ident[:])
                m.then_inc(turned.sem, 1)
            pe.wait_ge(*w_in.at(32))

            def up(b):
                if b >= 2:
                    pe.wait_ge(*hid_done.at(b - 1))
                x = k.XT[:, b * 512:(b + 1) * 512]
                nc.tensor.matmul(psG[0:F2, b % 2, :], wu[:, 0:F2], x, start=True, stop=True)
                nc.tensor.matmul(psU[0:F2, b % 2, :], wu[:, F2:2 * F2], x, start=True, stop=True)\
                    .then_inc(up_done.sem, 1)

            up(0)
            pe.wait_ge(*valued.at(2))
            for b in range(NBLK):
                if b + 1 < NBLK:
                    up(b + 1)
                pe.wait_ge(*hid_done.at(b + 1))
                nc.tensor.matmul(acc[:, b, :], wd[:], hid[:, b % 2, :], start=True, stop=True)\
                    .then_inc(down_done.sem, 1)
            pe.wait_ge(*halved.at(1))
            for h in range(2):
                m = nc.tensor.matmul(psU[0:E2, 0, h * SLOTS:(h + 1) * SLOTS], k.ident[:, h * E2:(h + 1) * E2],
                                     half_top[:], start=True, stop=True)
            m.then_inc(joined.sem, 1)
            pe.wait_ge(*listed.at(1))
            nc.tensor.matmul(psG[:, 0, 0:E2], top[:].rearrange("e h c -> e (h c)"), k.ident[0:E2, 0:E2],
                             start=True, stop=True).then_inc(spread.sem, 1)

        @block.scalar
        def _(act):
            for b in range(NBLK):
                act.wait_ge(*up_done.at(b + 1))
                nc.scalar.activation(sg[:, b % 2, :], psG[0:F2, b % 2, :], ACT.Silu).then_inc(silu_done.sem, 1)

        @block.vector
        def _(dve):
            dve.wait_ge(*made.at(2))
            for g in range(2):
                dve.wait_ge(*turned.at(g + 1))
                c = slice(g * 512, (g + 1) * 512)
                nc.vector.tensor_tensor(V[0][:, c], acc[:, g, :], late[:, c], ALU.mult).then_inc(valued.sem, 1)
            dve.drain()

            def firsts(top, lists, between=None):
                for r in range(SLOTS // 8):
                    nc.vector.max(top[:, 8 * r:8 * r + 8], lists[r % 2][:])
                    if between:
                        between(r)
                    dve.drain()
                    if r < SLOTS // 8 - 1:
                        nc.vector.match_replace(lists[(r + 1) % 2][:], top[:, 8 * r:8 * r + 8], lists[r % 2][:], 0.0)
                        dve.drain()

            def hide(r):
                b = r - 3
                if 0 <= b < NBLK:
                    dve.wait_ge(*silu_done.at(b + 1))
                    if b >= 2:
                        dve.wait_ge(*down_done.at(b - 1))
                    nc.vector.tensor_tensor(hid[:, b % 2, :], psU[0:F2, b % 2, :], sg[:, b % 2, :], ALU.mult)\
                        .then_inc(hid_done.sem, 1)

            firsts(half_top[:], V, hide)
            dve.sem_inc(halved.sem, 1)
            dve.wait_ge(*joined.at(1))
            nc.vector.tensor_copy(W[0][:], psU[0:E2, 0, 0:2 * SLOTS])
            dve.drain()
            firsts(top[:, 0, :], W)
            nc.vector.tensor_copy(top[:, 1, :], top[:, 0, :]).then_inc(listed.sem, 1)
            dve.wait_ge(*made.at(3))
            nc.vector.tensor_copy(count[:], numbers[:])
            dve.wait_ge(*spread.at(1))
            for h in range(2):
                half = slice(SLOTS * h, SLOTS * (h + 1))
                nc.vector.tensor_scalar(token[half, :], psG[half, 0, h:E2:2], -1.0, LATER, ALU.mult, ALU.add)
            dve.drain()
            nc.vector.tensor_scalar(row[:], token[:], float(N - 1), None, ALU.min)
    saved.close(32)
    w_in.close(32)
    made.close(3)
    for t in (up_done, silu_done, hid_done, down_done):
        t.close(NBLK)
    for t in (turned, valued):
        t.close(2)
    halved.close(1)
    joined.close(1)
    listed.close(1)
    spread.close(1)


def slot_experts_stage(k, a, acc, token, row, count):
    nc = k.nc
    gathered = [k.tally(f"gathered{m}") for m in range(UNROLL)]
    w_in = [k.tally(f"w_in{m}") for m in range(UNROLL)]
    turned, x_out, up_done, silu_done, hid_done, down_done, high_done, parts_done, placed, used = (
        k.tally(n) for n in ("turned", "x_out", "up_done", "silu_done", "hid_done", "down_done",
                                     "high_done", "parts_done", "placed", "used"))
    with ExitStack() as s:
        sb = lambda n, shape, dt=F32: s.enter_context(nc.sbuf_tensor(f"se_{n}", shape, dt))
        xs = [sb(f"xs{m}", [P, ROW]) for m in range(UNROLL)]
        wu = [sb(f"wu{m}", [P, 2, 2 * F2]) for m in range(UNROLL)]
        wd = [sb(f"wd{m}", [F2, 2, D]) for m in range(UNROLL)]
        weight = [sb(f"weight{m}", [P, 1]) for m in range(UNROLL)]
        xT = [sb(f"xT{b}", [P, P]) for b in range(2)]
        sg, hid = ([sb(f"{n}{b}", [F2, P]) for b in range(2)] for n in ("sg", "hid"))
        rest = sb("rest", [P, D])
        parts = [sb(f"parts{b}", [P, 3, D], BF16) for b in range(2)]
        place = [sb(f"place{b}", [P, N], BF16) for b in range(2)]
        psX, psY = (s.enter_context(nc.psum_tensor(f"se_ps{n}", [P, 512], F32)) for n in "XY")
        psH = [s.enter_context(nc.psum_tensor(f"se_psH{b}", [P, 2, 256], F32)) for b in range(2)]
        block = s.enter_context(nc.Block())

        @block.gpsimd
        def _(pool):
            for j in range(SLOT_TILES):
                m = j % UNROLL
                if j >= UNROLL:
                    pool.wait_ge(*x_out.at(j - UNROLL + 1))
                pool.indirect_dma_start(xs[m][:], None, k.token_rows, bass.IndirectOffsetOnAxis(row[:, j:j + 1], 0))\
                    .then_inc(gathered[m].sem, 16)

        @block.sync
        def _(sp):
            def step(v, m):
                if inside(v, SLOT_TILES):
                    if some(v - 3):
                        sp.wait_ge(*down_done.at(v - 3))
                    sp.dma_start(wu[m][:], a["L2_ffn_up"][bass.ds(v * 2, 2), :, :].rearrange("e p f -> p e f"))\
                        .then_inc(w_in[m].sem, 16)
                    sp.dma_start(wd[m][:], a["L2_ffn_down"][bass.ds(v * 2, 2), :, :].rearrange("e p f -> p e f"))\
                        .then_inc(w_in[m].sem, 16)

            steps(sp, step, SLOT_TILES)

        @block.tensor
        def _(pe):
            def step(v, m):
                j, b = v, m % 2
                if inside(j, SLOT_TILES):
                    pe.wait_ge(*gathered[m].at(rounds(v, m)))
                    if some(j):
                        pe.wait_ge(*x_out.at(j))
                    nc.tensor.transpose(psX[:, 0:P], xs[m][:, 0:D], k.ident[:]).then_inc(turned.sem, 1)
                j, m1, b = v - 1, (m - 1) % UNROLL, (m - 1) % 2
                if inside(j, SLOT_TILES):
                    pe.wait_ge(*w_in[m1].at(rounds(j, m1, each=32)))
                    pe.wait_ge(*x_out.at(j + 1))
                    if some(j - 1):
                        pe.wait_ge(*hid_done.at(j - 1))
                    for e in range(2):
                        half = slice(e * SLOTS, (e + 1) * SLOTS)
                        nc.tensor.matmul(psH[b][0:F2, 0, half], wu[m1][:, e, 0:F2], xT[b][:, half], start=True, stop=True)
                        i = nc.tensor.matmul(psH[b][0:F2, 1, half], wu[m1][:, e, F2:2 * F2], xT[b][:, half],
                                             start=True, stop=True)
                    i.then_inc(up_done.sem, 1)
                j, m2, b = v - 2, (m - 2) % UNROLL, (m - 2) % 2
                if inside(j, SLOT_TILES):
                    pe.wait_ge(*hid_done.at(j + 1))
                    if some(j):
                        pe.wait_ge(*parts_done.at(j))
                    for e in range(2):
                        half = slice(e * SLOTS, (e + 1) * SLOTS)
                        i = nc.tensor.matmul(psY[half, 0:D], hid[b][:, half], wd[m2][:, e, :], start=True, stop=True)
                    i.then_inc(down_done.sem, 1)
                j, b = v - 3, (m - 3) % 2
                if inside(j, SLOT_TILES):
                    pe.wait_ge(*parts_done.at(j + 1))
                    pe.wait_ge(*placed.at(j + 1))
                    for part in range(3):
                        for g in range(NBLK):
                            i = nc.tensor.matmul(acc[:, g, :], parts[b][:, part, :], place[b][:, g * 512:(g + 1) * 512],
                                                 start=False, stop=True, skip_group_check=True)
                    i.then_inc(used.sem, 1)

            steps(pe, step, SLOT_TILES, 3)

        @block.scalar
        def _(act):
            def step(v, m):
                j, b = v, m % 2
                if inside(j, SLOT_TILES):
                    act.wait_ge(*turned.at(j + 1))
                    if some(j - 3):
                        act.wait_ge(*parts_done.at(j - 3))
                    for e in range(2):
                        half = slice(e * SLOTS, (e + 1) * SLOTS)
                        nc.scalar.activation(weight[m][half, :], xs[m][half, bass.ds(j * 2 + (D + e), 1)], ACT.Copy)
                    if some(j - 1):
                        act.wait_ge(*up_done.at(j - 1))
                    nc.scalar.activation(xT[b][:], psX[:, 0:P], ACT.Copy).then_inc(x_out.sem, 1)
                j, b = v - 1, (m - 1) % 2
                if inside(j, SLOT_TILES):
                    act.wait_ge(*up_done.at(j + 1))
                    if some(j - 1):
                        act.wait_ge(*hid_done.at(j - 1))
                    nc.scalar.activation(sg[b][:], psH[b][0:F2, 0, 0:P], ACT.Silu).then_inc(silu_done.sem, 1)
                j, m2, b = v - 2, (m - 2) % UNROLL, (m - 2) % 2
                if inside(j, SLOT_TILES):
                    act.wait_ge(*down_done.at(j + 1))
                    if some(j - 1):
                        act.wait_ge(*used.at(j - 1))
                    nc.scalar.activation(parts[b][:, 0, :], psY[:, 0:D], ACT.Copy, scale=weight[m2][:, 0:1])\
                        .then_inc(high_done.sem, 1)

            steps(act, step, SLOT_TILES, 2)

        @block.vector
        def _(dve):
            def step(v, m):
                j, b = v - 1, (m - 1) % 2
                if inside(j, SLOT_TILES):
                    dve.wait_ge(*silu_done.at(j + 1))
                    if some(j - 1):
                        dve.wait_ge(*down_done.at(j - 1))
                    nc.vector.tensor_tensor(hid[b][:], psH[b][0:F2, 1, 0:P], sg[b][:], ALU.mult).then_inc(hid_done.sem, 1)
                j, m2, b = v - 2, (m - 2) % UNROLL, (m - 2) % 2
                if inside(j, SLOT_TILES):
                    dve.wait_ge(*high_done.at(j + 1))
                    nc.vector.scalar_tensor_tensor(out=rest[:], in0=psY[:, 0:D], scalar=weight[m2][:, 0:1],
                                                   in1=parts[b][:, 0, :], op0=ALU.mult, op1=ALU.subtract)
                    dve.drain()
                    nc.vector.tensor_copy(parts[b][:, 1, :], rest[:])
                    dve.drain()
                    nc.vector.tensor_tensor(parts[b][:, 2, :], rest[:], parts[b][:, 1, :], ALU.subtract)\
                        .then_inc(parts_done.sem, 1)
                    if some(j - 1):
                        dve.wait_ge(*used.at(j - 1))
                    nc.vector.tensor_scalar(place[b][:], count[:], token[:, bass.ds(j, 1)], None, ALU.is_equal)\
                        .then_inc(placed.sem, 1)

            steps(dve, step, SLOT_TILES, 2)
    for t in gathered:
        t.close(16 * SLOT_TILES // UNROLL)
    for t in w_in:
        t.close(32 * SLOT_TILES // UNROLL)
    for t in (turned, x_out, up_done, silu_done, hid_done, down_done, high_done, parts_done, placed, used):
        t.close(SLOT_TILES)


def add_turned_stage(k, acc, ps):
    nc = k.nc
    copied, turned, added = (k.tally(n) for n in ("copied", "turned", "added"))
    with nc.Block() as block:
        @block.scalar
        def _(act):
            for g in range(NBLK):
                nc.scalar.activation(k.XT[:, g * 512:(g + 1) * 512], acc[:, g, :], ACT.Copy).then_inc(copied.sem, 1)

        @block.tensor
        def _(pe):
            for g in range(NBLK):
                pe.wait_ge(*copied.at(g + 1))
                for j in range(4):
                    t = 4 * g + j
                    m = nc.tensor.transpose(ps[:, g, j * P:(j + 1) * P], k.XT[:, t * P:(t + 1) * P], k.ident[:])
                m.then_inc(turned.sem, 1)

        @block.vector
        def _(dve):
            for g in range(NBLK):
                dve.wait_ge(*turned.at(g + 1))
                x = k.X[:, 4 * g:4 * g + 4, :].rearrange("p t d -> p (t d)")
                nc.vector.tensor_tensor(x, ps[:, g, :], x, ALU.add).then_inc(added.sem, 1)
    for t in (copied, turned, added):
        t.close(NBLK)


E3, F3, LAYERS = 16, 512, 4
SORT_TILES = (N + E3 * (P - 1)) // P


def keep_l3_weights(k):
    nc = k.nc
    k.W1, k.W2 = k.keep("W1", [P, E3, F3]), k.keep("W2", [P, E3, F3])
    k.routers = k.keep("routers", [P, LAYERS, E3])
    k.zero = k.keep("zero", [P, D])
    k.sorted_x = nc.dram_tensor("sorted_x", (SORT_TILES * P, D), F32).ap()
    k.sorted_y = nc.dram_tensor("sorted_y", (SORT_TILES * P, D), F32).ap()


def start_l3_loads(k, a, sp, cleared):
    loaded, zeroed = k.tally("l3_loaded"), k.tally("l3_zeroed")
    sp.dma_start(k.routers[:], a["L3_ffn_routers"].rearrange("l p e -> p l e")).then_inc(loaded.sem, 16)
    for g in range(4):
        e = slice(4 * g, 4 * g + 4)
        sp.dma_start(k.W1[:, e, :], a["L3_ffn_up"][e].rearrange("e p f -> p e f")).then_inc(loaded.sem, 16)
        sp.dma_start(k.W2[:, e, :], a["L3_ffn_down"][e].rearrange("e p f -> p e f")).then_inc(loaded.sem, 16)
    sp.wait_ge(*cleared.at(1))
    sp.dma_start(k.sorted_x.rearrange("(j p) d -> p j d", p=P),
                 k.zero[:].unsqueeze(1).to_broadcast([P, SORT_TILES, D])).then_inc(zeroed.sem, 16)


def sorted_experts_stage(k, name, Y, slot, tile_expert, first):
    nc = k.nc
    C = F3 // P
    scattered, loaded_w, zeroed = k.tally("scattered"), k.tally("l3_loaded"), k.tally("l3_zeroed")
    x_in = [k.tally(f"x_in{i}") for i in range(4)]
    stored = [k.tally(f"stored{i}") for i in range(4)]
    turned_x, x_out, up_done, silu_done, turned_h, h_out, down_done, y_out = (
        k.tally(n) for n in
        ("turned_x", "x_out", "up_done", "silu_done", "turned_h", "h_out", "down_done", "y_out"))
    with ExitStack() as s:
        sb = lambda n, shape: s.enter_context(nc.sbuf_tensor(f"{name}_{n}", shape, F32))
        xs = [sb(f"xs{i}", [P, D]) for i in range(4)]
        ys = [sb(f"ys{i}", [P, D]) for i in range(4)]
        xT = [sb(f"xT{i}", [P, P]) for i in range(2)]
        h = [sb(f"h{i}", [P, F3]) for i in range(2)]
        hT = [sb(f"hT{i}", [P, F3]) for i in range(2)]
        pb = lambda n: s.enter_context(nc.psum_tensor(f"{name}_{n}", [P, 512], F32))
        psX, psH, psT, psY = ([pb(f"ps{n}{i}") for i in range(2)] for n in "XHTY")
        block = s.enter_context(nc.Block())
        tile_rows = lambda t, j: t.rearrange("(j p) d -> j p d", p=P)[bass.ds(j, 1), :, :]\
            .rearrange("a p d -> (a p) d")

        @block.gpsimd
        def _(pool):
            if first:
                pool.wait_ge(*zeroed.at(16))
            for t in range(T):
                pool.indirect_dma_start(k.sorted_x, bass.IndirectOffsetOnAxis(slot[:, t:t + 1], 0), Y[:, t, :], None)\
                    .then_inc(scattered.sem, 16)

        @block.sync
        def _(sp):
            sp.wait_ge(*scattered.at(16 * T))

            def step(v, m):
                if inside(v, SORT_TILES):
                    if some(v - 3):
                        sp.wait_ge(*turned_x.at(v - 3))
                    sp.dma_start(xs[m][:], tile_rows(k.sorted_x, v)).then_inc(x_in[m].sem, 16)
                j = v - 6
                if inside(j, SORT_TILES):
                    sp.wait_ge(*y_out.at(j + 1))
                    sp.dma_start(tile_rows(k.sorted_y, j), ys[(m - 6) % 4][:]).then_inc(stored[(m - 6) % 4].sem, 16)

            steps(sp, step, SORT_TILES, 6)
            for m, t in enumerate(stored):
                sp.wait_ge(*t.at(16 * len(range(m, SORT_TILES, 4))))

        @block.tensor
        def _(pe):
            if first:
                pe.wait_ge(*loaded_w.at(144))

            W1, W2 = (t[:].rearrange("p e f -> p (e f)") for t in (k.W1, k.W2))

            column = [pe.alloc_register(f"{name}_column{m}") for m in range(4)]
            weights = lambda m: pe.snap(column[m], min_val=0, max_val=(E3 - 1) * F3)

            def step(v, m):
                j = v
                if inside(j, SORT_TILES):
                    pe.wait_ge(*x_in[m].at(rounds(v, m)))
                    if some(j - 1):
                        pe.wait_ge(*x_out.at(j - 1))
                    nc.tensor.transpose(psX[m % 2][:, 0:P], xs[m][:], k.ident[:]).then_inc(turned_x.sem, 1)
                j, b = v - 1, (m - 1) % 2
                if inside(j, SORT_TILES):
                    pe.reg_load(column[(m - 1) % 4], tile_expert[0:1, bass.ds(j, 1)])
                    e = weights((m - 1) % 4)
                    pe.wait_ge(*x_out.at(j + 1))
                    if some(j - 1):
                        pe.wait_ge(*silu_done.at(j - 1))
                    nc.tensor.matmul(psH[b][:], xT[b][:], W1[:, bass.ds(e, F3)],
                                     start=True, stop=True).then_inc(up_done.sem, 1)
                j, b = v - 2, (m - 2) % 2
                if inside(j, SORT_TILES):
                    pe.wait_ge(*silu_done.at(j + 1))
                    if some(j - 1):
                        pe.wait_ge(*h_out.at(j - 1))
                    for c in range(C):
                        i = nc.tensor.transpose(psT[b][:, c * P:(c + 1) * P], h[b][:, c * P:(c + 1) * P], k.ident[:])
                    i.then_inc(turned_h.sem, 1)
                j, b = v - 3, (m - 3) % 2
                if inside(j, SORT_TILES):
                    e = weights((m - 3) % 4)
                    pe.wait_ge(*h_out.at(j + 1))
                    if some(j - 1):
                        pe.wait_ge(*y_out.at(j - 1))
                    for c in range(C):
                        i = nc.tensor.matmul(psY[b][:, 0:D], hT[b][:, c * P:(c + 1) * P],
                                             W2[:, bass.ds(e + c * D, D)],
                                             start=(c == 0), stop=(c == C - 1))
                    i.then_inc(down_done.sem, 1)

            steps(pe, step, SORT_TILES, 3)

        @block.scalar
        def _(act):
            def step(v, m):
                j, b = v - 1, (m - 1) % 2
                if inside(j, SORT_TILES):
                    act.wait_ge(*up_done.at(j + 1))
                    nc.scalar.activation(h[b][:], psH[b][:], ACT.Silu).then_inc(silu_done.sem, 1)
                j, b = v - 3, (m - 3) % 2
                if inside(j, SORT_TILES):
                    act.wait_ge(*down_done.at(j + 1))
                    q = (m - 3) % 4
                    if some(rounds(j, q, off=1)):
                        act.wait_ge(*stored[q].at(rounds(j, q, off=1)))
                    nc.scalar.activation(ys[q][:], psY[b][:, 0:D], ACT.Copy).then_inc(y_out.sem, 1)

            steps(act, step, SORT_TILES, 3)

        @block.vector
        def _(dve):
            def step(v, m):
                j = v
                if inside(j, SORT_TILES):
                    dve.wait_ge(*turned_x.at(j + 1))
                    nc.vector.tensor_copy(xT[m % 2][:], psX[m % 2][:, 0:P]).then_inc(x_out.sem, 1)
                j, b = v - 2, (m - 2) % 2
                if inside(j, SORT_TILES):
                    dve.wait_ge(*turned_h.at(j + 1))
                    nc.vector.tensor_copy(hT[b][:], psT[b][:]).then_inc(h_out.sem, 1)

            steps(dve, step, SORT_TILES, 2)
    scattered.close(16 * T)
    for m in range(4):
        x_in[m].close(16 * len(range(m, SORT_TILES, 4)))
        stored[m].close(16 * len(range(m, SORT_TILES, 4)))
    for t in (turned_x, x_out, up_done, silu_done, turned_h, h_out, down_done, y_out):
        t.close(SORT_TILES)
    if first:
        loaded_w.close(144)
        zeroed.close(16)


def gather_stage(k, name, G, Y, weight, slot, w_r=None, psL=None):
    nc = k.nc
    last = psL is None
    weighed, turned, copied = (k.tally(n) for n in ("weighed", "turned", "copied"))
    gathered = [k.tally(f"gathered{g}") for g in range(4)]
    with nc.psum_tensor(f"{name}_psY", [P, 4, 512], F32) as ps, nc.Block() as block:
        @block.gpsimd
        def _(pool):
            for t in range(T):
                pool.indirect_dma_start(G[:, t, :], None, k.sorted_y, bass.IndirectOffsetOnAxis(slot[:, t:t + 1], 0))\
                    .then_inc(gathered[t // 4].sem, 16)

        @block.vector
        def _(dve):
            for g in range(4):
                dve.wait_ge(*gathered[g].at(64))
                for t in range(4 * g, 4 * g + 4):
                    if last:
                        m = nc.vector.scalar_tensor_tensor(out=k.X[:, t, :], in0=G[:, t, :], scalar=weight[:, t:t + 1],
                                                           in1=k.X[:, t, :], op0=ALU.mult, op1=ALU.add)
                    else:
                        m = nc.vector.tensor_scalar(Y[:, t, :], G[:, t, :], weight[:, t:t + 1], None, ALU.mult)
                m.then_inc(weighed.sem, 1)

        if not last:
            @block.tensor
            def _(pe):
                def route(g):
                    pe.wait_ge(*copied.at(g + 1))
                    for t in range(4 * g, 4 * g + 4):
                        nc.tensor.matmul(psL[:, t, :], k.XT[:, t * P:(t + 1) * P], w_r, start=True, stop=True)

                for g in range(4):
                    pe.wait_ge(*weighed.at(g + 1))
                    for j in range(4):
                        m = nc.tensor.transpose(ps[:, g, j * P:(j + 1) * P], Y[:, 4 * g + j, :], k.ident[:])
                    m.then_inc(turned.sem, 1)
                    if g:
                        route(g - 1)
                route(3)

            @block.scalar
            def _(act):
                for g in range(4):
                    act.wait_ge(*turned.at(g + 1))
                    nc.scalar.activation(k.XT[:, g * 512:(g + 1) * 512], ps[:, g, :], ACT.Copy).then_inc(copied.sem, 1)
    for t in gathered:
        t.close(64)
    weighed.close(4)
    if not last:
        turned.close(4)
        copied.close(4)


def moe_l3_stage(k, a):
    nc = k.nc
    with ExitStack() as s:
        sb = lambda n, shape, dt=F32: s.enter_context(nc.sbuf_tensor(f"m3_{n}", shape, dt))
        G, Y, weight = sb("G", [P, T, D]), sb("Y", [P, T, D]), sb("weight", [P, T])
        slot, tile_expert = sb("slot", [P, T], mybir.dt.uint32), sb("tile_expert", [1, SORT_TILES], mybir.dt.int32)

        def route(layer, psL=None):
            route_stage(k, f"m3{layer}", None, None, E3, top=1, of_probs=True, renormed=False,
                        sort=(weight, slot, tile_expert), psL=psL)

        route(0)
        k.close_logits()
        for layer in range(LAYERS):
            sorted_experts_stage(k, f"m3{layer}", Y if layer else k.X, slot, tile_expert, layer == 0)
            if layer + 1 < LAYERS:
                with nc.psum_tensor(f"m3{layer}_logits", [P, T, E3], F32) as psL:
                    gather_stage(k, f"m3{layer}", G, Y, weight, slot, k.routers[:, layer + 1, :], psL)
                    route(layer + 1, psL)
            else:
                gather_stage(k, f"m3{layer}", G, Y, weight, slot)


def inverse_root(nc, dve, out, root, v, scratch):
    nc.vector.reciprocal(out, root)
    dve.drain()
    nc.vector.tensor_tensor(scratch, out, out, ALU.mult)
    dve.drain()
    nc.vector.tensor_tensor(scratch, scratch, v, ALU.mult)
    dve.drain()
    nc.vector.tensor_scalar(scratch, scratch, -0.5, 1.5, ALU.mult, ALU.add)
    dve.drain()
    nc.vector.tensor_tensor(out, out, scratch, ALU.mult)
    dve.drain()


CH = 32
DHEADS = D // CH
UN = N // CH
CPS = SEQ // CH
PE_TAPS = 22
POOL_TAPS = 18
LONG, SHORT, CONV = 64, 5, 4
EPS_L2 = 1e-6
FLOOR = 0.02



def delta_stage(k, a):
    nc = k.nc
    with ExitStack() as s:
        sb = lambda n, shape: s.enter_context(nc.sbuf_tensor(f"de_{n}", shape, F32))
        f = {n: sb(n, [P, N]) for n in (
            "qT", "kT", "short", "long", "qH", "kH", "vH", "sq", "kbH", "vbH", "attn", "delta")}
        pads = [sb(f"pad{i}", [P, BATCH, SEQ + CONV - 1]) for i in range(3)]
        vpad = sb("vpad", [P, BATCH, SEQ + LONG - 1])
        r1, r2, r3 = (t[:].rearrange("p b s -> p (b s)")[:, 0:N] for t in pads)
        w = {n: sb(n, [P, D]) for n in ("Wq", "Wk", "Wv", "Wxg", "Wg1x", "Wg1s", "Wg2", "Wo")}
        w["Wog1x"], w["Wog1s"], w["Wog2"] = sb("Wog1x", [P, D // 2]), sb("Wog1s", [P, D // 2]), sb("Wog2", [D // 2, D])
        taps = sb("taps", [P, 3 * CONV + SHORT + LONG])
        cols = sb("cols", [P, 6])
        rows = sb("rows", [P, 5])
        delta_filters(k, a, f, pads, vpad, w, taps, cols, rows)
        v = vpad[:, :, LONG - 1:]
        small = {n: sb(n, [P, UN]) for n in ("beta", "res", "ssk", "ssq", "rt", "rk", "rq", "t0")}
        sums = {n: sb(n, [P, 4, UN]) for n in ("sum", "abs", "square")}
        delta_heads(k, f, v, w, cols, small, r1, r2, r3)
        delta_scan(k, f, sums, r1, r2, r3)
        delta_gate(k, f, w, cols, rows, small, sums, r1, r2, r3)
        project_and_add_stage(k, "de", None, r1, w["Wo"])


def delta_filters(k, a, f, pads, vpad, w, taps, cols, rows):
    nc = k.nc
    w_in, made, projected, padded, convd, silud, longed, diags, tapped, part_done = (
        k.tally(f"df_{n}") for n in ("w_in", "made", "projected", "padded", "convd", "silud", "longed", "diags",
                                     "tapped", "part_done"))
    T0 = 3 * CONV
    T1 = T0 + SHORT
    products = (f["vbH"], f["attn"])
    with nc.sbuf_tensor("df_diag", [P, PE_TAPS, P], F32) as diag, nc.psum_tensor("df_ps", [P, 2, 4, 512], F32) as ps, \
            nc.Block() as block:
        ahead = CONV - 1

        @block.sync
        def _(sp):
            for n in ("Wv", "Wq", "Wk"):
                sp.dma_start(w[n][:], a[f"L1_attn_{n}"]).then_inc(w_in.sem, 16)
            sp.dma_start(taps[:], a["L1_attn_taps"]).then_inc(w_in.sem, 16)
            rest = [(w[n], a[f"L1_attn_{n}"]) for n in
                    ("Wxg", "Wg1x", "Wg1s", "Wg2", "Wo", "Wog1x", "Wog1s", "Wog2", "cols")
                    if n != "cols"] + [(cols, a["L1_attn_cols"]), (rows, a["L1_attn_rows"].partition_broadcast(P))]
            for t, d in rest:
                sp.dma_start(t[:], d).then_inc(w_in.sem, 16)
            sp.wait_ge(*w_in.at(16 * (4 + len(rest))))

        @block.gpsimd
        def _(pool):
            for t in pads:
                nc.gpsimd.memset(t[:, :, 0:ahead], 0.0)
            nc.gpsimd.memset(vpad[:, :, 0:LONG - 1], 0.0).then_inc(made.sem, 1)
            pool.wait_ge(*w_in.at(16 * 14))
            for j in range(PE_TAPS):
                nc.gpsimd.tensor_scalar(diag[:, j, :], k.ident[:], taps[:, T1 + j:T1 + j + 1], None, ALU.mult)\
                    .then_inc(diags.sem, 1)
            for j in range(1, POOL_TAPS):
                pool.wait_ge(*tapped.at(j + 1))
                if j > 1:
                    pool.wait_ge(*part_done.at(j - 1))
                nc.gpsimd.tensor_tensor(f["kbH"][:], products[(j - 1) % 2][:], f["kbH"][:], ALU.add)\
                    .then_inc(part_done.sem, 1)

        @block.tensor
        def _(pe):
            pe.wait_ge(*w_in.at(16 * 14))
            for i, n in enumerate(("Wv", "Wq", "Wk")):
                if i == 2:
                    pe.wait_ge(*padded.at(1))
                for g in range(4):
                    m = nc.tensor.matmul(ps[:, i % 2, g, :], w[n][:], k.XT[:, g * 512:(g + 1) * 512],
                                         start=True, stop=True)
                m.then_inc(projected.sem, 1)
            pe.wait_ge(*padded.at(2))
            pe.wait_ge(*silud.at(1))
            pe.wait_ge(*diags.at(PE_TAPS))
            for g in range(4):
                for j in range(PE_TAPS):
                    m = nc.tensor.matmul(ps[:, 1, g, :], diag[:, j, :], vpad[:, 2 * g:2 * g + 2, j:j + SEQ],
                                         start=(j == 0), stop=(j == PE_TAPS - 1))
            m.then_inc(longed.sem, 1)

        @block.scalar
        def _(act):
            for i in range(3):
                act.wait_ge(*projected.at(i + 1))
                nc.scalar.activation(pads[(i + 2) % 3][:, :, ahead:], ps[:, i % 2, :, :].rearrange(
                    "p g (b s) -> p (g b) s", s=SEQ), ACT.Copy).then_inc(padded.sem, 1)
            outs = (vpad[:, :, LONG - 1:], f["qT"][:].rearrange("p (b s) -> p b s", b=BATCH),
                    f["kT"][:].rearrange("p (b s) -> p b s", b=BATCH))
            srcs = (f["sq"], f["qH"], f["kH"])
            act.wait_ge(*made.at(1))

            def activate(i):
                act.wait_ge(*convd.at(i + 1))
                nc.scalar.activation(outs[i], srcs[i][:].rearrange("p (b s) -> p b s", b=BATCH), ACT.Silu)\
                    .then_inc(silud.sem, 1)

            activate(0)
            act.drain()
            for j in range(POOL_TAPS):
                if j in (4, 8):
                    activate(j // 4)
                if j >= 3:
                    act.wait_ge(*part_done.at(j - 2))
                x, t = vpad[:, :, PE_TAPS + j:PE_TAPS + j + SEQ], taps[:, T1 + PE_TAPS + j:T1 + PE_TAPS + j + 1]
                out = products[(j - 1) % 2] if j else f["kbH"]
                nc.scalar.activation(out[:].rearrange("p (b s) -> p b s", b=BATCH), x, ACT.Copy, scale=t)\
                    .then_inc(tapped.sem, 1)

        @block.vector
        def _(dve):
            def fir(out, src, first, n, start):
                o = out[:].rearrange("p (b s) -> p b s", b=BATCH)
                for j in range(n):
                    x, t = src[:, :, start + j:start + j + SEQ], taps[:, first + j:first + j + 1]
                    if j == 0:
                        m = nc.vector.tensor_scalar(o, x, t, None, ALU.mult)
                    else:
                        dve.drain()
                        m = nc.vector.scalar_tensor_tensor(out=o, in0=x, scalar=t, in1=o, op0=ALU.mult, op1=ALU.add)
                return m

            dve.wait_ge(*w_in.at(16 * 14))
            dve.wait_ge(*made.at(1))
            for i, (tile, pad) in enumerate(((f["sq"], pads[2]), (f["qH"], pads[0]), (f["kH"], pads[1]))):
                dve.wait_ge(*padded.at(i + 1))
                fir(tile, pad, CONV * ((i + 2) % 3), CONV, 0).then_inc(convd.sem, 1)
            dve.wait_ge(*silud.at(1))
            fir(f["short"], vpad, T0, SHORT, LONG - SHORT)
            fir(f["long"], vpad, T1 + PE_TAPS + POOL_TAPS, LONG - PE_TAPS - POOL_TAPS, PE_TAPS + POOL_TAPS)
            dve.wait_ge(*longed.at(1))
            dve.drain()
            l = f["long"][:]
            nc.vector.tensor_tensor(l, l, ps[:, 1, :, :].rearrange("p g c -> p (g c)"), ALU.add)
            dve.drain()
            dve.wait_ge(*part_done.at(POOL_TAPS - 1))
            nc.vector.tensor_tensor(l, l, f["kbH"][:], ALU.add)


def delta_heads(k, f, v, w, cols, small, r1, r2, r3):
    nc = k.nc
    gates, gout, turned, squared, summed, rooted, asked, sig = (
        k.tally(f"dh_{n}") for n in ("gates", "gout", "turned", "squared", "summed", "rooted", "asked", "sig"))
    H = lambda ap: ap.rearrange("p (u d) -> p u d", d=CH)
    bc = lambda t: t[:].unsqueeze(2).to_broadcast([P, UN, CH])
    with nc.psum_tensor("dh_ps", [P, 4, 512], F32) as ps, nc.Block() as block:
        @block.tensor
        def _(pe):
            for g in range(4):
                m = nc.tensor.matmul(ps[:, g, :], w["Wxg"][:], k.XT[:, g * 512:(g + 1) * 512], start=True, stop=True)
            m.then_inc(gates.sem, 1)

        @block.scalar
        def _(act):
            act.wait_ge(*gates.at(1))
            nc.scalar.activation(r3, ps[:].rearrange("p g c -> p (g c)"), ACT.Copy).then_inc(gout.sem, 1)
            for i, n in enumerate(("qH", "kH")):
                act.wait_ge(*turned.at(i + 1))
                if i == 1:
                    act.wait_ge(*summed.at(1))
                nc.scalar.activation(f["sq"][:], f[n][:], ACT.Square).then_inc(squared.sem, 1)
            for i, (t, o) in enumerate((("ssq", "rt"), ("ssk", "t0"))):
                act.wait_ge(*asked.at(1))
                m = nc.scalar.activation(small[o][:], small[t][:], ACT.Sqrt)
            m.then_inc(rooted.sem, 1)
            act.wait_ge(*turned.at(3))
            g = r2.rearrange("p (u s) -> p u s", s=CH)
            nc.scalar.activation(small["beta"][:], g[:, :, 0], ACT.Sigmoid)
            nc.scalar.activation(small["res"][:], g[:, :, 1], ACT.Sigmoid, bias=cols[:, 0:1]).then_inc(sig.sem, 1)

        @block.vector
        def _(dve):
            nc.vector.transpose(f["qH"][:], f["qT"][:]).then_inc(turned.sem, 1)
            nc.vector.transpose(f["kH"][:], f["kT"][:]).then_inc(turned.sem, 1)
            for b in range(BATCH):
                nc.vector.transpose(f["vH"][:, b * SEQ:(b + 1) * SEQ], v[:, b, :])
            dve.wait_ge(*gout.at(1))
            nc.vector.transpose(r2, r3).then_inc(turned.sem, 1)
            for i, n in enumerate(("ssq", "ssk")):
                dve.wait_ge(*squared.at(i + 1))
                m = nc.vector.tensor_reduce(small[n][:], H(f["sq"][:]), AX.X, ALU.add)
                m.then_inc(summed.sem, 1)
                dve.drain()
                m = nc.vector.tensor_scalar(small[n][:], small[n][:], EPS_L2, None, ALU.add)
            m.then_inc(asked.sem, 1)
            dve.wait_ge(*rooted.at(1))
            for ss, rt, r in (("ssq", "rt", "rq"), ("ssk", "t0", "rk")):
                inverse_root(nc, dve, small[r][:], small[rt][:], small[ss][:], small[rt][:])
            nc.vector.tensor_tensor(H(f["qH"][:]), H(f["qH"][:]), bc(small["rq"]), ALU.mult)
            nc.vector.tensor_tensor(H(f["kH"][:]), H(f["kH"][:]), bc(small["rk"]), ALU.mult)
            dve.wait_ge(*sig.at(1))
            nc.vector.tensor_tensor(H(f["vbH"][:]), H(f["vH"][:]), bc(small["beta"]), ALU.mult)
            dve.drain()
            nc.vector.tensor_tensor(H(f["kbH"][:]), H(f["kH"][:]), bc(small["beta"]), ALU.mult)
            nc.vector.transpose(f["qT"][:], f["qH"][:])
            nc.vector.transpose(f["kT"][:], f["kH"][:])
            dve.drain()
            nc.vector.transpose(r1, f["kbH"][:])
    gates.close(1); gout.close(1); turned.close(3); squared.close(2); summed.close(2)
    rooted.close(1); asked.close(1); sig.close(1)


def delta_scan(k, f, sums, r1, r2, r3):
    nc = k.nc
    blocked, staged, multiplied, masked, opened, begun = (
        k.tally(f"ds_{n}") for n in ("blocked", "staged", "multiplied", "masked", "opened", "begun"))
    with ExitStack() as s:
        sb = lambda n, shape: s.enter_context(nc.sbuf_tensor(f"ds_{n}", shape, F32))
        now = [{n: sb(f"{n}{q}", [P, BATCH, CH]) for n in ("kbT", "kT", "qT", "kH", "U", "attn")} for q in range(2)]
        strict, incl = sb("strict", [P, CH]), sb("incl", [P, CH])
        tmp = sb("tmp", [P, 2, CH * CH // 4 + CH])
        state, r, u2 = (sb(n, [P, BATCH, CH]) for n in ("state", "r", "u2"))
        squares = [sb(f"squares{q}", [P, 3, BATCH, CH]) for q in range(2)]
        parts = ((0, f["sq"][:]), (1, r3), (3, f["vH"][:]))
        unit = lambda t, j, n: t[:, j, :].rearrange("p (b n) -> p b n", n=CPS)[:, :, bass.ds(n, 1)]\
            .rearrange("p b a -> p (b a)")
        at = lambda t, n: t.rearrange("p (b n i) -> p b n i", b=BATCH, n=CPS)[:, :, bass.ds(n, 1), :]\
            .rearrange("p b a i -> p b (a i)")
        src = {"kbT": r1, "kT": f["kT"][:], "qT": f["qT"][:], "kH": f["kH"][:], "U": r2, "attn": f["attn"][:]}

        def stage(copy, name, n, q):
            return copy(now[q][name][:], at(src[name], n))

        def products(out, weights, x):
            nc.tensor.sem_inc(begun.sem, 1)
            for b in range(BATCH):
                for h in range(DHEADS):
                    p = slice(CH * h, CH * (h + 1))
                    m = nc.tensor.matmul(out[p, b * CH:(b + 1) * CH], weights[p, b, :], x(p, b), start=True, stop=True)
            return m

        def chunks(eng, body):
            with eng.Fori(0, CPS // 2 - 1) as i:
                for q in range(2):
                    body(i * 2 + q, q, True)
            body(CPS - 2, 0, True)
            body(CPS - 1, 1, False)

        def m3(t):
            return t[:].unsqueeze(1).to_broadcast([P, BATCH, CH])

        with ExitStack() as pc:
            psA, psB = ([pc.enter_context(nc.psum_tensor(f"ds_ps{n}{q}", [P, 512], F32)) for q in range(2)]
                        for n in "AB")
            block = pc.enter_context(nc.Block())
            b3 = lambda t: t[:, 0:BATCH * CH].rearrange("p (b c) -> p b c", c=CH)
            of = lambda t: lambda p, b: t[p, b, :]

            @block.gpsimd
            def _(pool):
                for h in range(DHEADS):
                    p = slice(CH * h, CH * (h + 1))
                    nc.gpsimd.affine_select(out=strict[p, :], in_=k.ones[p, 0:CH], compare_op=ALU.is_ge, fill=0.0,
                                            base=-1, pattern=[[-1, CH]], channel_multiplier=1)
                    m = nc.gpsimd.affine_select(out=incl[p, :], in_=k.ones[p, 0:CH], compare_op=ALU.is_ge, fill=0.0,
                                                base=0, pattern=[[1, CH]], channel_multiplier=-1)
                m.then_inc(masked.sem, 1)

            @block.scalar
            def _(act):
                def body(n, q, follows):
                    act.wait_ge(*multiplied.at(n + 1))
                    stage(nc.scalar.copy, "kT", n, q)
                    stage(nc.scalar.copy, "qT", n, q).then_inc(staged.sem, 1)

                chunks(act, body)

            @block.tensor
            def _(pe):
                pe.sem_inc(multiplied.sem, 2)

                def body(n, q, follows):
                    pe.wait_ge(*blocked.at(n + 1))
                    pe.wait_ge(*staged.at(n + 1))
                    pe.wait_ge(*opened.at(n + 1))
                    products(psA[q], now[q]["kbT"], of(now[q]["kT"]))
                    products(psB[q], now[q]["kT"], of(now[q]["qT"])).then_inc(multiplied.sem, 1)

                chunks(pe, body)

            @block.vector
            def _(dve):
                dve.sem_inc(opened.sem, 2)
                stage(nc.vector.tensor_copy, "kbT", 0, 0).then_inc(blocked.sem, 1)
                dve.wait_ge(*masked.at(1))

                def body(n, q, follows):
                    if follows:
                        dve.wait_ge(*multiplied.at(n + 2))
                        stage(nc.vector.tensor_copy, "kbT", n + 1, 1 - q).then_inc(blocked.sem, 1)
                    dve.wait_ge(*multiplied.at(n + 3))
                    nc.vector.tensor_tensor(at(r3, n), b3(psA[q]), m3(strict), ALU.mult)
                    nc.vector.tensor_tensor(at(f["attn"][:], n), b3(psB[q]), m3(incl), ALU.mult)\
                        .then_inc(opened.sem, 1)

                chunks(dve, body)
                dve.drain()
                nc.vector.transpose(r2.rearrange("p (g j i) -> p g j i", g=2, j=CH),
                                    r3.rearrange("p (g u j) -> p g j u", g=2, j=CH))
                Tm = f["sq"][:].rearrange("p (g i c) -> p g i c", g=2, i=CH)
                L = r2.rearrange("p (g j i) -> p g j i", g=2, j=CH)
                nc.vector.memset(f["sq"][:], 0.0)
                dve.drain()
                nc.vector.memset(f["sq"][:].rearrange("p (g x) -> p g x", g=2)[:, :, 0:CH * CH:CH + 1], 1.0)
                dve.drain()
                for j in range(CH - 1):
                    ni, nk = CH - 1 - j, j + 1
                    t = tmp[:, :, 0:ni * nk].rearrange("p g (i c) -> p g i c", c=nk)
                    nc.vector.tensor_tensor(t, L[:, :, j, j + 1:].unsqueeze(3).to_broadcast([P, 2, ni, nk]),
                                            Tm[:, :, j:j + 1, 0:nk].to_broadcast([P, 2, ni, nk]), ALU.mult)
                    dve.drain()
                    rows = Tm[:, :, j + 1:, 0:nk]
                    nc.vector.tensor_tensor(rows, rows, t, ALU.subtract)
                    dve.drain()
                nc.vector.transpose(r2.rearrange("p (g u i) -> p g i u", g=2, i=CH),
                                    f["sq"][:].rearrange("p (g i c) -> p g i c", g=2, i=CH))

        (staged_k, staged_p, staged_d, carried, asked, copied, less, solved, solved_out, read, added,
         out_done, summed) = (k.tally(f"dt_{n}") for n in
                              ("staged_k", "staged_p", "staged_d", "carried", "asked", "copied", "less", "solved",
                               "solved_out", "read", "added", "out_done", "summed"))
        with ExitStack() as pc:
            ps1, ps2, ps3, ps4, ps5 = (pc.enter_context(nc.psum_tensor(f"dt_ps{i}", [P, 512], F32))
                                       for i in range(1, 6))
            block = pc.enter_context(nc.Block())

            @block.gpsimd
            def _(pool):
                stage(nc.gpsimd.tensor_copy, "attn", 0, 0).then_inc(staged_p.sem, 1)

                def body(n, q, follows):
                    if follows:
                        pool.wait_ge(*summed.at(n + 1))
                        stage(nc.gpsimd.tensor_copy, "attn", n + 1, 1 - q).then_inc(staged_p.sem, 1)

                chunks(pool, body)

            @block.scalar
            def _(act):
                stage(nc.scalar.copy, "kbT", 0, 0)
                stage(nc.scalar.copy, "qT", 0, 0).then_inc(staged_k.sem, 1)

                def body(n, q, follows):
                    if follows:
                        stage(nc.scalar.copy, "kbT", n + 1, 1 - q)
                        stage(nc.scalar.copy, "qT", n + 1, 1 - q).then_inc(staged_k.sem, 1)
                    act.wait_ge(*solved.at(n + 1))
                    nc.scalar.copy(u2[:], b3(ps2)).then_inc(solved_out.sem, 1)
                    act.wait_ge(*asked.at(n + 1))
                    nc.scalar.copy(at(f["delta"][:], n), b3(ps3)).then_inc(copied.sem, 1)

                chunks(act, body)

            @block.tensor
            def _(pe):
                def body(n, q, follows):
                    pe.wait_ge(*added.at(n + 1))
                    pe.wait_ge(*staged_k.at(n + 1))
                    products(ps1, now[q]["kbT"], of(state)).then_inc(carried.sem, 1)
                    pe.wait_ge(*copied.at(n + 1))
                    products(ps3, now[q]["qT"], of(state)).then_inc(asked.sem, 1)
                    pe.wait_ge(*staged_d.at(n + 1))
                    pe.wait_ge(*less.at(n + 1))
                    products(ps2, now[q]["U"], of(r)).then_inc(solved.sem, 1)
                    pe.wait_ge(*solved_out.at(n + 1))
                    products(ps4, now[q]["kH"], of(u2)).then_inc(read.sem, 1)
                    pe.wait_ge(*staged_p.at(n + 1))
                    pe.wait_ge(*summed.at(n + 1))
                    products(ps5, now[q]["attn"], of(u2)).then_inc(out_done.sem, 1)

                pe.sem_inc(copied.sem, 1)
                pe.sem_inc(summed.sem, 1)
                chunks(pe, body)

            @block.vector
            def _(dve):
                nc.vector.memset(state[:], 0.0).then_inc(added.sem, 1)
                stage(nc.vector.tensor_copy, "U", 0, 0)
                stage(nc.vector.tensor_copy, "kH", 0, 0).then_inc(staged_d.sem, 1)
                nc.vector.transpose(f["sq"][:], f["short"][:])
                nc.vector.transpose(r3, f["long"][:])
                dve.drain()

                def body(n, q, follows):
                    dve.wait_ge(*carried.at(n + 1))
                    nc.vector.tensor_tensor(r[:], at(f["vbH"][:], n), b3(ps1), ALU.subtract).then_inc(less.sem, 1)
                    if follows:
                        stage(nc.vector.tensor_copy, "U", n + 1, 1 - q)
                        stage(nc.vector.tensor_copy, "kH", n + 1, 1 - q).then_inc(staged_d.sem, 1)
                    for i, (_, x) in enumerate(parts):
                        nc.vector.tensor_tensor(squares[q][:, i], at(x, n), at(x, n), ALU.mult)
                    dve.wait_ge(*read.at(n + 1))
                    nc.vector.tensor_tensor(state[:], state[:], b3(ps4), ALU.add).then_inc(added.sem, 1)
                    dve.wait_ge(*copied.at(n + 2))
                    dve.wait_ge(*out_done.at(n + 1))
                    o = at(f["delta"][:], n)
                    nc.vector.tensor_tensor(o, b3(ps5), o, ALU.add).then_inc(summed.sem, 1)
                    dve.drain()
                    for i, (j, x) in enumerate(parts):
                        nc.vector.tensor_reduce(unit(sums["sum"], j, n), at(x, n), AX.X, ALU.add)
                        nc.vector.tensor_reduce(unit(sums["abs"], j, n), at(x, n), AX.X, ALU.add,
                                                apply_absolute_value=True)
                        nc.vector.tensor_reduce(unit(sums["square"], j, n), squares[q][:, i], AX.X, ALU.add)

                chunks(dve, body)


def delta_gate(k, f, w, cols, rows, small, sums, r1, r2, r3):
    nc = k.nc
    H = lambda ap: ap.rearrange("p (u d) -> p u d", d=CH)
    with ExitStack() as s:
        sb = lambda n, shape: s.enter_context(nc.sbuf_tensor(f"dg_{n}", shape, F32))
        Z = sb("Z", [P, UN, CH])
        l2 = sb("l2", [P, 4, UN])
        su, t1 = sb("su", [P, UN]), sb("t1", [P, UN])
        squared = sb("squared", [P, 4, UN])
        lg, pr = sb("lg", [P, UN, 4]), sb("pr", [P, UN, 4])
        one = sb("one", [P, 4])
        og, fac = sb("og", [P, UN]), sb("fac", [P, UN])
        sqd, ask, rt, zt, hid, gel, lgt, lgc, asko, cons = (k.tally(f"dg_{n}") for n in (
            "squared", "roots_asked", "roots_taken", "stats_turned", "hidden", "activated", "logits", "logits_copied",
            "gate_asked", "constants"))
        hpart = {"short": f["sq"][:], "long": r3, "delta": f["delta"][:], "v": f["vH"][:]}
        ZT = f["qT"][:]
        G = f["kT"]
        o = f["qH"][:]
        tmp = f["kbH"][:]

        ss = sums["square"]
        column = lambda i, parts: Z[:, :, i:4 * parts:4].rearrange("p u j -> p j u")

        def sum_up(dve, x, j, squares):
            nc.vector.tensor_reduce(sums["sum"][:, j, :], H(x), AX.X, ALU.add)
            nc.vector.tensor_reduce(sums["abs"][:, j, :], H(x), AX.X, ALU.add, apply_absolute_value=True)
            dve.wait_ge(*sqd.at(squares))
            nc.vector.tensor_reduce(ss[:, j, :], H(r2), AX.X, ALU.add)
            dve.drain()

        def stats(dve, parts):
            nc.vector.tensor_scalar(column(0, parts), sums["sum"][:, 0:parts], 1.0 / D, None, ALU.mult)
            nc.vector.tensor_scalar(column(2, parts), sums["abs"][:, 0:parts], 1.0 / D, None, ALU.mult)
            t = squared[:, 0:parts]
            nc.vector.tensor_tensor(t, sums["sum"][:, 0:parts], sums["sum"][:, 0:parts], ALU.mult)
            dve.drain()
            nc.vector.tensor_scalar(t, t, -1.0 / (D * CH), None, ALU.mult)
            dve.drain()
            m = nc.vector.scalar_tensor_tensor(out=column(1, parts), in0=ss[:, 0:parts], scalar=1.0 / D, in1=t,
                                               op0=ALU.mult, op1=ALU.add)
            dve.drain()
            return m

        with nc.psum_tensor("dg_ps", [P, 4, 512], F32) as ps, nc.psum_tensor("dg_ps2", [P, 4, 512], F32) as ps2, \
                nc.Block() as block:
            @block.vector
            def _(dve):
                nc.vector.memset(Z[:], 0.0)
                sum_up(dve, f["delta"][:], 2, 1)
                stats(dve, 4).then_inc(ask.sem, 1)
                dve.wait_ge(*rt.at(1))
                nc.vector.tensor_scalar(column(3, 4), l2[:], 1.0 / DHEADS, None, ALU.mult)
                dve.drain()
                nc.vector.transpose(ZT, Z[:].rearrange("p u s -> p (u s)")).then_inc(zt.sem, 1)
                dve.wait_ge(*lgc.at(1))
                nc.vector.transpose(o, tmp)
                dve.drain()
                dve.wait_ge(*cons.at(1))
                nc.vector.tensor_scalar(one[:, 2:3], rows[:, 4:5], 0.0, None, ALU.max)
                dve.drain()
                nc.vector.tensor_tensor(one[:, 2:3], one[:, 2:3], one[:, 1:2], ALU.add)
                dve.drain()
                nc.vector.reciprocal(one[:, 3:4], one[:, 2:3])
                nc.vector.tensor_tensor(lg[:], H(o)[:, :, 0:4], rows[:, 0:4].unsqueeze(1).to_broadcast([P, UN, 4]),
                                        ALU.add)
                dve.drain()
                nc.vector.tensor_scalar(lg[:], lg[:], one[:, 3:4], None, ALU.mult)
                dve.drain()
                nc.vector.tensor_reduce(su[:], lg[:], AX.X, ALU.max)
                dve.drain()
                b4 = lambda t: t[:].unsqueeze(2).to_broadcast([P, UN, 4])
                nc.vector.tensor_tensor(lg[:], lg[:], b4(su), ALU.subtract).then_inc(ask.sem, 1)
                dve.wait_ge(*rt.at(2))
                for i in range(2):
                    nc.vector.tensor_reduce(su[:], pr[:], AX.X, ALU.add)
                    dve.drain()
                    nc.vector.reciprocal(t1[:], su[:])
                    dve.drain()
                    nc.vector.tensor_tensor(pr[:], pr[:], b4(t1), ALU.mult)
                    dve.drain()
                    if i == 0:
                        nc.vector.tensor_scalar(pr[:], pr[:], FLOOR, None, ALU.max)
                        dve.drain()
                nc.vector.scalar_tensor_tensor(out=pr[:, :, 0], in0=small["res"][:], scalar=one[:, 0:1],
                                               in1=pr[:, :, 0], op0=ALU.mult, op1=ALU.add)
                dve.drain()
                b32 = lambda t: t.unsqueeze(2).to_broadcast([P, UN, CH])
                for j, n in enumerate(("short", "long", "delta", "v")):
                    dst = o if j == 0 else tmp
                    nc.vector.tensor_tensor(H(dst), H(hpart[n]), b32(pr[:, :, j]), ALU.mult)
                    dve.drain()
                    if j:
                        m = nc.vector.tensor_tensor(o, o, tmp, ALU.add)
                        dve.drain()
                m.then_inc(ask.sem, 1)
                sum_up(dve, o, 0, 2)
                stats(dve, 1).then_inc(ask.sem, 1)
                dve.wait_ge(*rt.at(3))
                nc.vector.tensor_scalar(Z[:, :, 3], l2[:, 0, :], 1.0 / DHEADS, None, ALU.mult)
                dve.drain()
                nc.vector.transpose(ZT, Z[:].rearrange("p u s -> p (u s)")).then_inc(zt.sem, 1)
                dve.wait_ge(*lgc.at(2))
                nc.vector.transpose(r2, tmp).then_inc(asko.sem, 1)
                dve.wait_ge(*rt.at(4))
                nc.vector.tensor_tensor(t1[:], og[:], og[:], ALU.mult)
                dve.drain()
                nc.vector.tensor_tensor(t1[:], t1[:], ss[:, 0, :], ALU.mult)
                dve.drain()
                nc.vector.tensor_scalar(t1[:], t1[:], 1.0 / CH, LN_EPS, ALU.mult, ALU.add).then_inc(asko.sem, 1)
                dve.wait_ge(*rt.at(5))
                inverse_root(nc, dve, fac[:], su[:], t1[:], l2[:, 1, :])
                nc.vector.tensor_tensor(fac[:], fac[:], og[:], ALU.mult)
                dve.drain()
                nc.vector.tensor_tensor(H(o), H(o), b32(fac[:]), ALU.mult)
                dve.drain()
                nc.vector.transpose(r1, o)
                nc.vector.tensor_scalar(w["Wo"][:], w["Wo"][:], cols[:, 2:3], None, ALU.mult)

            @block.scalar
            def _(act):
                nc.scalar.activation(one[:, 0:1], cols[:, 1:2], ACT.Sigmoid)
                nc.scalar.activation(one[:, 1:2], rows[:, 4:5], ACT.Abs)
                act.drain()
                nc.scalar.activation(one[:, 1:2], one[:, 1:2], ACT.Exp, scale=-1.0)
                act.drain()
                nc.scalar.activation(one[:, 1:2], one[:, 1:2], ACT.Ln, bias=k.ones[:, 0:1]).then_inc(cons.sem, 1)
                nc.scalar.activation(r2, hpart["delta"], ACT.Square).then_inc(sqd.sem, 1)
                act.wait_ge(*ask.at(1))
                nc.scalar.activation(l2[:], ss[:], ACT.Sqrt).then_inc(rt.sem, 1)
                for g in range(4):
                    act.wait_ge(*hid.at(g + 1))
                    nc.scalar.activation(G[:, g * 512:(g + 1) * 512], ps[:, g, :], ACT.Gelu, bias=cols[:, 3:4])\
                        .then_inc(gel.sem, 1)
                for g in range(4):
                    act.wait_ge(*lgt.at(g + 1))
                    m = nc.scalar.activation(tmp[:, g * 512:(g + 1) * 512], ps2[:, g, :], ACT.Copy)
                m.then_inc(lgc.sem, 1)
                act.wait_ge(*ask.at(2))
                nc.scalar.activation(pr[:], lg[:], ACT.Exp).then_inc(rt.sem, 1)
                act.wait_ge(*ask.at(3))
                nc.scalar.activation(r2, o, ACT.Square).then_inc(sqd.sem, 1)
                act.wait_ge(*ask.at(4))
                nc.scalar.activation(l2[:, 0, :], ss[:, 0, :], ACT.Sqrt).then_inc(rt.sem, 1)
                for g in range(4):
                    act.wait_ge(*hid.at(4 + g + 1))
                    nc.scalar.activation(G[0:D // 2, g * 512:(g + 1) * 512], ps[0:D // 2, g, :], ACT.Gelu,
                                         bias=cols[0:D // 2, 4:5]).then_inc(gel.sem, 1)
                for g in range(4):
                    act.wait_ge(*lgt.at(4 + g + 1))
                    m = nc.scalar.activation(tmp[:, g * 512:(g + 1) * 512], ps2[:, g, :], ACT.Copy)
                m.then_inc(lgc.sem, 1)
                act.wait_ge(*asko.at(1))
                nc.scalar.activation(og[:], H(r2)[:, :, 0], ACT.Sigmoid, bias=cols[:, 5:6]).then_inc(rt.sem, 1)
                act.wait_ge(*asko.at(2))
                nc.scalar.activation(su[:], t1[:], ACT.Sqrt).then_inc(rt.sem, 1)

            @block.tensor
            def _(pe):
                for i, (wx, ws, w2, M) in enumerate((("Wg1x", "Wg1s", "Wg2", P), ("Wog1x", "Wog1s", "Wog2", D // 2))):
                    if i == 1:
                        pe.wait_ge(*lgc.at(1))
                    pe.wait_ge(*zt.at(i + 1))
                    for g in range(4):
                        c = slice(g * 512, (g + 1) * 512)
                        nc.tensor.matmul(ps[0:M, g, :], w[wx][:], k.XT[:, c], start=True, stop=False)
                        nc.tensor.matmul(ps[0:M, g, :], w[ws][:], ZT[:, c], start=False, stop=True)\
                            .then_inc(hid.sem, 1)
                    for g in range(4):
                        pe.wait_ge(*gel.at(4 * i + g + 1))
                        nc.tensor.matmul(ps2[:, g, :], w[w2][:], G[0:M, g * 512:(g + 1) * 512], start=True, stop=True)\
                            .then_inc(lgt.sem, 1)


def retention_stage(k, a):
    nc = k.nc
    w_in, consts, made, projected, turned, gated, asked, rooted, scaled, tail = (
        k.tally(f"re_{n}") for n in
        ("w_in", "consts", "made", "projected", "turned", "gated", "asked", "rooted", "scaled", "tail"))
    with ExitStack() as s:
        sb = lambda n, shape: s.enter_context(nc.sbuf_tensor(f"re_{n}", shape, F32))
        w = {n: sb(n, [P, D]) for n in ("wq", "wv", "wg", "wo")}
        col = sb("col", [P, 3])
        lam = sb("lam", [P, 1])
        decay = sb("decay", [P, BATCH, SEQ])
        state, yT, gate, y2T = (sb(n, [P, N]) for n in ("state", "yT", "gate", "y2T"))
        Y = sb("Y", [P, T, D])
        stats, agg = sb("stats", [P, T, 6]), sb("agg", [P, T, 2])
        vare, root, rstd, scratch = (sb(n, [P, T]) for n in ("vare", "root", "rstd", "scratch"))
        with nc.psum_tensor("re_psQ", [P, N], F32) as psQ, nc.psum_tensor("re_psV", [P, N], F32) as psV, \
                nc.Block() as block:
            @block.sync
            def _(sp):
                sp.dma_start(col[:], a["L2_attn_cols"]).then_inc(consts.sem, 16)
                for n in ("wv", "wq", "wg", "wo"):
                    sp.dma_start(w[n][:], a[f"L2_attn_{n}"]).then_inc(w_in.sem, 16)
                sp.wait_ge(*w_in.at(64))

            @block.tensor
            def _(pe):
                pe.wait_ge(*w_in.at(64))
                for n, ps in (("wv", psV), ("wq", psQ)):
                    for g in range(4):
                        m = nc.tensor.matmul(ps[:, g * 512:(g + 1) * 512], w[n][:], k.XT[:, g * 512:(g + 1) * 512],
                                             start=True, stop=True)
                    m.then_inc(projected.sem, 1)

            @block.scalar
            def _(act):
                act.wait_ge(*consts.at(16))
                nc.scalar.activation(lam[:], col[:, 0:1], ACT.Sigmoid).then_inc(made.sem, 1)

            @block.vector
            def _(dve):
                nc.vector.memset(decay[:], 1.0)
                dve.wait_ge(*made.at(1))
                dve.drain()
                nc.vector.tensor_scalar(decay[:], decay[:], lam[:, 0:1], None, ALU.mult)
                dve.drain()
                nc.vector.memset(decay[:, :, 0:1], 0.0)
                dve.drain()
                dve.wait_ge(*projected.at(1))
                nc.vector.tensor_tensor_scan(state[:], decay[:].rearrange("p b s -> p (b s)"), psV[:], 0.0,
                                             ALU.mult, ALU.add)
                dve.drain()
                dve.wait_ge(*projected.at(2))
                nc.vector.tensor_tensor(yT[:], psQ[:], state[:], ALU.mult)

        with nc.psum_tensor("re_psY", [P, T, D], F32) as psY, nc.psum_tensor("re_psG", [P, 4, 512], F32) as psG, \
                nc.Block() as block:
            @block.tensor
            def _(pe):
                for t in range(T):
                    m = nc.tensor.transpose(psY[:, t, :], yT[:, t * P:(t + 1) * P], k.ident[:])
                    if t % 4 == 3:
                        m.then_inc(turned.sem, 1)
                for g in range(4):
                    nc.tensor.matmul(psG[:, g, :], w["wg"][:], k.XT[:, g * 512:(g + 1) * 512], start=True, stop=True)\
                        .then_inc(gated.sem, 1)

            @block.scalar
            def _(act):
                act.wait_ge(*asked.at(1))
                nc.scalar.activation(root[:], vare[:], ACT.Sqrt).then_inc(rooted.sem, 1)
                for g in range(4):
                    act.wait_ge(*gated.at(g + 1))
                    nc.scalar.activation(gate[:, g * 512:(g + 1) * 512], psG[:, g, :], ACT.Silu)

            @block.vector
            def _(dve):
                for t in range(T):
                    if t % 4 == 0:
                        dve.wait_ge(*turned.at(t // 4 + 1))
                    nc.vector.bn_stats(stats[:, t, :], psY[:, t, :])
                dve.drain()
                for t in range(T):
                    nc.vector.bn_aggr(agg[:, t, :], stats[:, t, :])
                dve.drain()
                nc.vector.tensor_scalar(vare[:], agg[:, :, 1], LN_EPS, None, ALU.add).then_inc(asked.sem, 1)
                dve.wait_ge(*rooted.at(1))
                inverse_root(nc, dve, rstd[:], root[:], vare[:], scratch[:])
                for t in range(T):
                    nc.vector.tensor_scalar(Y[:, t, :], psY[:, t, :], agg[:, t, 0:1], rstd[:, t:t + 1],
                                            ALU.subtract, ALU.mult)

        with nc.psum_tensor("re_psN", [P, 4, 512], F32) as psN, nc.Block() as block:
            @block.tensor
            def _(pe):
                for g in range(4):
                    for j in range(4):
                        m = nc.tensor.transpose(psN[:, g, j * P:(j + 1) * P], Y[:, 4 * g + j, :], k.ident[:])
                    m.then_inc(tail.sem, 1)

            @block.scalar
            def _(act):
                for g in range(4):
                    act.wait_ge(*tail.at(g + 1))
                    nc.scalar.activation(y2T[:, g * 512:(g + 1) * 512], psN[:, g, :], ACT.Identity,
                                         scale=col[:, 1:2], bias=col[:, 2:3]).then_inc(scaled.sem, 1)

            @block.vector
            def _(dve):
                for g in range(4):
                    dve.wait_ge(*scaled.at(g + 1))
                    c = slice(g * 512, (g + 1) * 512)
                    nc.vector.tensor_tensor(y2T[:, c], y2T[:, c], gate[:, c], ALU.mult)
        project_and_add_stage(k, "re", None, y2T, w["wo"])


def lru_stage(k, a):
    nc = k.nc
    w_in, iotad, exped, prepared, sined, projected, scaled, out_done = (
        k.tally(f"lr_{n}") for n in
        ("w_in", "iotad", "exped", "prepared", "sined", "projected", "scaled", "out_done"))
    cleared, aside, scanned = (k.tally(f"lr_{n}") for n in ("cleared", "aside", "scanned"))
    keep_l3_weights(k)
    TURN_HI, TURN_LO = 6.28125, float(2 * np.pi - 6.28125)
    with ExitStack() as s:
        sb = lambda n, shape: s.enter_context(nc.sbuf_tensor(f"lr_{n}", shape, F32))
        w = {n: sb(n, [P, D]) for n in ("Br", "Bi", "Cr", "Ci")}
        col = sb("col", [P, 3])
        nu, th, mag, mag2, gamma, g1 = (sb(n, [P, 1]) for n in ("nu", "th", "mag", "mag2", "gamma", "g1"))
        time, angle, turns, sin, half, cos = (sb(n, [P, SEQ]) for n in ("time", "angle", "turns", "sin", "half", "cos"))
        diag = sb("diag", [P, D])
        decay, br, bi, m1, m2, hr, hi = (sb(n, [P, BATCH, SEQ]) for n in ("decay", "br", "bi", "m1", "m2", "hr", "hi"))
        gr, gi = sb("gr", [P, BATCH, SEQ]), sb("gi", [P, BATCH, SEQ])
        all_seqs = lambda t: t[:].unsqueeze(1).to_broadcast([P, BATCH, SEQ])
        flat = lambda t: t[:].rearrange("p b s -> p (b s)")
        with nc.psum_tensor("lr_psR", [P, N], F32) as psR, nc.psum_tensor("lr_psI", [P, N], F32) as psI, \
                nc.Block() as block:
            @block.sync
            def _(sp):
                sp.dma_start(col[:], a["L3_attn_cols"]).then_inc(w_in.sem, 16)
                for n in w:
                    sp.dma_start(w[n][:], a[f"L3_attn_{n}"]).then_inc(w_in.sem, 16)
                start_l3_loads(k, a, sp, cleared)

            @block.gpsimd
            def _(pool):
                nc.gpsimd.iota(time[:], [[1, SEQ]], base=0, channel_multiplier=0,
                               allow_small_or_imprecise_dtypes=True).then_inc(iotad.sem, 1)
                pool.wait_ge(*sined.at(1))
                pool.wait_ge(*scaled.at(1))
                nc.gpsimd.tensor_tensor(m2[:], br[:], all_seqs(sin), ALU.mult).then_inc(aside.sem, 1)
                pool.wait_ge(*scanned.at(1))
                nc.gpsimd.tensor_tensor(m2[:], bi[:], all_seqs(cos), ALU.mult).then_inc(aside.sem, 1)

            @block.tensor
            def _(pe):
                pe.wait_ge(*w_in.at(80))
                for n, ps in (("Br", psR), ("Bi", psI)):
                    for g in range(4):
                        m = nc.tensor.matmul(ps[:, g * 512:(g + 1) * 512], w[n][:], k.XT[:, g * 512:(g + 1) * 512],
                                             start=True, stop=True)
                    m.then_inc(projected.sem, 1)

            @block.scalar
            def _(act):
                act.wait_ge(*w_in.at(80))
                nc.scalar.activation(nu[:], col[:, 0:1], ACT.Exp)
                nc.scalar.activation(th[:], col[:, 1:2], ACT.Exp)
                act.drain()
                nc.scalar.activation(mag[:], nu[:], ACT.Exp, scale=-1.0)
                nc.scalar.activation(mag2[:], nu[:], ACT.Exp, scale=-2.0).then_inc(exped.sem, 1)
                act.wait_ge(*prepared.at(1))
                nc.scalar.activation(gamma[:], g1[:], ACT.Sqrt)
                act.drain()
                act.wait_ge(*projected.at(1))
                nc.scalar.activation(flat(br), psR[:], ACT.Copy, scale=gamma[:, 0:1])
                act.wait_ge(*projected.at(2))
                nc.scalar.activation(flat(bi), psI[:], ACT.Copy, scale=gamma[:, 0:1]).then_inc(scaled.sem, 1)
                act.wait_ge(*prepared.at(2))
                nc.scalar.activation(sin[:], angle[:], ACT.Sin)
                nc.scalar.activation(half[:], angle[:], ACT.Sin, scale=0.5).then_inc(sined.sem, 1)

            @block.vector
            def _(dve):
                nc.vector.memset(k.zero[:], 0.0).then_inc(cleared.sem, 1)
                dve.wait_ge(*exped.at(1))
                nc.vector.tensor_scalar(g1[:], mag2[:], -1.0, 1.0, ALU.mult, ALU.add)
                dve.drain()
                nc.vector.tensor_scalar(g1[:], g1[:], LN_EPS, None, ALU.add).then_inc(prepared.sem, 1)
                dve.wait_ge(*iotad.at(1))
                nc.vector.tensor_scalar(angle[:], time[:], th[:, 0:1], None, ALU.mult)
                dve.drain()
                nc.vector.tensor_scalar(turns[:], angle[:], float(1 / (2 * np.pi)), ROUND, ALU.mult, ALU.add)
                dve.drain()
                nc.vector.tensor_scalar(turns[:], turns[:], -ROUND, None, ALU.add)
                dve.drain()
                nc.vector.scalar_tensor_tensor(out=angle[:], in0=turns[:], scalar=-TURN_HI, in1=angle[:],
                                               op0=ALU.mult, op1=ALU.add)
                dve.drain()
                nc.vector.scalar_tensor_tensor(out=angle[:], in0=turns[:], scalar=-TURN_LO, in1=angle[:],
                                               op0=ALU.mult, op1=ALU.add)
                dve.drain()
                nc.vector.tensor_scalar(angle[:], angle[:], 3.1415925, -3.1415925, ALU.min, ALU.max)\
                    .then_inc(prepared.sem, 1)
                nc.vector.memset(decay[:], 1.0)
                dve.drain()
                nc.vector.tensor_scalar(decay[:], decay[:], mag[:, 0:1], None, ALU.mult)
                dve.drain()
                nc.vector.memset(decay[:, :, 0:1], 0.0)
                dve.wait_ge(*w_in.at(80))
                nc.vector.tensor_scalar(diag[:], k.ident[:], col[:, 2:3], None, ALU.mult)
                nc.vector.tensor_scalar(w["Ci"][:], w["Ci"][:], -1.0, None, ALU.mult)
                dve.wait_ge(*sined.at(1))
                nc.vector.tensor_tensor(cos[:], half[:], half[:], ALU.mult)
                dve.drain()
                nc.vector.tensor_scalar(cos[:], cos[:], -2.0, 1.0, ALU.mult, ALU.add)
                dve.drain()
                dve.wait_ge(*scaled.at(1))
                C, S = all_seqs(cos), all_seqs(sin)
                nc.vector.tensor_tensor(gr[:], br[:], C, ALU.mult)
                nc.vector.tensor_tensor(m1[:], bi[:], S, ALU.mult)
                nc.vector.tensor_tensor(gi[:], bi[:], C, ALU.mult)
                dve.drain()
                dve.wait_ge(*aside.at(1))
                nc.vector.tensor_tensor(gr[:], gr[:], m1[:], ALU.add)
                nc.vector.tensor_tensor(gi[:], gi[:], m2[:], ALU.subtract)
                dve.drain()
                nc.vector.tensor_tensor_scan(flat(br), flat(decay), flat(gr), 0.0, ALU.mult, ALU.add)
                nc.vector.tensor_tensor_scan(flat(bi), flat(decay), flat(gi), 0.0, ALU.mult, ALU.add)\
                    .then_inc(scanned.sem, 1)
                dve.drain()
                nc.vector.tensor_tensor(hr[:], br[:], C, ALU.mult)
                nc.vector.tensor_tensor(m1[:], bi[:], S, ALU.mult)
                nc.vector.tensor_tensor(hi[:], br[:], S, ALU.mult)
                dve.drain()
                dve.wait_ge(*aside.at(2))
                nc.vector.tensor_tensor(hr[:], hr[:], m1[:], ALU.subtract)
                nc.vector.tensor_tensor(hi[:], hi[:], m2[:], ALU.add)

        with nc.psum_tensor("lr_psO", [P, 4, 512], F32) as psO, nc.Block() as block:
            @block.tensor
            def _(pe):
                for g in range(4):
                    for j in range(4):
                        t = 4 * g + j
                        o, c = psO[:, g, j * P:(j + 1) * P], slice(t * P, (t + 1) * P)
                        nc.tensor.matmul(o, flat(hr)[:, c], w["Cr"][:], start=True, stop=False)
                        nc.tensor.matmul(o, flat(hi)[:, c], w["Ci"][:], start=False, stop=False)
                        m = nc.tensor.matmul(o, k.XT[:, c], diag[:], start=False, stop=True)
                    m.then_inc(out_done.sem, 1)

            @block.vector
            def _(dve):
                for g in range(4):
                    dve.wait_ge(*out_done.at(g + 1))
                    x = k.X[:, 4 * g:4 * g + 4, :]
                    nc.vector.tensor_tensor(x, x, psO[:, g, :].rearrange("p (t d) -> p t d", d=D), ALU.add)


def store_stage(k, out):
    nc = k.nc
    stored = k.tally("stored")
    with nc.Block() as block:
        @block.sync
        def _(sp):
            sp.dma_start(out.rearrange("b (t p) d -> p (b t) d", p=P), k.X[:]).then_inc(stored.sem, 16)
            sp.wait_ge(*stored.at(16))


def program(nc, a, out, upto=8, start=0):
    with ExitStack() as ctx:
        k = Core(nc, ctx)
        setup_stage(k, a["L0_attn_x"])
        stages = [
            lambda: attention_stage(k, a["L0_attn_W_Q"], a["L0_attn_W_K"], a["L0_attn_W_V"], a["L0_attn_W_O"]),
            lambda: moe_l0_stage(k, a),
            lambda: delta_stage(k, a),
            lambda: moe_l1_stage(k, a),
            lambda: retention_stage(k, a),
            lambda: moe_l2_stage(k, a),
            lambda: lru_stage(k, a),
            lambda: moe_l3_stage(k, a),
        ]
        for n in range(start, upto):
            stages[n]()
            router = {0: a["L0_ffn_router"], 2: a["L1_ffn_router"], 4: a["L2_ffn_router"],
                      6: a["L3_ffn_routers"][0]}.get(n)
            if router is not None:
                k.open_logits(f"logits{n}", router.shape[1])
            layernorm_stage(k, f"ln{n}", turn=n < 7, router=router)
        store_stage(k, out)


def lay_out(v):
    r = {}
    r["L0_attn_x"] = v["L0_attn_x"]
    for n in "QKVO":
        r[f"L0_attn_W_{n}"] = v[f"L0_attn_W_{n}"].T
    cat = lambda *x: np.concatenate(x, axis=2)
    E, F = v["L0_ffn_b1"].shape
    cols = lambda b: b.reshape(E, F // P, P).transpose(0, 2, 1)
    down = lambda w: w.reshape(w.shape[0], -1, P, D).transpose(0, 2, 1, 3).reshape(w.shape[0], P, -1)
    r["L0_ffn_router"] = v["L0_ffn_Wg"].T
    r["L0_ffn_up"] = cat(v["L0_ffn_W1"].transpose(0, 2, 1), v["L0_ffn_W2"].transpose(0, 2, 1),
                         cols(v["L0_ffn_b1"]), cols(v["L0_ffn_b2"]))
    r["L0_ffn_down"] = down(v["L0_ffn_W3"].transpose(0, 2, 1))
    r["L0_ffn_b3"] = v["L0_ffn_b3"]
    for n in "qkvo":
        r[f"L1_attn_W{n}"] = v[f"L1_attn_W{n}"]
    r["L1_attn_taps"] = np.concatenate(
        [v["L1_attn_wq_conv"], v["L1_attn_wk_conv"], v["L1_attn_wv_conv"], v["L1_attn_fir_short"].reshape(D, -1),
         v["L1_attn_fir_long"].reshape(D, -1)], axis=1)

    def spread(rows, columns):
        out = np.zeros((rows, DHEADS, CH), np.float32)
        for s, c in columns.items():
            out[:, :, s] = c if c.ndim == 2 else c[:, None]
        return out.reshape(rows, D)

    wg1, wg2, wog1, wog2 = (v[f"L1_attn_{n}"] for n in ("Wg1", "Wg2", "Wog1", "Wog2"))
    r["L1_attn_Wxg"] = spread(D, {0: v["L1_attn_Wb"], 1: v["L1_attn_Wres"]})
    r["L1_attn_Wg1x"], r["L1_attn_Wog1x"] = wg1[:D], wog1[:D]
    r["L1_attn_Wg1s"] = spread(D, {i: wg1[D + i] for i in range(16)}).T
    r["L1_attn_Wog1s"] = spread(D // 2, {(i if i < 4 else 8 + i): wog1[D + i] for i in range(8)}).T
    r["L1_attn_Wg2"] = spread(D, {i: wg2[:, i] for i in range(4)})
    r["L1_attn_Wog2"] = spread(D // 2, {0: wog2[:, 0]})
    r["L1_attn_cols"] = np.stack(
        [np.repeat(v["L1_attn_bres"], CH), np.repeat(v["L1_attn_conv_res_logit"], CH),
         np.tile(v["L1_attn_norm_w"], DHEADS), v["L1_attn_bg1"],
         np.concatenate([v["L1_attn_bog1"], np.zeros(D // 2, np.float32)]), np.repeat(v["L1_attn_bog2"], D)], axis=1)
    r["L1_attn_rows"] = np.concatenate([v["L1_attn_bg2"], v["L1_attn_logit_temp"]])
    r["L1_ffn_router"] = v["L1_ffn_router_w"].T
    r["L1_ffn_router_bias"] = v["L1_ffn_router_bias"]
    halves = lambda w: w.T.reshape(D, 2, -1).transpose(1, 0, 2)
    two = lambda w: w.reshape(-1, 2, D, w.shape[2]).transpose(0, 2, 1, 3).reshape(w.shape[0] // 2, D, -1)
    r["L1_ffn_up"] = cat(two(np.concatenate([v["L1_ffn_gate_proj"], halves(v["L1_ffn_sh_gate"])])),
                         two(np.concatenate([v["L1_ffn_up_proj"], halves(v["L1_ffn_sh_up"])])))
    r["L1_ffn_down"] = np.concatenate([v["L1_ffn_down_proj"], v["L1_ffn_sh_down"].T.reshape(2, -1, D)])\
        .reshape(-1, P, D)
    r["L2_ffn_router"] = v["L2_ffn_router_w"].T
    r["L2_ffn_up"] = np.concatenate([cat(v["L2_ffn_w_gate"], v["L2_ffn_w_up"]), v["L2_ffn_ws_gate_up"][None]])
    r["L2_ffn_down"] = np.concatenate([v["L2_ffn_w_down"], v["L2_ffn_ws_down"][None]])
    c = lambda *x: np.stack(x, axis=1)
    r["L2_attn_cols"] = c(np.repeat(v["L2_attn_beta"], HD), v["L2_attn_ln_gamma"], v["L2_attn_ln_beta"])
    for n in "qvgo":
        r[f"L2_attn_w{n}"] = v[f"L2_attn_W{n}"].T
    r["L3_attn_cols"] = c(v["L3_attn_nu_log"], v["L3_attn_theta_log"], v["L3_attn_D_skip"])
    for n, m in (("Br", "B_re"), ("Bi", "B_im"), ("Cr", "C_re"), ("Ci", "C_im")):
        r[f"L3_attn_{n}"] = v[f"L3_attn_{m}"].T
    r["L3_ffn_routers"] = v["L3_ffn_routers"]
    r["L3_ffn_up"] = v["L3_ffn_W1"]
    r["L3_ffn_down"] = down(v["L3_ffn_W2"])
    return r


def kernel(**inputs):
    import concourse.bacc as bacc
    from concourse.bass_utils import run_bass_kernel_spmd

    laid = {n: np.ascontiguousarray(x) for n, x in lay_out({n: np.asarray(x) for n, x in inputs.items()}).items()}
    nc = bacc.Bacc("TRN2", target_bir_lowering=False, num_devices=1)
    aps = {n: nc.dram_tensor(f"in_{n}", x.shape, mybir.dt.from_np(x.dtype), kind="ExternalInput").ap()
           for n, x in laid.items()}
    out = nc.dram_tensor("out", (BATCH, SEQ, D), F32, kind="ExternalOutput").ap()
    program(nc, aps, out)
    r = run_bass_kernel_spmd(nc, [{f"in_{n}": x for n, x in laid.items()}], core_ids=[0])
    return r.results[0]["out"]
```
